# Optimizing a Trainium2 kernel written in Bass

```python
import numpy as np
import jax
import jax.numpy as jnp

def _softmax(x, axis=-1):
    return jax.nn.softmax(x, axis=axis)

def _gelu(x):
    return jax.nn.gelu(x, approximate=True)

def _silu(x):
    return jax.nn.silu(x)

def _sigmoid(x):
    return jax.nn.sigmoid(x)

def _layernorm(x, axis=-1, eps=1e-05):
    m = jnp.mean(x, axis=axis, keepdims=True)
    v = jnp.var(x, axis=axis, keepdims=True)
    return (x - m) / jnp.sqrt(v + eps)

def _scatter_add(tgt, idx, src, axis=0):
    return tgt.at[idx].add(src)

def _segment_sum(src, seg, n):
    return jax.ops.segment_sum(src, seg, n)
kernel_name = 'mk_early_fusion_d4_tok_img256_r4_1fc1f6'

def setup_inputs(seed: int=0):
    np.random.seed(seed)
    _w = jnp.asarray

    def _rec_inputs():
        import jax
        import jax.numpy as jnp
        _rk = jax.random.key(seed)
        x = -0.00016672 + 0.999947 * jax.random.normal(jax.random.fold_in(_rk, 1), (8, 3, 96, 96), jnp.float32)
        txt = 0.000202745 + 0.998873 * jax.random.normal(jax.random.fold_in(_rk, 2), (8, 128, 64), jnp.float32)
        return (x, txt)
    x, txt = _rec_inputs()

    def _L0_tok_setup():
        import jax, jax.numpy as jnp
        import numpy as np
        PATCH = 16
        key = jax.random.key(seed)
        k1, k2, k3 = jax.random.split(key, 3)
        B, C, H, Wd = (64, 3, 96, 96)
        E = 64
        pdim = PATCH * PATCH * C
        x = jax.random.normal(k1, (B, C, H, Wd), dtype=jnp.float32)
        W = jax.random.normal(k2, (E, pdim), dtype=jnp.float32) * pdim ** (-0.5)
        b = jax.random.normal(k3, (E,), dtype=jnp.float32) * 0.01
        return {'x': x, 'W': W, 'b': b}
    _L0_tok_all = _L0_tok_setup()
    _L0_tok_in = {k: v for k, v in _L0_tok_all.items() if k in ('W', 'b')}
    del _L0_tok_all

    def _L0_attn_setup():
        import jax, jax.numpy as jnp
        import numpy as np
        from jax import lax
        B_, L_, D_ = (4, 512, 64)
        DI, NS, DC, DTR = (128, 16, 4, 16)
        DFF = 4 * D_

        def _layer_norm(x, g, b, eps=1e-05):
            m = jnp.mean(x, -1, keepdims=True)
            v = jnp.mean((x - m) ** 2, -1, keepdims=True)
            return (x - m) / jnp.sqrt(v + eps) * g + b

        def _mamba(x, in_proj_w, in_proj_b, conv_w, conv_b, x_proj_w, dt_proj_w, dt_proj_b, A_log, D_ssm, out_proj_w, out_proj_b):
            B, L, D = x.shape
            xz = x @ in_proj_w.T + in_proj_b
            xi, z = jnp.split(xz, 2, axis=-1)
            xc = jnp.transpose(xi, (0, 2, 1))
            xc = lax.conv_general_dilated(xc, conv_w[:, None, :], (1,), [(DC - 1, 0)], dimension_numbers=('NCH', 'OIH', 'NCH'), feature_group_count=DI)
            xi = jax.nn.silu(jnp.transpose(xc + conv_b[None, :, None], (0, 2, 1)))
            x_dbl = xi @ x_proj_w.T
            dt, Bs, Cs = jnp.split(x_dbl, [DTR, DTR + NS], axis=-1)
            dt = jax.nn.softplus(dt @ dt_proj_w.T + dt_proj_b)
            A = -jnp.exp(A_log)
            dA = jnp.exp(dt[..., None] * A)
            dBu = dt[..., None] * Bs[:, :, None, :] * xi[..., None]
            dA_t = jnp.moveaxis(dA, 1, 0)
            dBu_t = jnp.moveaxis(dBu, 1, 0)
            C_t = jnp.moveaxis(Cs, 1, 0)

            def step(h, inp):
                a, bu, c = inp
                h = a * h + bu
                y = jnp.einsum('bdn,bn->bd', h, c)
                return (h, y)
            h0 = jnp.zeros((B, DI, NS), x.dtype)
            _, ys = lax.scan(step, h0, (dA_t, dBu_t, C_t))
            y = jnp.moveaxis(ys, 0, 1) + xi * D_ssm
            y = y * jax.nn.silu(z)
            return y @ out_proj_w.T + out_proj_b
        key = jax.random.key(seed)
        ks = jax.random.split(key, 20)
        rn = lambda k, s, sc=0.02: jax.random.normal(k, s, jnp.float32) * sc
        return {'x': jax.random.normal(ks[0], (B_, L_, D_), jnp.float32), 'in_proj_w': rn(ks[1], (2 * DI, D_)), 'in_proj_b': jnp.zeros((2 * DI,), jnp.float32), 'conv_w': rn(ks[2], (DI, DC), 0.1), 'conv_b': jnp.zeros((DI,), jnp.float32), 'x_proj_w': rn(ks[3], (DTR + 2 * NS, DI)), 'dt_proj_w': rn(ks[4], (DI, DTR), 0.1), 'dt_proj_b': rn(ks[5], (DI,), 0.5), 'A_log': jnp.log(jnp.tile(jnp.arange(1, NS + 1, dtype=jnp.float32), (DI, 1))), 'D_ssm': jnp.ones((DI,), jnp.float32), 'out_proj_w': rn(ks[6], (D_, DI)), 'out_proj_b': jnp.zeros((D_,), jnp.float32), 'ln1_g': jnp.ones((D_,), jnp.float32), 'ln1_b': jnp.zeros((D_,), jnp.float32), 'fc1_w': rn(ks[7], (DFF, D_)), 'fc1_b': jnp.zeros((DFF,), jnp.float32), 'fc2_w': rn(ks[8], (D_, DFF)), 'fc2_b': jnp.zeros((D_,), jnp.float32), 'ln2_g': jnp.ones((D_,), jnp.float32), 'ln2_b': jnp.zeros((D_,), jnp.float32)}
    _L0_attn_all = _L0_attn_setup()
    _L0_attn_in = {k: v for k, v in _L0_attn_all.items() if k in ('in_proj_w', 'in_proj_b', 'conv_w', 'conv_b', 'x_proj_w', 'dt_proj_w', 'dt_proj_b', 'A_log', 'D_ssm', 'out_proj_w', 'out_proj_b', 'ln1_g', 'ln1_b', 'fc1_w', 'fc1_b', 'fc2_w', 'fc2_b', 'ln2_g', 'ln2_b')}
    del _L0_attn_all

    def _L0_ffn_setup():
        import jax, jax.numpy as jnp
        import numpy as np
        C = 64
        HID = 256
        E = 8
        TEMP = 1.0
        key = jax.random.key(seed)
        ks = jax.random.split(key, 7)
        x = jax.random.normal(ks[0], (8, 4096, C), dtype=jnp.float32)
        W1 = jax.random.normal(ks[1], (C, HID), dtype=jnp.float32) * 0.02
        b1 = jnp.zeros((HID,), dtype=jnp.float32)
        Wg = jax.random.normal(ks[2], (HID, E), dtype=jnp.float32) * 0.02
        bg = jnp.zeros((E,), dtype=jnp.float32)
        Wd = jax.random.normal(ks[3], (E, HID, C), dtype=jnp.float32) * 0.02
        bd = jnp.zeros((E, C), dtype=jnp.float32)
        return {'x': x, 'W1': W1, 'b1': b1, 'Wg': Wg, 'bg': bg, 'Wd': Wd, 'bd': bd}
    _L0_ffn_all = _L0_ffn_setup()
    _L0_ffn_in = {k: v for k, v in _L0_ffn_all.items() if k in ('W1', 'b1', 'Wg', 'bg', 'Wd', 'bd')}
    del _L0_ffn_all

    def _L1_attn_setup():
        import jax, jax.numpy as jnp
        import numpy as np
        EPS = 1e-09

        def _glorot(key, shape):
            fan_in, fan_out = (shape[-2], shape[-1])
            std = (2.0 / (fan_in + fan_out)) ** 0.5
            return jax.random.normal(key, shape, dtype=jnp.float32) * std

        def _reference_tuple_inner(x, Wks, Wqs, Wvs, Wo):
            keys = jnp.einsum('bsd,hdk->hbsk', x, Wks)
            queries = jnp.einsum('bsd,hdk->hbsk', x, Wqs)
            values = jnp.einsum('bsd,hde->hbse', x, Wvs)
            keys = jax.nn.elu(keys) + 1.0
            queries = jax.nn.elu(queries) + 1.0
            att = jnp.einsum('hbsk,hbtk->hbst', queries, keys)
            S = att.shape[-1]
            causal = jnp.tril(jnp.ones((S, S), dtype=att.dtype))
            att = att * causal
            att = att / (jnp.sum(att, axis=-1, keepdims=True) + EPS)
            kv = jnp.einsum('hbsk,hbsd->hbsdk', keys, values)
            kv_cum = jnp.cumsum(kv, axis=2)
            numerator = jnp.einsum('hbsdk,hbsk->hbsd', kv_cum, queries)
            denominator = jnp.einsum('hbsk,hbsk->hbs', jnp.cumsum(keys, axis=2), queries)
            node = numerator / (denominator[..., None] + EPS)
            out = jnp.einsum('hbsd,hde->bse', node, Wo)
            return (out, att)
        key = jax.random.key(seed)
        kx, k1, k2, k3, k4 = jax.random.split(key, 5)
        B, S, D = (2, 256, 64)
        H, K = (8, 32)
        return {'x': jax.random.normal(kx, (B, S, D), dtype=jnp.float32), 'Wks': _glorot(k1, (H, D, K)), 'Wqs': _glorot(k2, (H, D, K)), 'Wvs': _glorot(k3, (H, D, D)), 'Wo': _glorot(k4, (H, D, D))}
    _L1_attn_all = _L1_attn_setup()
    _L1_attn_in = {k: v for k, v in _L1_attn_all.items() if k in ('Wks', 'Wqs', 'Wvs', 'Wo')}
    del _L1_attn_all

    def _L1_ffn_setup():
        import jax, jax.numpy as jnp
        import numpy as np
        B, S, H, NH, NE = (4, 256, 64, 4, 4)
        D = H // NH
        EPS = 1e-08

        def layernorm(x, g, b):
            m = jnp.mean(x, axis=-1, keepdims=True)
            v = jnp.mean((x - m) ** 2, axis=-1, keepdims=True)
            return (x - m) / jnp.sqrt(v + EPS) * g + b
        key = jax.random.key(seed)
        ks = jax.random.split(key, 18)
        sc = 0.05
        return {'x': jax.random.normal(ks[0], (B, S, H), jnp.float32), 'hl_w': jax.random.normal(ks[1], (NH, D, H), jnp.float32) * sc, 'hl_b': jax.random.normal(ks[2], (NH, D), jnp.float32) * sc, 'wq': jax.random.normal(ks[3], (NH, NE, D, D), jnp.float32) * sc, 'wk': jax.random.normal(ks[4], (NH, D, D), jnp.float32) * sc, 'wv': jax.random.normal(ks[5], (NH, D, D), jnp.float32) * sc, 'gate_w': jax.random.normal(ks[6], (NH, NE, NE * D), jnp.float32) * sc, 'gate_b': jax.random.normal(ks[7], (NH, NE), jnp.float32) * sc, 'ln_g': jnp.ones((D,), jnp.float32), 'ln_b': jnp.zeros((D,), jnp.float32), 'fc1_w': jax.random.normal(ks[8], (D, D), jnp.float32) * sc, 'fc1_b': jax.random.normal(ks[9], (D,), jnp.float32) * sc, 'fc2_w': jax.random.normal(ks[10], (D, D), jnp.float32) * sc, 'fc2_b': jax.random.normal(ks[11], (D,), jnp.float32) * sc, 'fnorm_g': jnp.ones((D,), jnp.float32), 'fnorm_b': jnp.zeros((D,), jnp.float32), 'fgate_w': jax.random.normal(ks[12], (NH, H), jnp.float32) * sc}
    _L1_ffn_all = _L1_ffn_setup()
    _L1_ffn_in = {k: v for k, v in _L1_ffn_all.items() if k in ('hl_w', 'hl_b', 'wq', 'wk', 'wv', 'gate_w', 'gate_b', 'ln_g', 'ln_b', 'fc1_w', 'fc1_b', 'fc2_w', 'fc2_b', 'fnorm_g', 'fnorm_b', 'fgate_w')}
    del _L1_ffn_all

    def _L2_attn_setup():
        import jax, jax.numpy as jnp
        import numpy as np
        HEADS, DIM_HEAD = (8, 64)
        EPS = 1e-05

        def instance_norm(t):
            mu = jnp.mean(t, axis=-1, keepdims=True)
            var = jnp.mean((t - mu) ** 2, axis=-1, keepdims=True)
            return (t - mu) * jax.lax.rsqrt(var + EPS)
        key = jax.random.key(seed)
        k1, k2, k3, k4 = jax.random.split(key, 4)
        B, N, D = (8, 2048, 64)
        inner = HEADS * DIM_HEAD
        x = jax.random.normal(k1, (B, N, D), jnp.float32)
        w_qkv = jax.random.normal(k2, (3 * inner, D), jnp.float32) / np.sqrt(D).astype(np.float32)
        w_out = jax.random.normal(k3, (D, inner), jnp.float32) / np.sqrt(inner).astype(np.float32)
        b_out = 0.01 * jax.random.normal(k4, (D,), jnp.float32)
        return {'x': x, 'w_qkv': w_qkv, 'w_out': w_out, 'b_out': b_out}
    _L2_attn_all = _L2_attn_setup()
    _L2_attn_in = {k: v for k, v in _L2_attn_all.items() if k in ('w_qkv', 'w_out', 'b_out')}
    del _L2_attn_all

    def _L2_ffn_setup():
        import jax, jax.numpy as jnp
        import numpy as np
        B, T, C = (64, 96, 64)
        NH, NKV = (4, 2)
        HD = C // NH
        NREP = NH // NKV
        NE, TOPK = (8, 2)
        HID = int(8 / 3 * C)
        EPS_RMS = 1e-06

        def _rope_tables(t_len):
            inv_freq = 1.0 / 10000.0 ** (np.arange(0, HD, 2, dtype=np.float32) / HD)
            t = np.arange(t_len, dtype=np.float32)
            freqs = np.outer(t, inv_freq)
            emb = np.concatenate([freqs, freqs], axis=-1)
            return (jnp.asarray(np.cos(emb)), jnp.asarray(np.sin(emb)))

        def _rotate_half(x):
            h = x.shape[-1] // 2
            return jnp.concatenate([-x[..., h:], x[..., :h]], axis=-1)

        def _rmsnorm(v, w):
            return v * jax.lax.rsqrt(jnp.mean(v * v, axis=-1, keepdims=True) + EPS_RMS) * w
        key = jax.random.key(seed)
        ks = jax.random.split(key, 10)
        s = lambda k, shape: jax.random.normal(k, shape, jnp.float32) * 0.02
        return {'x': jax.random.normal(ks[0], (B, T, C), jnp.float32), 'ln1_w': jnp.ones((C,), jnp.float32), 'ln2_w': jnp.ones((C,), jnp.float32), 'wq': s(ks[1], (NH * HD, C)), 'wk': s(ks[2], (NKV * HD, C)), 'wv': s(ks[3], (NKV * HD, C)), 'wo': s(ks[4], (C, C)), 'router_w': s(ks[5], (NE, C)), 'w1': s(ks[6], (NE, HID, C)), 'w2': s(ks[7], (NE, C, HID)), 'w3': s(ks[8], (NE, HID, C))}
    _L2_ffn_all = _L2_ffn_setup()
    _L2_ffn_in = {k: v for k, v in _L2_ffn_all.items() if k in ('ln1_w', 'ln2_w', 'wq', 'wk', 'wv', 'wo', 'router_w', 'w1', 'w2', 'w3')}
    del _L2_ffn_all

    def _L3_attn_setup():
        import jax, jax.numpy as jnp
        import numpy as np
        import math
        D_MODEL = 64
        NHEAD = 8
        D_LATTICE = 512
        D_K = D_LATTICE // NHEAD
        PHI = (1.0 + math.sqrt(5.0)) / 2.0
        PHI_INV = 1.0 / PHI
        PHI_INT = 1618.0
        C1 = PHI * math.sqrt(2.0) * 51.85
        C2 = math.pi / PHI

        def qrt_damping(x):
            return jnp.sin(C1 * x) * jnp.exp(-(x * x) / PHI) + jnp.cos(C2 * x)

        def ttt_filter(scores):
            int_scores = (jnp.abs(scores) * PHI_INT).astype(jnp.int32)
            mod9 = int_scores % 9
            chaos = (mod9 == 0) | (mod9 == 3) | (mod9 == 6)
            penalty = jnp.where(chaos, jnp.float32(PHI_INV), jnp.float32(1.0))
            return scores * penalty
        key = jax.random.key(seed)
        ks = jax.random.split(key, 9)
        B, S = (2, 512)
        s_in = 1.0 / math.sqrt(D_MODEL)
        s_lat = 1.0 / math.sqrt(D_LATTICE)
        return {'x': jax.random.normal(ks[0], (B, S, D_MODEL), dtype=jnp.float32), 'Wq': jax.random.normal(ks[1], (D_MODEL, D_LATTICE), dtype=jnp.float32) * s_in, 'bq': jax.random.normal(ks[2], (D_LATTICE,), dtype=jnp.float32) * 0.01, 'Wk': jax.random.normal(ks[3], (D_MODEL, D_LATTICE), dtype=jnp.float32) * s_in, 'bk': jax.random.normal(ks[4], (D_LATTICE,), dtype=jnp.float32) * 0.01, 'Wv': jax.random.normal(ks[5], (D_MODEL, D_LATTICE), dtype=jnp.float32) * s_in, 'bv': jax.random.normal(ks[6], (D_LATTICE,), dtype=jnp.float32) * 0.01, 'Wo': jax.random.normal(ks[7], (D_LATTICE, D_MODEL), dtype=jnp.float32) * s_lat, 'bo': jax.random.normal(ks[8], (D_MODEL,), dtype=jnp.float32) * 0.01}
    _L3_attn_all = _L3_attn_setup()
    _L3_attn_in = {k: v for k, v in _L3_attn_all.items() if k in ('Wq', 'bq', 'Wk', 'bk', 'Wv', 'bv', 'Wo', 'bo')}
    del _L3_attn_all

    def _L3_ffn_setup():
        import jax, jax.numpy as jnp
        import numpy as np
        E = 8
        K = 2
        D = 64
        H = 128
        DOUT = 64
        EPS = 1e-05
        key = jax.random.key(seed)
        ks = jax.random.split(key, 9)
        s = 0.02
        return {'x': jax.random.normal(ks[0], (4, 2048, D), jnp.float32), 'gamma': 1.0 + 0.05 * jax.random.normal(ks[1], (D,), jnp.float32), 'beta': 0.05 * jax.random.normal(ks[2], (D,), jnp.float32), 'Wr': 0.01 * jax.random.normal(ks[3], (D, E), jnp.float32), 'br': jnp.zeros((E,), jnp.float32), 'W1': s * jax.random.normal(ks[4], (E, D, H), jnp.float32), 'b1': s * jax.random.normal(ks[5], (E, H), jnp.float32), 'W2': s * jax.random.normal(ks[6], (E, H, DOUT), jnp.float32), 'b2': s * jax.random.normal(ks[7], (E, DOUT), jnp.float32)}
    _L3_ffn_all = _L3_ffn_setup()
    _L3_ffn_in = {k: v for k, v in _L3_ffn_all.items() if k in ('gamma', 'beta', 'Wr', 'br', 'W1', 'b1', 'W2', 'b2')}
    del _L3_ffn_all
    return {'x': x, 'txt': txt, 'L0_tok_W': _L0_tok_in['W'], 'L0_tok_b': _L0_tok_in['b'], 'L0_attn_in_proj_w': _L0_attn_in['in_proj_w'], 'L0_attn_in_proj_b': _L0_attn_in['in_proj_b'], 'L0_attn_conv_w': _L0_attn_in['conv_w'], 'L0_attn_conv_b': _L0_attn_in['conv_b'], 'L0_attn_x_proj_w': _L0_attn_in['x_proj_w'], 'L0_attn_dt_proj_w': _L0_attn_in['dt_proj_w'], 'L0_attn_dt_proj_b': _L0_attn_in['dt_proj_b'], 'L0_attn_A_log': _L0_attn_in['A_log'], 'L0_attn_D_ssm': _L0_attn_in['D_ssm'], 'L0_attn_out_proj_w': _L0_attn_in['out_proj_w'], 'L0_attn_out_proj_b': _L0_attn_in['out_proj_b'], 'L0_attn_ln1_g': _L0_attn_in['ln1_g'], 'L0_attn_ln1_b': _L0_attn_in['ln1_b'], 'L0_attn_fc1_w': _L0_attn_in['fc1_w'], 'L0_attn_fc1_b': _L0_attn_in['fc1_b'], 'L0_attn_fc2_w': _L0_attn_in['fc2_w'], 'L0_attn_fc2_b': _L0_attn_in['fc2_b'], 'L0_attn_ln2_g': _L0_attn_in['ln2_g'], 'L0_attn_ln2_b': _L0_attn_in['ln2_b'], 'L0_ffn_W1': _L0_ffn_in['W1'], 'L0_ffn_b1': _L0_ffn_in['b1'], 'L0_ffn_Wg': _L0_ffn_in['Wg'], 'L0_ffn_bg': _L0_ffn_in['bg'], 'L0_ffn_Wd': _L0_ffn_in['Wd'], 'L0_ffn_bd': _L0_ffn_in['bd'], 'L1_attn_Wks': _L1_attn_in['Wks'], 'L1_attn_Wqs': _L1_attn_in['Wqs'], 'L1_attn_Wvs': _L1_attn_in['Wvs'], 'L1_attn_Wo': _L1_attn_in['Wo'], 'L1_ffn_hl_w': _L1_ffn_in['hl_w'], 'L1_ffn_hl_b': _L1_ffn_in['hl_b'], 'L1_ffn_wq': _L1_ffn_in['wq'], 'L1_ffn_wk': _L1_ffn_in['wk'], 'L1_ffn_wv': _L1_ffn_in['wv'], 'L1_ffn_gate_w': _L1_ffn_in['gate_w'], 'L1_ffn_gate_b': _L1_ffn_in['gate_b'], 'L1_ffn_ln_g': _L1_ffn_in['ln_g'], 'L1_ffn_ln_b': _L1_ffn_in['ln_b'], 'L1_ffn_fc1_w': _L1_ffn_in['fc1_w'], 'L1_ffn_fc1_b': _L1_ffn_in['fc1_b'], 'L1_ffn_fc2_w': _L1_ffn_in['fc2_w'], 'L1_ffn_fc2_b': _L1_ffn_in['fc2_b'], 'L1_ffn_fnorm_g': _L1_ffn_in['fnorm_g'], 'L1_ffn_fnorm_b': _L1_ffn_in['fnorm_b'], 'L1_ffn_fgate_w': _L1_ffn_in['fgate_w'], 'L2_attn_w_qkv': _L2_attn_in['w_qkv'], 'L2_attn_w_out': _L2_attn_in['w_out'], 'L2_attn_b_out': _L2_attn_in['b_out'], 'L2_ffn_ln1_w': _L2_ffn_in['ln1_w'], 'L2_ffn_ln2_w': _L2_ffn_in['ln2_w'], 'L2_ffn_wq': _L2_ffn_in['wq'], 'L2_ffn_wk': _L2_ffn_in['wk'], 'L2_ffn_wv': _L2_ffn_in['wv'], 'L2_ffn_wo': _L2_ffn_in['wo'], 'L2_ffn_router_w': _L2_ffn_in['router_w'], 'L2_ffn_w1': _L2_ffn_in['w1'], 'L2_ffn_w2': _L2_ffn_in['w2'], 'L2_ffn_w3': _L2_ffn_in['w3'], 'L3_attn_Wq': _L3_attn_in['Wq'], 'L3_attn_bq': _L3_attn_in['bq'], 'L3_attn_Wk': _L3_attn_in['Wk'], 'L3_attn_bk': _L3_attn_in['bk'], 'L3_attn_Wv': _L3_attn_in['Wv'], 'L3_attn_bv': _L3_attn_in['bv'], 'L3_attn_Wo': _L3_attn_in['Wo'], 'L3_attn_bo': _L3_attn_in['bo'], 'L3_ffn_gamma': _L3_ffn_in['gamma'], 'L3_ffn_beta': _L3_ffn_in['beta'], 'L3_ffn_Wr': _L3_ffn_in['Wr'], 'L3_ffn_br': _L3_ffn_in['br'], 'L3_ffn_W1': _L3_ffn_in['W1'], 'L3_ffn_b1': _L3_ffn_in['b1'], 'L3_ffn_W2': _L3_ffn_in['W2'], 'L3_ffn_b2': _L3_ffn_in['b2']}

def reference(x, txt, L0_tok_W, L0_tok_b, L0_attn_in_proj_w, L0_attn_in_proj_b, L0_attn_conv_w, L0_attn_conv_b, L0_attn_x_proj_w, L0_attn_dt_proj_w, L0_attn_dt_proj_b, L0_attn_A_log, L0_attn_D_ssm, L0_attn_out_proj_w, L0_attn_out_proj_b, L0_attn_ln1_g, L0_attn_ln1_b, L0_attn_fc1_w, L0_attn_fc1_b, L0_attn_fc2_w, L0_attn_fc2_b, L0_attn_ln2_g, L0_attn_ln2_b, L0_ffn_W1, L0_ffn_b1, L0_ffn_Wg, L0_ffn_bg, L0_ffn_Wd, L0_ffn_bd, L1_attn_Wks, L1_attn_Wqs, L1_attn_Wvs, L1_attn_Wo, L1_ffn_hl_w, L1_ffn_hl_b, L1_ffn_wq, L1_ffn_wk, L1_ffn_wv, L1_ffn_gate_w, L1_ffn_gate_b, L1_ffn_ln_g, L1_ffn_ln_b, L1_ffn_fc1_w, L1_ffn_fc1_b, L1_ffn_fc2_w, L1_ffn_fc2_b, L1_ffn_fnorm_g, L1_ffn_fnorm_b, L1_ffn_fgate_w, L2_attn_w_qkv, L2_attn_w_out, L2_attn_b_out, L2_ffn_ln1_w, L2_ffn_ln2_w, L2_ffn_wq, L2_ffn_wk, L2_ffn_wv, L2_ffn_wo, L2_ffn_router_w, L2_ffn_w1, L2_ffn_w2, L2_ffn_w3, L3_attn_Wq, L3_attn_bq, L3_attn_Wk, L3_attn_bk, L3_attn_Wv, L3_attn_bv, L3_attn_Wo, L3_attn_bo, L3_ffn_gamma, L3_ffn_beta, L3_ffn_Wr, L3_ffn_br, L3_ffn_W1, L3_ffn_b1, L3_ffn_W2, L3_ffn_b2):
    import jax
    import jax.numpy as jnp

    def _L0_tok_ref(x, W, b):
        import jax, jax.numpy as jnp
        import numpy as np
        PATCH = 16
        B, C, H, Wd = x.shape
        p = PATCH
        nH, nW = (H // p, Wd // p)
        patches = x.reshape(B, C, nH, p, nW, p)
        patches = patches.transpose(0, 2, 4, 1, 3, 5)
        patches = patches.reshape(B, nH * nW, C * p * p)
        return jnp.einsum('bnk,ek->bne', patches, W) + b

    def _L0_attn_ref(x, in_proj_w, in_proj_b, conv_w, conv_b, x_proj_w, dt_proj_w, dt_proj_b, A_log, D_ssm, out_proj_w, out_proj_b, ln1_g, ln1_b, fc1_w, fc1_b, fc2_w, fc2_b, ln2_g, ln2_b):
        import jax, jax.numpy as jnp
        import numpy as np
        from jax import lax
        B_, L_, D_ = (4, 512, 64)
        DI, NS, DC, DTR = (128, 16, 4, 16)
        DFF = 4 * D_

        def _layer_norm(x, g, b, eps=1e-05):
            m = jnp.mean(x, -1, keepdims=True)
            v = jnp.mean((x - m) ** 2, -1, keepdims=True)
            return (x - m) / jnp.sqrt(v + eps) * g + b

        def _mamba(x, in_proj_w, in_proj_b, conv_w, conv_b, x_proj_w, dt_proj_w, dt_proj_b, A_log, D_ssm, out_proj_w, out_proj_b):
            B, L, D = x.shape
            xz = x @ in_proj_w.T + in_proj_b
            xi, z = jnp.split(xz, 2, axis=-1)
            xc = jnp.transpose(xi, (0, 2, 1))
            xc = lax.conv_general_dilated(xc, conv_w[:, None, :], (1,), [(DC - 1, 0)], dimension_numbers=('NCH', 'OIH', 'NCH'), feature_group_count=DI)
            xi = jax.nn.silu(jnp.transpose(xc + conv_b[None, :, None], (0, 2, 1)))
            x_dbl = xi @ x_proj_w.T
            dt, Bs, Cs = jnp.split(x_dbl, [DTR, DTR + NS], axis=-1)
            dt = jax.nn.softplus(dt @ dt_proj_w.T + dt_proj_b)
            A = -jnp.exp(A_log)
            dA = jnp.exp(dt[..., None] * A)
            dBu = dt[..., None] * Bs[:, :, None, :] * xi[..., None]
            dA_t = jnp.moveaxis(dA, 1, 0)
            dBu_t = jnp.moveaxis(dBu, 1, 0)
            C_t = jnp.moveaxis(Cs, 1, 0)

            def step(h, inp):
                a, bu, c = inp
                h = a * h + bu
                y = jnp.einsum('bdn,bn->bd', h, c)
                return (h, y)
            h0 = jnp.zeros((B, DI, NS), x.dtype)
            _, ys = lax.scan(step, h0, (dA_t, dBu_t, C_t))
            y = jnp.moveaxis(ys, 0, 1) + xi * D_ssm
            y = y * jax.nn.silu(z)
            return y @ out_proj_w.T + out_proj_b
        gelu = lambda t: jax.nn.gelu(t, approximate=False)
        ssm = _mamba(x, in_proj_w, in_proj_b, conv_w, conv_b, x_proj_w, dt_proj_w, dt_proj_b, A_log, D_ssm, out_proj_w, out_proj_b)
        y = _layer_norm(x + ssm, ln1_g, ln1_b)
        ffn = gelu(gelu(y @ fc1_w.T + fc1_b) @ fc2_w.T + fc2_b)
        return _layer_norm(y + ffn, ln2_g, ln2_b)

    def _L0_ffn_ref(x, W1, b1, Wg, bg, Wd, bd):
        import jax, jax.numpy as jnp
        import numpy as np
        C = 64
        HID = 256
        E = 8
        TEMP = 1.0
        orig_shape = x.shape
        xf = x.reshape(-1, orig_shape[-1])
        H = jax.nn.gelu(xf @ W1 + b1, approximate=False)
        probs = jax.nn.softmax((H @ Wg + bg) / TEMP, axis=-1)
        assign = jnp.argmax(probs, axis=-1)
        out = jnp.zeros_like(xf)
        for e in range(Wd.shape[0]):
            y = H @ Wd[e] + bd[e]
            sel = (assign == e)[:, None]
            out = out + jnp.where(sel, probs[:, e:e + 1] * y, 0.0)
        return out.reshape(orig_shape)

    def _L1_attn_ref(x, Wks, Wqs, Wvs, Wo):
        import jax, jax.numpy as jnp
        import numpy as np
        EPS = 1e-09

        def _glorot(key, shape):
            fan_in, fan_out = (shape[-2], shape[-1])
            std = (2.0 / (fan_in + fan_out)) ** 0.5
            return jax.random.normal(key, shape, dtype=jnp.float32) * std

        def _reference_tuple_inner(x, Wks, Wqs, Wvs, Wo):
            keys = jnp.einsum('bsd,hdk->hbsk', x, Wks)
            queries = jnp.einsum('bsd,hdk->hbsk', x, Wqs)
            values = jnp.einsum('bsd,hde->hbse', x, Wvs)
            keys = jax.nn.elu(keys) + 1.0
            queries = jax.nn.elu(queries) + 1.0
            att = jnp.einsum('hbsk,hbtk->hbst', queries, keys)
            S = att.shape[-1]
            causal = jnp.tril(jnp.ones((S, S), dtype=att.dtype))
            att = att * causal
            att = att / (jnp.sum(att, axis=-1, keepdims=True) + EPS)
            kv = jnp.einsum('hbsk,hbsd->hbsdk', keys, values)
            kv_cum = jnp.cumsum(kv, axis=2)
            numerator = jnp.einsum('hbsdk,hbsk->hbsd', kv_cum, queries)
            denominator = jnp.einsum('hbsk,hbsk->hbs', jnp.cumsum(keys, axis=2), queries)
            node = numerator / (denominator[..., None] + EPS)
            out = jnp.einsum('hbsd,hde->bse', node, Wo)
            return (out, att)
        return _reference_tuple_inner(x, Wks, Wqs, Wvs, Wo)[0]

    def _L1_ffn_ref(x, hl_w, hl_b, wq, wk, wv, gate_w, gate_b, ln_g, ln_b, fc1_w, fc1_b, fc2_w, fc2_b, fnorm_g, fnorm_b, fgate_w):
        import jax, jax.numpy as jnp
        import numpy as np
        B, S, H, NH, NE = (4, 256, 64, 4, 4)
        D = H // NH
        EPS = 1e-08

        def layernorm(x, g, b):
            m = jnp.mean(x, axis=-1, keepdims=True)
            v = jnp.mean((x - m) ** 2, axis=-1, keepdims=True)
            return (x - m) / jnp.sqrt(v + EPS) * g + b
        b, s, h = x.shape
        nh, d, _ = wk.shape
        ne = wq.shape[1]
        sx = jnp.einsum('bsh,ndh->bnsd', x, hl_w) + hl_b[None, :, None, :]
        pad = sx == 0
        q = jnp.einsum('bnsd,neod->bneso', sx, wq)
        k = jnp.einsum('bnsd,nod->bnso', sx, wk)
        v = jnp.einsum('bnsd,nod->bnso', sx, wv)
        causal = jnp.where(jnp.tril(jnp.ones((s, s), bool)), 0.0, -jnp.inf).astype(x.dtype)
        scores = jnp.einsum('bnesd,bntd->bnest', q, k) * d ** 0.5 + causal
        att = jax.nn.softmax(scores, axis=-1)
        qkv = jnp.einsum('bnest,bntd->bnesd', att, v)
        qkv = jnp.where(pad[:, :, None], 0.0, qkv)
        out = jnp.transpose(qkv, (0, 1, 3, 2, 4)).reshape(b, nh, s, ne * d)
        gs = jax.nn.softmax(jnp.einsum('bnsf,nef->bnse', out, gate_w) + gate_b[None, :, None, :], axis=-1)
        mixed = jnp.einsum('bnsed,bnse->bnsd', out.reshape(b, nh, s, ne, d), gs)
        resid = sx[jnp.arange(nh), jnp.arange(nh)]
        hn = layernorm(mixed + resid, ln_g, ln_b)
        f_n = jnp.transpose(hn, (0, 2, 1, 3)).reshape(b, s, h)
        fx = f_n.reshape(b, s, nh, d)
        pm = fx == 0
        hx = jnp.where(pm, 0.0, fx @ fc1_w.T + fc1_b)
        hx = jax.nn.relu(hx)
        hx = jnp.where(pm, 0.0, hx @ fc2_w.T + fc2_b)
        hx = layernorm(hx + fx, fnorm_g, fnorm_b)
        fout = hx.reshape(b, s, h)
        fg = jax.nn.softmax(fout @ fgate_w.T, axis=-1)
        return (fout.reshape(b, s, nh, d) * fg[..., None]).reshape(b, s, h)

    def _L2_attn_ref(x, w_qkv, w_out, b_out):
        import jax, jax.numpy as jnp
        import numpy as np
        HEADS, DIM_HEAD = (8, 64)
        EPS = 1e-05

        def instance_norm(t):
            mu = jnp.mean(t, axis=-1, keepdims=True)
            var = jnp.mean((t - mu) ** 2, axis=-1, keepdims=True)
            return (t - mu) * jax.lax.rsqrt(var + EPS)
        B, N, _ = x.shape
        H, Dh = (HEADS, DIM_HEAD)
        qkv = jnp.einsum('bnd,ed->bne', x, w_qkv)
        q, k, v = jnp.split(qkv, 3, axis=-1)

        def to_heads(t):
            return t.reshape(B, N, H, Dh).transpose(0, 2, 1, 3)
        q, k, v = (to_heads(q), to_heads(k), to_heads(v))
        k = instance_norm(k)
        v = instance_norm(v)
        dots = jnp.einsum('bhnd,bhne->bhde', k, v)
        out = jnp.einsum('bhnd,bhde->bhne', q, dots) / N
        out = out.transpose(0, 2, 1, 3).reshape(B, N, H * Dh)
        return jnp.einsum('bne,de->bnd', out, w_out) + b_out

    def _L2_ffn_ref(x, ln1_w, ln2_w, wq, wk, wv, wo, router_w, w1, w2, w3):
        import jax, jax.numpy as jnp
        import numpy as np
        B, T, C = (64, 96, 64)
        NH, NKV = (4, 2)
        HD = C // NH
        NREP = NH // NKV
        NE, TOPK = (8, 2)
        HID = int(8 / 3 * C)
        EPS_RMS = 1e-06

        def _rope_tables(t_len):
            inv_freq = 1.0 / 10000.0 ** (np.arange(0, HD, 2, dtype=np.float32) / HD)
            t = np.arange(t_len, dtype=np.float32)
            freqs = np.outer(t, inv_freq)
            emb = np.concatenate([freqs, freqs], axis=-1)
            return (jnp.asarray(np.cos(emb)), jnp.asarray(np.sin(emb)))

        def _rotate_half(x):
            h = x.shape[-1] // 2
            return jnp.concatenate([-x[..., h:], x[..., :h]], axis=-1)

        def _rmsnorm(v, w):
            return v * jax.lax.rsqrt(jnp.mean(v * v, axis=-1, keepdims=True) + EPS_RMS) * w
        Bx, Tx, Cx = x.shape
        h = _rmsnorm(x, ln1_w)
        q = (h @ wq.T).reshape(Bx, Tx, NH, HD).transpose(0, 2, 1, 3)
        k = (h @ wk.T).reshape(Bx, Tx, NKV, HD).transpose(0, 2, 1, 3)
        v = (h @ wv.T).reshape(Bx, Tx, NKV, HD).transpose(0, 2, 1, 3)
        cos, sin = _rope_tables(Tx)
        cos, sin = (cos[None, None], sin[None, None])
        q = q * cos + _rotate_half(q) * sin
        k = k * cos + _rotate_half(k) * sin
        k = jnp.repeat(k, NREP, axis=1)
        v = jnp.repeat(v, NREP, axis=1)
        scores = jnp.einsum('bhtd,bhsd->bhts', q, k) / jnp.sqrt(jnp.float32(HD))
        causal = jnp.tril(jnp.ones((Tx, Tx), dtype=bool))
        scores = jnp.where(causal[None, None], scores, jnp.float32(-1e+30))
        att = jax.nn.softmax(scores, axis=-1)
        y = jnp.einsum('bhts,bhsd->bhtd', att, v).transpose(0, 2, 1, 3).reshape(Bx, Tx, Cx)
        x = x + y @ wo.T
        flat = _rmsnorm(x, ln2_w).reshape(-1, Cx)
        probs = jax.nn.softmax(flat @ router_w.T, axis=-1)
        tp, ti = jax.lax.top_k(probs, TOPK)
        tp = tp / (jnp.sum(tp, axis=-1, keepdims=True) + 1e-09)
        weights = jnp.sum(tp[..., None] * jax.nn.one_hot(ti, NE, dtype=flat.dtype), axis=1)
        out = jnp.zeros_like(flat)
        for e in range(NE):
            hh = jax.nn.silu(flat @ w1[e].T) * (flat @ w3[e].T)
            out = out + weights[:, e:e + 1] * (hh @ w2[e].T)
        return x + out.reshape(Bx, Tx, Cx)

    def _L3_attn_ref(x, Wq, bq, Wk, bk, Wv, bv, Wo, bo):
        import jax, jax.numpy as jnp
        import numpy as np
        import math
        D_MODEL = 64
        NHEAD = 8
        D_LATTICE = 512
        D_K = D_LATTICE // NHEAD
        PHI = (1.0 + math.sqrt(5.0)) / 2.0
        PHI_INV = 1.0 / PHI
        PHI_INT = 1618.0
        C1 = PHI * math.sqrt(2.0) * 51.85
        C2 = math.pi / PHI

        def qrt_damping(x):
            return jnp.sin(C1 * x) * jnp.exp(-(x * x) / PHI) + jnp.cos(C2 * x)

        def ttt_filter(scores):
            int_scores = (jnp.abs(scores) * PHI_INT).astype(jnp.int32)
            mod9 = int_scores % 9
            chaos = (mod9 == 0) | (mod9 == 3) | (mod9 == 6)
            penalty = jnp.where(chaos, jnp.float32(PHI_INV), jnp.float32(1.0))
            return scores * penalty
        B, S, _ = x.shape

        def split_heads(t):
            return t.reshape(B, S, NHEAD, D_K).transpose(0, 2, 1, 3)
        q = split_heads(x @ Wq + bq)
        k = split_heads(x @ Wk + bk)
        v = split_heads(x @ Wv + bv)
        scores = jnp.einsum('bhqd,bhkd->bhqk', q, k) / jnp.float32(math.sqrt(D_K))
        scores = ttt_filter(scores)
        attn = jax.nn.softmax(scores, axis=-1)
        attn = attn * qrt_damping(attn)
        ctx = jnp.einsum('bhqk,bhkd->bhqd', attn, v)
        ctx = ctx.transpose(0, 2, 1, 3).reshape(B, S, D_LATTICE)
        return ctx @ Wo + bo

    def _L3_ffn_ref(x, gamma, beta, Wr, br, W1, b1, W2, b2):
        import jax, jax.numpy as jnp
        import numpy as np
        E = 8
        K = 2
        D = 64
        H = 128
        DOUT = 64
        EPS = 1e-05
        mu = jnp.mean(x, axis=-1, keepdims=True)
        var = jnp.mean(jnp.square(x - mu), axis=-1, keepdims=True)
        xn = (x - mu) * jax.lax.rsqrt(var + EPS) * gamma + beta
        logits = jnp.einsum('bsd,de->bse', xn, Wr) + br
        top_vals, top_idx = jax.lax.top_k(logits, K)
        w = jax.nn.softmax(top_vals, axis=-1)
        w_full = jnp.einsum('bsk,bske->bse', w, jax.nn.one_hot(top_idx, E, dtype=w.dtype))
        y = jnp.zeros(x.shape[:-1] + (DOUT,), x.dtype)
        for e in range(E):
            h = jax.nn.gelu(jnp.einsum('bsd,dh->bsh', xn, W1[e]) + b1[e], approximate=False)
            y_e = jnp.einsum('bsh,hd->bsd', h, W2[e]) + b2[e]
            y = y + y_e * w_full[..., e, None]
        return y
    h = _L0_tok_ref(x, L0_tok_W, L0_tok_b)
    h = jnp.concatenate([h, txt], axis=1)
    h = h + _L0_attn_ref(_layernorm(h, axis=-1), L0_attn_in_proj_w, L0_attn_in_proj_b, L0_attn_conv_w, L0_attn_conv_b, L0_attn_x_proj_w, L0_attn_dt_proj_w, L0_attn_dt_proj_b, L0_attn_A_log, L0_attn_D_ssm, L0_attn_out_proj_w, L0_attn_out_proj_b, L0_attn_ln1_g, L0_attn_ln1_b, L0_attn_fc1_w, L0_attn_fc1_b, L0_attn_fc2_w, L0_attn_fc2_b, L0_attn_ln2_g, L0_attn_ln2_b)
    h = h + _L0_ffn_ref(_layernorm(h, axis=-1), L0_ffn_W1, L0_ffn_b1, L0_ffn_Wg, L0_ffn_bg, L0_ffn_Wd, L0_ffn_bd)
    h = h + _L1_attn_ref(_layernorm(h, axis=-1), L1_attn_Wks, L1_attn_Wqs, L1_attn_Wvs, L1_attn_Wo)
    h = h + _L1_ffn_ref(_layernorm(h, axis=-1), L1_ffn_hl_w, L1_ffn_hl_b, L1_ffn_wq, L1_ffn_wk, L1_ffn_wv, L1_ffn_gate_w, L1_ffn_gate_b, L1_ffn_ln_g, L1_ffn_ln_b, L1_ffn_fc1_w, L1_ffn_fc1_b, L1_ffn_fc2_w, L1_ffn_fc2_b, L1_ffn_fnorm_g, L1_ffn_fnorm_b, L1_ffn_fgate_w)
    h = h + _L2_attn_ref(_layernorm(h, axis=-1), L2_attn_w_qkv, L2_attn_w_out, L2_attn_b_out)
    h = h + _L2_ffn_ref(_layernorm(h, axis=-1), L2_ffn_ln1_w, L2_ffn_ln2_w, L2_ffn_wq, L2_ffn_wk, L2_ffn_wv, L2_ffn_wo, L2_ffn_router_w, L2_ffn_w1, L2_ffn_w2, L2_ffn_w3)
    h = h + _L3_attn_ref(_layernorm(h, axis=-1), L3_attn_Wq, L3_attn_bq, L3_attn_Wk, L3_attn_bk, L3_attn_Wv, L3_attn_bv, L3_attn_Wo, L3_attn_bo)
    h = h + _L3_ffn_ref(_layernorm(h, axis=-1), L3_ffn_gamma, L3_ffn_beta, L3_ffn_Wr, L3_ffn_br, L3_ffn_W1, L3_ffn_b1, L3_ffn_W2, L3_ffn_b2)
    return h

_drawn_inputs = setup_inputs


def setup_inputs(seed=0):
    import zlib

    import numpy as np

    out = dict(_drawn_inputs(seed))
    spreads = {'L0_attn_in_proj_b': (0.0, 0.425),
     'L0_attn_conv_b': (0.0, 0.426),
     'L0_attn_D_ssm': (1.0, 0.6),
     'L0_attn_out_proj_b': (0.0, 0.1),
     'L0_attn_ln1_g': (1.0, 0.2),
     'L0_attn_ln1_b': (0.0, 0.1),
     'L0_attn_fc1_b': (0.0, 0.364),
     'L0_attn_fc2_b': (0.0, 0.1),
     'L0_attn_ln2_g': (1.0, 0.2),
     'L0_attn_ln2_b': (0.0, 0.1),
     'L0_ffn_b1': (0.0, 0.416),
     'L0_ffn_bg': (0.0, 0.319),
     'L0_ffn_bd': (0.0, 0.324),
     'L1_ffn_ln_g': (1.0, 0.2),
     'L1_ffn_ln_b': (0.0, 0.314),
     'L1_ffn_fnorm_g': (1.0, 0.2),
     'L1_ffn_fnorm_b': (0.0, 0.302),
     'L2_ffn_ln1_w': (1.0, 0.6),
     'L2_ffn_ln2_w': (1.0, 0.6),
     'L3_ffn_br': (0.0, 0.8)}
    factors = {'L0_tok_b': 3.194,
     'L0_attn_in_proj_w': 4.223,
     'L0_attn_conv_w': 4.348,
     'L0_attn_x_proj_w': 8.0,
     'L0_attn_dt_proj_w': 8.0,
     'L0_attn_dt_proj_b': 8.0,
     'L0_attn_A_log': 8.0,
     'L0_attn_out_proj_w': 4.151,
     'L0_attn_fc1_w': 3.572,
     'L0_attn_fc2_w': 2.835,
     'L0_ffn_W1': 4.162,
     'L0_ffn_Wg': 4.192,
     'L0_ffn_Wd': 4.071,
     'L1_ffn_wq': 4.204,
     'L1_ffn_wk': 4.232,
     'L1_ffn_wv': 3.072,
     'L1_ffn_gate_w': 8.0,
     'L1_ffn_gate_b': 8.0,
     'L1_ffn_fc1_w': 4.063,
     'L1_ffn_fc1_b': 4.193,
     'L1_ffn_fc2_w': 3.877,
     'L1_ffn_fc2_b': 3.057,
     'L2_attn_b_out': 3.846,
     'L2_ffn_wq': 8.0,
     'L2_ffn_wk': 8.0,
     'L2_ffn_wv': 4.166,
     'L2_ffn_wo': 4.099,
     'L2_ffn_router_w': 4.225,
     'L2_ffn_w1': 4.206,
     'L2_ffn_w2': 4.18,
     'L2_ffn_w3': 4.169,
     'L3_attn_bq': 4.241,
     'L3_attn_bk': 4.237,
     'L3_attn_bv': 8.0,
     'L3_attn_bo': 8.0,
     'L3_ffn_gamma': 8.0,
     'L3_ffn_beta': 8.0,
     'L3_ffn_Wr': 8.0,
     'L3_ffn_W1': 8.0,
     'L3_ffn_b1': 27.951,
     'L3_ffn_W2': 8.0,
     'L3_ffn_b2': 38.479}
    for name, (base, spread) in spreads.items():
        noise = np.random.default_rng([zlib.crc32(name.encode()), seed]).standard_normal(out[name].shape)
        drawn = base * np.exp(spread * noise) if base else spread * noise
        out[name] = jnp.asarray(drawn.astype(out[name].dtype))
    for name, factor in factors.items():
        out[name] = (out[name] * factor).astype(out[name].dtype)
    return out
```

```python
import math
from contextlib import ExitStack

import numpy as np

import concourse.bass as bass
from concourse import mybir

F32 = mybir.dt.float32
BF16 = mybir.dt.bfloat16
I32 = mybir.dt.int32
U32 = mybir.dt.uint32
ALU = mybir.AluOpType
ACT = mybir.ActivationFunctionType
X = mybir.AxisListType.X

B = 8
PATCH, IMG_C, IMG = 16, 3, 96
GRID = IMG // PATCH
N_IMG = GRID * GRID
N_TXT = 128
SEQ = N_IMG + N_TXT
TP = SEQ // 2
D = 64
G = 2
U = 2 * G
COLS = G * SEQ
GROUPS = 2
PASSES = B // (G * GROUPS)
PDIM = PATCH * PATCH * IMG_C
KC = PDIM // 128
DI, NST, DTR, DCONV = 128, 16, 16, 4
NEG = -float(2.0 ** 100)
MAGIC = 12582912.0
BANK = 512


class Steps:

    def __init__(self, sem):
        self.sem, self.n = sem, 0

    def did(self, ins):
        ins.then_inc(self.sem, 1)
        self.n += 1

    def wait(self, eng):
        eng.wait_ge(self.sem, self.n)


class Core:
    pass


def wide(ap, n):
    return ap.unsqueeze(2).broadcast_to([ap.shape[0], ap.shape[1], n])


def each(ap, n):
    return ap.unsqueeze(1).broadcast_to([ap.shape[0], n, ap.shape[1]])


def allocate(nc, ctx, w):

    def sb(name, shape, dt=F32):
        return ctx.enter_context(nc.sbuf_tensor(name, shape, dt))

    w.banks = ctx.enter_context(nc.psum_tensor("banks", [128, 8, BANK], F32))
    w.psum = [w.banks[:, i, :] for i in range(8)]
    NT = GROUPS * U
    w.h = sb("h", [TP, NT, D])
    w.xT = sb("xT", [D + 1, GROUPS, COLS])
    w.xn = sb("xn", [TP, NT, D])
    w.resid = sb("resid", [TP, 2, 4, 16])
    w.in_first = sb("in_first", [TP, 2, 4, 16], U32)
    w.ident = sb("ident", [128, 128])
    w.ident_b = sb("ident_b", [TP, TP], BF16)
    w.causal01 = sb("causal01", [TP, 3 * TP])
    w.maskT = sb("maskT", [TP, SEQ], BF16)
    w.maskQ = sb("maskQ", [TP, SEQ], BF16)
    w.rank = sb("rank", [TP, 8])
    w.sel_bc = sb("sel_bc", [96, 2 * NST, 128], BF16)
    w.sel_map = sb("sel_map", [96, 16, TP], BF16)
    w.rope_cos = sb("rope_cos", [128, SEQ])
    w.rope_sin = sb("rope_sin", [128, SEQ])
    w.ones_row = sb("ones_row", [1, 128])
    w.neg_half = sb("neg_half", [128, 64])
    w.img_tok = sb("img_tok", [N_IMG, B, D])
    w.inT = sb("inT", [D + 1, 2 * DI])
    w.conv_w = sb("conv_w", [DI, DCONV])
    w.conv_b = sb("conv_b", [DI, 1])
    w.xp_dtT = sb("xp_dtT", [DI, DTR])
    w.xp_bcT = sb("xp_bcT", [DI, 3, 2 * NST])
    w.dtT = sb("dtT", [DTR, DI])
    w.dt_b = sb("dt_b", [DI, 1])
    w.A = sb("A", [DI, NST])
    w.D_ssm = sb("D_ssm", [DI, 1])
    w.outT = sb("outT", [DI, D])
    w.out_b = sb("out_b", [1, D])
    w.m_ln1_g = sb("m_ln1_g", [TP, D])
    w.m_ln1_b = sb("m_ln1_b", [TP, D])
    w.m_ln2_g = sb("m_ln2_g", [TP, D])
    w.m_ln2_b = sb("m_ln2_b", [TP, D])
    w.fc1T = sb("fc1T", [D + 1, 256])
    w.fc2T = sb("fc2T", [128, 2, D])
    w.fc2_b = sb("fc2_b", [1, D])
    w.f0_W1 = sb("f0_W1", [D + 1, 256])
    w.f0_Wg = sb("f0_Wg", [128, 2, 8])
    w.f0_bg = sb("f0_bg", [1, 8])
    w.f0_Wd = sb("f0_Wd", [128, 2, 8, D])
    w.f0_bd = sb("f0_bd", [1, 8, D])
    w.a1_Wk = sb("a1_Wk", [D, 8, 32])
    w.a1_Wq = sb("a1_Wq", [D, 8, 32])
    w.a1_Wvo = sb("a1_Wvo", [D, 8, D])
    w.f1_hlT = sb("f1_hlT", [D + 1, D])
    w.f1_qT = sb("f1_qT", [D, 4, 128])
    w.f1_kT = sb("f1_kT", [D, 4, 128])
    w.f1_vT = sb("f1_vT", [D, D])
    w.f1_gateT = sb("f1_gateT", [128, 2, 16])
    w.f1_gate_b = sb("f1_gate_b", [1, 16])
    w.f1_fc1T = sb("f1_fc1T", [D + 1, D])
    w.f1_fc2T = sb("f1_fc2T", [D + 1, D])
    w.f1_ln_g = sb("f1_ln_g", [TP, 16])
    w.f1_ln_b = sb("f1_ln_b", [TP, 16])
    w.f1_fn_g = sb("f1_fn_g", [TP, 16])
    w.f1_fn_b = sb("f1_fn_b", [TP, 16])
    w.f1_fgT = sb("f1_fgT", [D, 4])
    w.a2_Wq = sb("a2_Wq", [128, 4, D])
    w.a2_kT = sb("a2_kT", [D, 8, D])
    w.a2_vT = sb("a2_vT", [D, 8, D])
    w.a2_woT = sb("a2_woT", [128, 4, D])
    w.a2_M = sb("a2_M", [D + 1, G * GROUPS, D])
    w.f2_ln1 = sb("f2_ln1", [D, 1])
    w.f2_ln2 = sb("f2_ln2", [D, 1])
    w.f2_qT = sb("f2_qT", [D, 2, 128])
    w.f2_kT = sb("f2_kT", [D, 2, 128])
    w.f2_vT = sb("f2_vT", [D, 32])
    w.f2_oT = sb("f2_oT", [D, D])
    w.f2_routerT = sb("f2_routerT", [D, 8])
    w.f2_w1T = sb("f2_w1T", [D, 16, 85])
    w.f2_w3T = sb("f2_w3T", [D, 16, 85])
    w.f2_w2T = sb("f2_w2T", [85, 16, D])
    w.a3_Wq = sb("a3_Wq", [D + 1, 8, D])
    w.a3_Wk = sb("a3_Wk", [D + 1, 8, D])
    w.a3_Wvo = sb("a3_Wvo", [D + 1, 8, D])
    w.a3_bo = sb("a3_bo", [1, D])
    w.f3_g = sb("f3_g", [D, 1])
    w.f3_b = sb("f3_b", [D, 1])
    w.f3_Wr = sb("f3_Wr", [D + 1, 8])
    w.f3_W1 = sb("f3_W1", [D + 1, 8, 128])
    w.f3_W2 = sb("f3_W2", [128, 8, D])
    w.f3_b2 = sb("f3_b2", [1, 8, D])


def load_weights(nc, d, w, loaded_p):
    with ExitStack() as ctx:
        def sb(name, shape, dt=F32):
            return ctx.enter_context(nc.sbuf_tensor(name, shape, dt))

        sems = []

        def sem(name):
            sems.append(ctx.enter_context(nc.semaphore(name)))
            return sems[-1]

        n_tok = sb("n_tok", [D, IMG_C, PATCH, PATCH])
        image = sb("image", [IMG, B, IMG_C, IMG])
        tokB = sb("tokB", [IMG, IMG_C * PATCH, 2, D])
        tok6 = sb("tok6", [D, IMG_C, PATCH, GRID, PATCH])
        row_half = sb("row_half", [IMG, 2])
        img_featT = sb("img_featT", [D, B, GRID, GRID])
        tok_b = sb("tok_b", [1, D])
        n_in = sb("n_in", [128, 2, D])
        n_xp = sb("n_xp", [DTR + 2 * NST, DI])
        n_dt = sb("n_dt", [DI, DTR])
        n_out = sb("n_out", [D, DI])
        n_fc1 = sb("n_fc1", [128, 2, D])
        n_fc2 = sb("n_fc2", [D, 256])
        n_Wv1 = sb("n_Wv1", [D, 8, D])
        a1_WvT, a1_Wo = sb("a1_WvT", [128, 4, D]), sb("a1_Wo", [128, 4, D])
        a3_WvT, a3_Wo = sb("a3_WvT", [128, 4, D + 1]), sb("a3_Wo", [128, 4, D])
        n_hl = sb("n_hl", [D, D])
        n_q = sb("n_q", [128, 320])
        n_k = sb("n_k", [128, 320])
        n_v = sb("n_v", [D, D])
        n_f1 = sb("n_f1", [D, D])
        n_f2 = sb("n_f2", [D, D])
        n_gate = sb("n_gate", [16, 256])
        n_fg = sb("n_fg", [4, D])
        n_kv = sb("n_kv", [128, 8, D])
        n_wo2 = sb("n_wo2", [D, 512])
        n_q2 = sb("n_q2", [128, 2, D])
        n_k2 = sb("n_k2", [128, 2, D])
        n_v2 = sb("n_v2", [32, D])
        n_o2 = sb("n_o2", [D, D])
        n_r2 = sb("n_r2", [8, D])
        n_w1 = sb("n_w1", [85, 16, D])
        n_w3 = sb("n_w3", [85, 16, D])
        n_w2 = sb("n_w2", [D, 8, 170])
        n_Wv3 = sb("n_Wv3", [D + 1, 8, D])
        n_sel_bc, n_sel_map = sb("n_sel_bc", [96, 2 * NST, 128]), sb("n_sel_map", [96, 16, TP])
        n_maskT, n_maskQ = sb("n_maskT", [TP, SEQ]), sb("n_maskQ", [TP, SEQ])
        mean_k = sb("mean_k", [D, 2, 8])
        a_pos = sb("a_pos", [DI, NST])

        zeroed, loaded_s, loaded_a = sem("zeroed"), sem("loaded_s"), sem("loaded_a")
        turned, copied_v, copied_a = sem("turned"), sem("copied_v"), sem("copied_a")
        vo_done, decay_exp, centred, scaled = sem("vo_done"), sem("decay_exp"), sem("centred"), sem("scaled")

        image_in, tok_turned, tok_copied, tok_ps, feat_ready, img_turned = map(
            sem, ("image_in", "tok_turned", "tok_copied", "tok_ps", "feat_ready", "img_turned"))
        tok_spread, narrowed = sem("tok_spread"), sem("narrowed")
        CP = IMG_C * PATCH
        turns = [(n_in[:, c, :], w.inT[0:D, c * 128:(c + 1) * 128]) for c in range(2)]
        turns += [(n_xp[:, :], None)]
        XP = len(turns) - 1
        turns += [(n_dt[:, :], w.dtT[:, :]), (n_out[:, :], w.outT[:, :])]
        turns += [(n_fc1[:, c, :], w.fc1T[0:D, c * 128:(c + 1) * 128]) for c in range(2)]
        turns += [(n_fc2[:, c * 128:(c + 1) * 128], w.fc2T[:, c, :]) for c in range(2)]
        turns += [(n_Wv1[:, 2 * c:2 * c + 2, :].rearrange("p a b -> p (a b)"), a1_WvT[:, c, :]) for c in range(4)]
        turns += [(n_hl[:, :], w.f1_hlT[0:D, :])]
        turns += [(n_q[:, n * D:(n + 1) * D], w.f1_qT[:, n, :]) for n in range(4)]
        turns += [(n_k[:, n * D:(n + 1) * D], w.f1_kT[:, n, :]) for n in range(4)]
        turns += [(n_v[:, :], w.f1_vT[:, :]), (n_f1[:, :], w.f1_fc1T[0:D, :]), (n_f2[:, :], w.f1_fc2T[0:D, :])]
        turns += [(n_gate[:, c * 128:(c + 1) * 128], w.f1_gateT[:, c, :]) for c in range(2)]
        turns += [(n_fg[:, :], w.f1_fgT[:, :])]
        for c in range(4):
            turns += [(n_kv[:, c, :], w.a2_kT[:, 2 * c:2 * c + 2, :].rearrange("p a b -> p (a b)")),
                      (n_kv[:, 4 + c, :], w.a2_vT[:, 2 * c:2 * c + 2, :].rearrange("p a b -> p (a b)")),
                      (n_wo2[:, c * 128:(c + 1) * 128], w.a2_woT[:, c, :])]
        for c in range(2):
            turns += [(n_q2[:, c, :], w.f2_qT[:, c, :]), (n_k2[:, c, :], w.f2_kT[:, c, :])]
        turns += [(n_v2[:, :], w.f2_vT[:, :]), (n_o2[:, :], w.f2_oT[:, :]), (n_r2[:, :], w.f2_routerT[:, :])]
        for c in range(16):
            turns += [(n_w1[:, c, :], w.f2_w1T[:, c, :]), (n_w3[:, c, :], w.f2_w3T[:, c, :]),
                      (n_w2[:, c // 2, (c % 2) * 85:(c % 2 + 1) * 85], w.f2_w2T[:, c, :])]
        turns += [(n_Wv3[:, 2 * c:2 * c + 2, :].rearrange("p a b -> p (a b)"), a3_WvT[:, c, :]) for c in range(4)]
        fours = [turns[i:i + 4] for i in range(0, len(turns), 4)]
        assert XP < 4

        def slot(i, j, rows, cols):
            return w.psum[i % 6][0:rows, j * 128:j * 128 + cols]

        block = ctx.enter_context(nc.Block())
        row = lambda ap: ap.rearrange("(a n) -> a n", a=1)
        col = lambda ap: ap.rearrange("(n a) -> n a", a=1)
        spread = lambda ap, p: row(ap).broadcast_to([p, ap.shape[0]])

        direct = [
            (n_tok[:, :, :, :].rearrange("p a b c -> p (a b c)"), d["L0_tok_W"]), (tok_b[:, :], row(d["L0_tok_b"])),
            (row_half[:, :], d["c_row_half"]), (w.ident[:, :], d["c_ident"]),
            (n_in[:, :, :], d["L0_attn_in_proj_w"].rearrange("(c p) k -> p c k", p=128)),
            (w.inT[D:D + 1, :], row(d["L0_attn_in_proj_b"])),
            (w.conv_w[:, :], d["L0_attn_conv_w"]), (w.conv_b[:, :], col(d["L0_attn_conv_b"])),
            (n_xp[:, :], d["L0_attn_x_proj_w"]), (n_dt[:, :], d["L0_attn_dt_proj_w"]),
            (w.dt_b[:, :], col(d["L0_attn_dt_proj_b"])), (w.A[:, :], d["L0_attn_A_log"]),
            (w.D_ssm[:, :], col(d["L0_attn_D_ssm"])), (n_out[:, :], d["L0_attn_out_proj_w"]),
            (w.out_b[:, :], row(d["L0_attn_out_proj_b"])),
            (n_sel_bc[:, :, :], d["c_sel_bc"]),
            (n_fc1[:, :, :], d["L0_attn_fc1_w"].rearrange("(c p) k -> p c k", p=128)),
            (w.fc1T[D:D + 1, :], row(d["L0_attn_fc1_b"])), (n_fc2[:, :], d["L0_attn_fc2_w"]),
            (w.fc2_b[:, :], row(d["L0_attn_fc2_b"])),
            (w.f0_W1[0:D, :], d["L0_ffn_W1"]), (w.f0_W1[D:D + 1, :], row(d["L0_ffn_b1"])),
            (w.f0_Wg[:, :, :], d["L0_ffn_Wg"].rearrange("(c p) e -> p c e", p=128)),
            (w.f0_bg[:, :], row(d["L0_ffn_bg"])),
            (w.f0_Wd[:, 0, :, :], d["L0_ffn_Wd"][:, 0:128, :].rearrange("e p n -> p e n")),
            (w.f0_Wd[:, 1, :, :], d["L0_ffn_Wd"][:, 128:256, :].rearrange("e p n -> p e n")),
            (w.f0_bd[0:1, :, :], d["L0_ffn_bd"].rearrange("(a e) n -> a e n", a=1)),
            (w.a1_Wk[:, :, :], d["L1_attn_Wks"].rearrange("h p k -> p h k")),
            (w.a1_Wq[:, :, :], d["L1_attn_Wqs"].rearrange("h p k -> p h k")),
            (n_Wv1[:, :, :], d["L1_attn_Wvs"].rearrange("h p k -> p h k")),
            (a1_Wo[:, :, :], d["L1_attn_Wo"].rearrange("(c a) p k -> (a p) c k", a=2)),
            (n_hl[:, :], d["L1_ffn_hl_w"].rearrange("n o k -> (n o) k")),
            (w.f1_hlT[D:D + 1, :], d["L1_ffn_hl_b"].rearrange("(a n) o -> a (n o)", a=1)),
            (w.f1_gate_b[:, :], d["L1_ffn_gate_b"].rearrange("(a n) o -> a (n o)", a=1)),
            (n_fg[:, :], d["L1_ffn_fgate_w"]),
            (w.a2_Wq[:, :, :], d["L2_attn_w_qkv"][0:512, :].rearrange("(c p) k -> p c k", p=128)),
            (n_kv[:, :, :], d["L2_attn_w_qkv"][512:1536, :].rearrange("(c p) k -> p c k", p=128)),
            (n_wo2[:, :], d["L2_attn_w_out"]),
            (w.f2_ln1[:, :], col(d["L2_ffn_ln1_w"])), (w.f2_ln2[:, :], col(d["L2_ffn_ln2_w"])),
            (n_v2[:, :], d["L2_ffn_wv"]), (n_o2[:, :], d["L2_ffn_wo"]), (n_r2[:, :], d["L2_ffn_router_w"]),
            (n_w1[:, :, :], d["L2_ffn_w1"].rearrange("e (c p) k -> p (e c) k", p=85)),
            (n_w3[:, :, :], d["L2_ffn_w3"].rearrange("e (c p) k -> p (e c) k", p=85)),
            (n_w2[:, :, :], d["L2_ffn_w2"].rearrange("e p f -> p e f")),
            (w.a3_Wq[0:D, :, :], d["L3_attn_Wq"].rearrange("p (h k) -> p h k", h=8)),
            (w.a3_Wk[0:D, :, :], d["L3_attn_Wk"].rearrange("p (h k) -> p h k", h=8)),
            (n_Wv3[0:D, :, :], d["L3_attn_Wv"].rearrange("p (h k) -> p h k", h=8)),
            (w.a3_Wq[D:D + 1, :, :], row(d["L3_attn_bq"]).rearrange("a (h k) -> a h k", h=8)),
            (w.a3_Wk[D:D + 1, :, :], row(d["L3_attn_bk"]).rearrange("a (h k) -> a h k", h=8)),
            (n_Wv3[D:D + 1, :, :], row(d["L3_attn_bv"]).rearrange("a (h k) -> a h k", h=8)),
            (a3_Wo[:, :, :], d["L3_attn_Wo"].rearrange("(c p) k -> p c k", p=128)),
            (w.a3_bo[:, :], row(d["L3_attn_bo"])),
            (w.f3_g[:, :], col(d["L3_ffn_gamma"])), (w.f3_b[:, :], col(d["L3_ffn_beta"])),
            (w.f3_Wr[0:D, :], d["L3_ffn_Wr"]), (w.f3_Wr[D:D + 1, :], row(d["L3_ffn_br"])),
            (w.f3_W1[0:D, :, :], d["L3_ffn_W1"].rearrange("e p n -> p e n")),
            (w.f3_W1[D:D + 1, :, :], d["L3_ffn_b1"].rearrange("(a e) n -> a e n", a=1)),
            (w.f3_W2[:, :, :], d["L3_ffn_W2"].rearrange("e p n -> p e n")),
            (w.f3_b2[:, :, :], d["L3_ffn_b2"].rearrange("(a e) n -> a e n", a=1)),
            (w.causal01[:, :], d["c_causal01"]),
            (n_maskT[:, :], d["c_maskT"]), (n_maskQ[:, :], d["c_maskQ"]), (w.rank[:, :], d["c_rank"]),
            (n_sel_map[:, :, :], d["c_sel_map"]),
            (w.rope_cos[:, :], d["c_rope_cos"]), (w.rope_sin[:, :], d["c_rope_sin"]),
        ]
        for a, n, k in ((w.m_ln1_g, "L0_attn_ln1_g", D), (w.m_ln1_b, "L0_attn_ln1_b", D),
                        (w.m_ln2_g, "L0_attn_ln2_g", D), (w.m_ln2_b, "L0_attn_ln2_b", D),
                        (w.f1_ln_g, "L1_ffn_ln_g", 16), (w.f1_ln_b, "L1_ffn_ln_b", 16),
                        (w.f1_fn_g, "L1_ffn_fnorm_g", 16), (w.f1_fn_b, "L1_ffn_fnorm_b", 16)):
            direct.append((a[:, :], spread(d[n], TP)))
        for b in range(G * GROUPS):
            direct.append((w.a2_M[D:D + 1, b, :], row(d["L2_attn_b_out"])))
        for n in range(4):
            direct.append((w.f1_fc1T[D:D + 1, 16 * n:16 * n + 16], row(d["L1_ffn_fc1_b"])))
            direct.append((w.f1_fc2T[D:D + 1, 16 * n:16 * n + 16], row(d["L1_ffn_fc2_b"])))

        sparse = []
        for e in range(4):
            for tile, name in ((n_q, "L1_ffn_wq"), (n_k, "L1_ffn_wk")):
                src = d[name][:, e, :, :] if tile is n_q else d[name]
                dst = tile[32 * e:32 * e + 16, :].rearrange("p (n c) -> p n c", c=80)[:, :, 0:16]
                sparse.append((dst, src.rearrange("n o k -> o n k")))
        for n in range(4):
            at = slice(16 * n, 16 * n + 16)
            sparse += [(n_v[at, at], d["L1_ffn_wv"][n]), (n_f1[at, at], d["L1_ffn_fc1_w"]),
                       (n_f2[at, at], d["L1_ffn_fc2_w"]),
                       (n_gate[4 * n:4 * n + 4, 64 * n:64 * n + 64], d["L1_ffn_gate_w"][n])]
            sparse += [(n_q2[32 * n:32 * n + 16, 0, :], d["L2_ffn_wq"][16 * n:16 * n + 16, :]),
                       (n_q2[32 * n:32 * n + 8, 1, :], d["L2_ffn_wq"][16 * n + 8:16 * n + 16, :]),
                       (n_q2[32 * n + 8:32 * n + 16, 1, :], d["L2_ffn_wq"][16 * n:16 * n + 8, :])]
            m = 16 * (n // 2)
            sparse += [(n_k2[32 * n:32 * n + 16, 0, :], d["L2_ffn_wk"][m:m + 16, :]),
                       (n_k2[32 * n:32 * n + 8, 1, :], d["L2_ffn_wk"][m + 8:m + 16, :]),
                       (n_k2[32 * n + 8:32 * n + 16, 1, :], d["L2_ffn_wk"][m:m + 8, :])]
        zero = [n_q, n_k, n_v, n_f1, n_f2, n_gate, n_q2, n_k2]
        n_half = len(direct) // 2

        def all_loaded(eng):
            eng.wait_ge(loaded_s, 16 * n_half)
            eng.wait_ge(loaded_a, 16 * (len(direct) - n_half))
            eng.wait_ge(loaded_p, 16 * len(sparse))

        @block.sync
        def _(sp):
            for b in range(B):
                sp.dma_start(image[:, b, :, :], d["x"][b].rearrange("c y x -> y c x")).then_inc(image_in, 16)
            for dst, src in direct[:n_half]:
                sp.dma_start(dst, src).then_inc(loaded_s, 16)
            sp.wait_ge(loaded_s, 16 * n_half)

        @block.gpsimd
        def _(pool):
            for t in zero:
                pool.memset(t[:], 0.0).then_inc(zeroed, 1)
            rest = [(w.ones_row[:, :], 1.0), (w.neg_half[:, :], -0.5), (w.in_first[:], 1), (w.resid[:], 0.0),
                    (w.xT[D:D + 1, :, :], 1.0)]
            for i, (t, value) in enumerate(rest):
                pool.wait_ge(zeroed, len(zero) + i)
                pool.memset(t, value).then_inc(zeroed, 1)
            pool.wait_ge(zeroed, len(zero) + len(rest))
            for dst, src in sparse:
                pool.dma_start(dst, src).then_inc(loaded_p, 16)
            pool.wait_ge(loaded_p, 16 * len(sparse))
            all_loaded(pool)
            for i, (dst, src) in enumerate(((w.sel_bc[:, :, :], n_sel_bc[:, :, :]), (w.sel_map[:, :, :], n_sel_map[:, :, :]),
                                            (w.maskT[:, :], n_maskT[:, :]), (w.maskQ[:, :], n_maskQ[:, :]),
                                            (w.ident_b[:, :], w.ident[0:TP, 0:TP]))):
                if i:
                    pool.wait_ge(narrowed, i)
                pool.tensor_copy(dst, src).then_inc(narrowed, 1)

        @block.tensor
        def _(pe):
            all_loaded(pe)
            for i, four in enumerate(fours):
                if i >= 6:
                    pe.wait_ge(copied_v if i % 2 == 0 else copied_a, (i - 6) // 2 + 1)
                for j, (src, _) in enumerate(four):
                    r, c = src.shape
                    last = pe.transpose(slot(i, j, c, r), src, w.ident[0:r, 0:r])
                last.then_inc(turned, 1)
            pe.wait_ge(copied_v, (len(fours) + 1) // 2)
            pe.wait_ge(copied_a, len(fours) // 2)
            pe.wait_ge(tok_spread, IMG_C)
            for k in range(CP):
                src = tok6[:, k // PATCH, k % PATCH, :, :].rearrange("p y r -> p (y r)")
                last = pe.transpose(w.psum[k // 8][0:IMG, (k % 8) * D:(k % 8 + 1) * D], src, w.ident[0:D, 0:D])
                if k % 8 == 7:
                    last.then_inc(tok_turned, 1)
            pe.wait_ge(tok_copied, 2 * CP // 8)
            pe.wait_ge(image_in, 16 * B)
            for c in range(GRID // 2):
                rows = slice(32 * c, 32 * c + 32)
                for k in range(CP):
                    cols = image[rows, :, k // PATCH, k % PATCH::PATCH]
                    last = pe.matmul(w.psum[c][:, 0:B * GRID], tokB[rows, k, :, :].rearrange("p a n -> p (a n)"), cols,
                                     start=(k == 0), stop=(k == CP - 1))
                last.then_inc(tok_ps, 1)
            pe.wait_ge(feat_ready, GRID)
            for b in range(B):
                o = w.psum[4][0:N_IMG, b * D:(b + 1) * D]
                pe.matmul(o, img_featT[:, b, :, :].rearrange("p y x -> p (y x)"), w.ident[0:D, 0:D],
                          start=True, stop=False)
                last = pe.matmul(o, w.ones_row[:, 0:N_IMG], tok_b[:, :], start=False, stop=True)
            last.then_inc(img_turned, 1)
            for i, (vT, wo) in enumerate(((a1_WvT, a1_Wo), (a3_WvT, a3_Wo))):
                rows = vT.shape[2]
                for hd in range(8):
                    at = slice(64 * (hd % 2), 64 * (hd % 2) + 64)
                    last = pe.matmul(w.psum[2 * i + hd % 2][0:rows, hd // 2 * D:(hd // 2 + 1) * D], vT[at, hd // 2, :],
                                     wo[at, hd // 2, :], start=True, stop=True)
                last.then_inc(vo_done, 1)

        @block.vector
        def _(dve):
            all_loaded(dve)
            for c in range(IMG_C):
                dve.tensor_copy(tok6[:, c, :, :, :], n_tok[:, c, :, :].rearrange("p r k -> p k r").unsqueeze(2)
                                .broadcast_to([D, PATCH, GRID, PATCH])).then_inc(tok_spread, 1)
            for i in range(0, len(fours), 2):
                dve.wait_ge(turned, i + 1)
                for j, (src, dst) in enumerate(fours[i]):
                    r, c = src.shape
                    if 4 * i + j == XP:
                        dve.tensor_copy(w.xp_dtT[:, :], slot(i, j, c, r)[:, 0:DTR])
                        ins = dve.tensor_copy(w.xp_bcT[:, :, :], each(slot(i, j, c, r)[:, DTR:r], 3))
                    else:
                        ins = dve.tensor_copy(dst, slot(i, j, c, r))
                ins.then_inc(copied_v, 1)
            dve.wait_ge(copied_v, (len(fours) + 1) // 2)
            dve.wait_ge(copied_a, len(fours) // 2)
            for i, t in enumerate((w.a2_kT, w.a2_vT)):
                dve.tensor_reduce(mean_k[:, i, :], t[:, :, :], X, ALU.add).then_inc(centred, 1)
            for i, t in enumerate((w.a2_kT, w.a2_vT)):
                dve.wait_ge(centred, i + 1)
                dve.scalar_tensor_tensor(out=t[:, :, :], in0=wide(mean_k[:, i, :], D), scalar=1.0 / D,
                                         in1=t[:, :, :], op0=ALU.mult, op1=ALU.subtract, reverse1=True)
            dve.tensor_scalar(w.inT[:, DI:2 * DI], w.inT[:, DI:2 * DI], 0.5, None, ALU.mult)
            dve.tensor_scalar(w.conv_w[:, :], w.conv_w[:, :], 0.5, None, ALU.mult)
            dve.tensor_scalar(w.conv_b[:, :], w.conv_b[:, :], 0.5, None, ALU.mult)
            dve.tensor_scalar(w.f1_qT[:, :, :], w.f1_qT[:, :, :], 4.0, None, ALU.mult)
            dve.tensor_scalar(w.f2_qT[:, :, :], w.f2_qT[:, :, :], w.f2_ln1[:, 0:1], 0.25, ALU.mult, ALU.mult)
            dve.tensor_scalar(w.f2_kT[:, :, :], w.f2_kT[:, :, :], w.f2_ln1[:, 0:1], None, ALU.mult)
            dve.tensor_scalar(w.f2_vT[:, :], w.f2_vT[:, :], w.f2_ln1[:, 0:1], None, ALU.mult)
            for t in (w.f2_w1T, w.f2_w3T):
                dve.tensor_scalar(t[:, :, :], t[:, :, :], w.f2_ln2[:, 0:1], None, ALU.mult)
            dve.tensor_scalar(w.f2_routerT[:, :], w.f2_routerT[:, :], w.f2_ln2[:, 0:1], None, ALU.mult)
            dve.wait_ge(decay_exp, 1)
            dve.tensor_scalar(w.A[:, :], a_pos[:, :], -1.0, None, ALU.mult)
            for k in range(CP // 8):
                dve.wait_ge(tok_turned, k + 1)
                for half in range(2):
                    dve.tensor_scalar(tokB[:, 8 * k:8 * k + 8, half, :], w.psum[k][0:IMG, :].rearrange(
                        "p (k n) -> p k n", k=8), row_half[:, half:half + 1], None, ALU.mult).then_inc(tok_copied, 1)
            for c in range(GRID // 2):
                dve.wait_ge(tok_ps, c + 1)
                for half in range(2):
                    dve.tensor_copy(img_featT[:, :, 2 * c + half, :], w.psum[c][half * D:half * D + D, 0:B * GRID]
                                    .rearrange("p (b x) -> p b x", b=B)).then_inc(feat_ready, 1)
            dve.wait_ge(img_turned, 1)
            dve.tensor_copy(w.img_tok[:, :, :], w.psum[4][0:N_IMG, :].rearrange("p (b n) -> p b n", b=B))
            dve.wait_ge(vo_done, 2)
            for i, (t, rows) in enumerate(((w.a1_Wvo, D), (w.a3_Wvo, D + 1))):
                for odd in range(2):
                    dve.tensor_copy(t[:, odd:8:2, :], w.psum[2 * i + odd][0:rows, 0:4 * D].rearrange(
                        "p (h n) -> p h n", h=4))

        @block.scalar
        def _(act):
            for dst, src in direct[n_half:]:
                act.dma_start(dst, src).then_inc(loaded_a, 16)
            all_loaded(act)
            act.activation(a_pos[:, :], w.A[:, :], ACT.Exp).then_inc(decay_exp, 1)
            for i in range(1, len(fours), 2):
                act.wait_ge(turned, i + 1)
                for j, (src, dst) in enumerate(fours[i]):
                    r, c = src.shape
                    ins = act.activation(dst, slot(i, j, c, r), ACT.Copy)
                ins.then_inc(copied_a, 1)

        return sems


def wait_back(steps, eng, back):
    eng.wait_ge(steps.sem, steps.n - back)


def normalize(dve, steps, groups, eps, var_ready, rstd_ready, base, centre=True, ready=None):
    back = len(groups) - 1
    f = groups[0][0].shape[2]
    if centre:
        for src, dst, squares, sums in groups:
            steps.did(dve.tensor_reduce(sums, src, X, ALU.add))
        for src, dst, squares, sums in groups:
            wait_back(steps, dve, back)
            steps.did(dve.scalar_tensor_tensor(out=dst, in0=wide(sums, f), scalar=1.0 / f, in1=src,
                                               op0=ALU.mult, op1=ALU.subtract, reverse1=True))
    for src, dst, squares, sums in groups:
        if centre:
            wait_back(steps, dve, back)
        x = dst if centre else src
        steps.did(dve.tensor_tensor(squares, x, x, ALU.mult))
    for src, dst, squares, sums in groups:
        wait_back(steps, dve, back)
        steps.did(dve.tensor_reduce(sums, squares, X, ALU.add))
    for i, (src, dst, squares, sums) in enumerate(groups):
        wait_back(steps, dve, back - i)
        dve.tensor_scalar(sums, sums, 1.0 / f, eps, ALU.mult, ALU.add).then_inc(var_ready, 1)
    for i, (src, dst, squares, sums) in enumerate(groups):
        dve.wait_ge(rstd_ready, base + i + 1)
        ins = dve.tensor_tensor(dst, dst if centre else src, wide(sums, f), ALU.mult)
        if ready is None:
            steps.did(ins)
        else:
            ins.then_inc(ready, 1)


def roots(pool, w, all_sums, var_ready, rstd_ready, base):
    for i, sums in enumerate(all_sums):
        pool.wait_ge(var_ready, base + i + 1)
        half = w.neg_half[0:sums.shape[0], 0:sums.shape[1]]
        pool.tensor_tensor(sums, sums, half, ALU.pow).then_inc(rstd_ready, 1)


def tiles(t, g):
    return t[:, g * U:(g + 1) * U, :]


def turn_tokens(pe, w, bank, src):
    f = src.shape[2]
    for u in range(U):
        last = pe.transpose(w.psum[bank][0:f, u * TP:(u + 1) * TP], src[:, u, :], w.ident[0:TP, 0:TP])
    return last


def tok(nc, d, w, p):
    NB = G * GROUPS
    with ExitStack() as ctx:
        text_in, placed = ctx.enter_context(nc.semaphore("text_in")), ctx.enter_context(nc.semaphore("placed"))
        block = ctx.enter_context(nc.Block())

        @block.sync
        def _(sp):
            txt = d["txt"][bass.ds(p * NB, NB)]
            sp.dma_start(w.h[N_IMG:TP, 0:2 * NB:2, :], txt[:, 0:TP - N_IMG].rearrange("b t k -> t b k")
                         ).then_inc(text_in, 16)
            sp.dma_start(w.h[:, 1:2 * NB:2, :], txt[:, TP - N_IMG:N_TXT].rearrange("b t k -> t b k")
                         ).then_inc(text_in, 16)
            sp.wait_ge(text_in, 32)

        @block.vector
        def _(dve):
            dve.tensor_copy(w.h[0:N_IMG, 0:2 * NB:2, :], w.img_tok[:, bass.ds(p * NB, NB), :]).then_inc(placed, 1)
            dve.wait_ge(placed, 1)

        return text_in, placed


def mamba(nc, d, w):
    Q = NST * GROUPS
    with ExitStack() as ctx:
        def sb(name, shape, dt=F32):
            return ctx.enter_context(nc.sbuf_tensor(name, shape, dt))

        sems = []

        def sem(name):
            sems.append(ctx.enter_context(nc.semaphore(name)))
            return sems[-1]

        NT = GROUPS * U
        squares = sb("squares", [TP, NT, D])
        sums = sb("sums", [TP, NT])
        xi_pad = sb("xi_pad", [DI, GROUPS, G, DCONV - 1 + SEQ])
        conv = sb("conv", [DI, GROUPS, G, SEQ])
        xi = sb("xi", [DI, GROUPS, COLS])
        gate = sb("gate", [DI, GROUPS, COLS])
        dt_low = sb("dt_low", [DTR, GROUPS, COLS])
        expo = sb("expo", [DI, GROUPS, COLS])
        rest = sb("rest", [DI, GROUPS, COLS])
        dt = sb("dt", [DI, GROUPS, COLS])
        dtx = sb("dtx", [DI, GROUPS, COLS])
        bc_parts = sb("bc_parts", [96, GROUPS, COLS], BF16)
        bc_rest = sb("bc_rest", [96, GROUPS, COLS])
        bc_mid = sb("bc_mid", [96, GROUPS, COLS], BF16)
        decay = sb("decay", [DI, 4, G, SEQ])
        drive = sb("drive", [DI, 3, G, SEQ])
        state = sb("state", [DI, 3, G, SEQ])
        prod = sb("prod", [DI, 3, COLS])
        y = sb("y", [DI, GROUPS, COLS])
        mix = sb("mix", [TP, NT, D])
        hid = sb("hid", [128, GROUPS, 2, COLS])
        ffn = sb("ffn", [TP, NT, D])

        v_step, a_step = Steps(sem("v_step")), Steps(sem("a_step"))
        var_ready, rstd_ready, xn_ready, turned, xT_ready = map(sem, ("var", "rstd", "xn_ready", "turned", "xT_ready"))
        xz_ps, pad_ready, gate_ready, conv_ready, xi_ready = map(sem, ("xz", "pad_ready", "gate_ready", "conv_ready", "xi_ready"))
        bcd_ps, low_ready, dt_ps, soft_ready, dt_ready, parts_ready = map(
            sem, ("bcd", "low_ready", "dt_ps", "soft_ready", "dt_ready", "parts_ready"))
        b_ps, c_ps, decay_ready, drive_ready, scanned, prod_ready, y_sum = map(
            sem, ("b_ps", "c_ps", "decay_ready", "drive_ready", "scanned", "prod_ready", "y_sum"))
        y_ready, mix_ps, mixed, y_turned, yT_ready, fc1_ps, hid_ready, fc2_ps, ffn_ready = map(
            sem, ("y_ready", "mix_ps", "mixed", "y_turned", "yT_ready", "fc1_ps", "hid_ready", "fc2_ps", "ffn_ready"))
        zero_ready, tanh_ready, xt_ready = map(sem, ("zero_ready", "tanh_ready", "xt_ready"))
        block = ctx.enter_context(nc.Block())
        ps = w.psum

        @block.gpsimd
        def _(pool):
            pool.memset(xi_pad[:, :, :, 0:DCONV - 1], 0.0).then_inc(zero_ready, 1)
            pool.memset(decay[:, :, :, 0:1], 0.0).then_inc(zero_ready, 1)
            pool.wait_ge(zero_ready, 2)
            for i in range(3):
                roots(pool, w, [sums[:, g * U:(g + 1) * U] for g in range(GROUPS)], var_ready, rstd_ready, i * GROUPS)

        @block.tensor
        def _(pe):
            for g in range(GROUPS):
                pe.wait_ge(xn_ready, g + 1)
                turn_tokens(pe, w, g, tiles(w.xn, g)).then_inc(turned, 1)
            for g in range(GROUPS):
                pe.wait_ge(xT_ready, g + 1)
                for c in range(2):
                    pe.matmul(ps[2 + 2 * g + c][:, 0:COLS], w.inT[:, c * DI:(c + 1) * DI], w.xT[:, g, :],
                              start=True, stop=True).then_inc(xz_ps, 1)
            for g in range(GROUPS):
                pe.wait_ge(xi_ready, g + 1)
                pe.matmul(ps[g][0:96, 0:COLS], w.xp_bcT[:, :, :].rearrange("p a b -> p (a b)"), xi[:, g, :],
                          start=True, stop=True)
                pe.matmul(ps[6 + g][0:DTR, 0:COLS], w.xp_dtT[:, :], xi[:, g, :], start=True, stop=True
                          ).then_inc(bcd_ps, 1)
            for g in range(GROUPS):
                pe.wait_ge(low_ready, g + 1)
                pe.matmul(ps[2 + g][:, 0:COLS], w.dtT[:, :], dt_low[:, g, :], start=True, stop=True
                          ).then_inc(dt_ps, 1)

            def spread(q):
                n, g = q // GROUPS, q % GROUPS
                if q >= 3:
                    pe.wait_ge(drive_ready, q - 2)
                    pe.wait_ge(prod_ready, q - 2)
                pe.matmul(ps[2 + q % 3][:, 0:COLS], w.sel_bc[:, n, :], bc_parts[:, g, :], start=True, stop=True
                          ).then_inc(b_ps, 1)
                pe.matmul(ps[5 + q % 3][:, 0:COLS], w.sel_bc[:, NST + n, :], bc_parts[:, g, :],
                          start=True, stop=True).then_inc(c_ps, 1)

            pe.wait_ge(parts_ready, GROUPS)
            pe.wait_ge(gate_ready, GROUPS)
            pe.wait_ge(soft_ready, 2 * GROUPS)
            for q in range(3):
                spread(q)
            for q in range(Q):
                n, g = q // GROUPS, q % GROUPS
                pe.wait_ge(prod_ready, q + 1)
                pe.matmul(ps[g][:, 0:COLS], w.ident[:, :], prod[:, q % 3, :], start=(n == 0), stop=(n == NST - 1)
                          ).then_inc(y_sum, 1)
                if q + 3 < Q:
                    spread(q + 3)
            for g in range(GROUPS):
                pe.wait_ge(y_ready, g + 1)
                for u in range(U):
                    o = ps[2 + g][0:TP, u * D:(u + 1) * D]
                    pe.matmul(o, y[:, g, u * TP:(u + 1) * TP], w.outT[:, :], start=True, stop=False)
                    last = pe.matmul(o, w.ones_row[:, 0:TP], w.out_b[:, :], start=False, stop=True)
                last.then_inc(mix_ps, 1)
            for g in range(GROUPS):
                pe.wait_ge(mixed, g + 1)
                turn_tokens(pe, w, 4 + g, tiles(mix, g)).then_inc(y_turned, 1)
            for g in range(GROUPS):
                pe.wait_ge(yT_ready, g + 1)
                for c in range(2):
                    pe.matmul(ps[[0, 1, 6, 7][2 * g + c]][:, 0:COLS], w.fc1T[:, c * 128:(c + 1) * 128], w.xT[:, g, :],
                              start=True, stop=True).then_inc(fc1_ps, 1)
            for g in range(GROUPS):
                pe.wait_ge(hid_ready, 2 * g + 2)
                for u in range(U):
                    o = ps[2 + g][0:TP, u * D:(u + 1) * D]
                    for c in range(2):
                        pe.matmul(o, hid[:, g, c, u * TP:(u + 1) * TP], w.fc2T[:, c, :], start=(c == 0), stop=False)
                    last = pe.matmul(o, w.ones_row[:, 0:TP], w.fc2_b[:, :], start=False, stop=True)
                last.then_inc(fc2_ps, 1)

        @block.scalar
        def _(act):
            act.preload_act_table(ACT.Tanh)
            for g in range(GROUPS):
                act.wait_ge(turned, g + 1)
                act.activation(w.xT[0:D, g, :], ps[g][0:D, 0:COLS], ACT.Copy).then_inc(xT_ready, 1)
            for g in range(GROUPS):
                act.wait_ge(xz_ps, 2 * g + 1)
                act.activation(xi_pad[:, g, :, DCONV - 1:], ps[2 + 2 * g][:, 0:COLS].rearrange("p (b t) -> p b t", b=G),
                               ACT.Copy).then_inc(pad_ready, 1)
                act.wait_ge(xz_ps, 2 * g + 2)
                act.activation(gate[:, g, :], ps[3 + 2 * g][:, 0:COLS], ACT.Tanh).then_inc(tanh_ready, 1)
            for g in range(GROUPS):
                act.wait_ge(conv_ready, g + 1)
                act.activation(xi[:, g, :], conv[:, g, :, :].rearrange("p b t -> p (b t)"), ACT.Tanh
                               ).then_inc(xt_ready, 1)
            for g in range(GROUPS):
                act.wait_ge(bcd_ps, g + 1)
                act.activation(dt_low[:, g, :], ps[6 + g][0:DTR, 0:COLS], ACT.Copy).then_inc(low_ready, 1)
            act.preload_act_table_set("natural_log_exp_and_others")
            for g in range(GROUPS):
                act.wait_ge(dt_ps, g + 1)
                a_step.did(act.activation(expo[:, g, :], ps[2 + g][:, 0:COLS], ACT.Abs, bias=w.dt_b[:, 0:1]))
                act.activation(rest[:, g, :], ps[2 + g][:, 0:COLS], ACT.Relu, bias=w.dt_b[:, 0:1]).then_inc(soft_ready, 1)
            for g in range(GROUPS):
                wait_back(a_step, act, GROUPS - 1)
                a_step.did(act.activation(expo[:, g, :], expo[:, g, :], ACT.Exp, scale=-1.0))
            for g in range(GROUPS):
                wait_back(a_step, act, GROUPS - 1 - g)
                act.activation(expo[:, g, :], expo[:, g, :], ACT.Ln, bias=1.0).then_inc(soft_ready, 1)
            act.wait_ge(zero_ready, 2)
            for q in range(Q):
                n, g = q // GROUPS, q % GROUPS
                if q < GROUPS:
                    act.wait_ge(dt_ready, g + 1)
                if q >= 4:
                    act.wait_ge(scanned, G * (q - 3))
                act.activation(decay[:, q % 4, :, 1:], dt[:, g, :].rearrange("p (b t) -> p b t", b=G)[:, :, 1:],
                               ACT.Exp, scale=w.A[:, n:n + 1]).then_inc(decay_ready, 1)
            for g in range(GROUPS):
                act.wait_ge(y_turned, g + 1)
                act.activation(w.xT[0:D, g, :], ps[4 + g][0:D, 0:COLS], ACT.Copy).then_inc(yT_ready, 1)
            for g in range(GROUPS):
                for c in range(2):
                    act.wait_ge(fc1_ps, 2 * g + c + 1)
                    act.activation(hid[:, g, c, :], ps[[0, 1, 6, 7][2 * g + c]][:, 0:COLS], ACT.Gelu
                                   ).then_inc(hid_ready, 1)
            for g in range(GROUPS):
                act.wait_ge(fc2_ps, g + 1)
                act.activation(tiles(ffn, g), ps[2 + g][0:TP, 0:U * D].rearrange("p (u n) -> p u n", u=U), ACT.Gelu
                               ).then_inc(ffn_ready, 1)

        @block.vector
        def _(dve):
            def norm(src, dst, i, ready=None):
                normalize(dve, v_step, [(tiles(src, g), tiles(dst, g), tiles(squares, g), sums[:, g * U:(g + 1) * U])
                                        for g in range(GROUPS)], 1e-5, var_ready, rstd_ready, i * GROUPS,
                          ready=ready)

            def gains(gain, bias, t, did, dve):
                for g in range(GROUPS):
                    wait_back(v_step, dve, GROUPS - 1)
                    v_step.did(dve.tensor_tensor(tiles(t, g), tiles(t, g), each(gain[:, :], U), ALU.mult))
                for g in range(GROUPS):
                    wait_back(v_step, dve, GROUPS - 1 - g)
                    ins = dve.tensor_tensor(tiles(t, g), tiles(t, g), each(bias[:, :], U), ALU.add)
                    did(ins)

            norm(w.h, w.xn, 0, ready=xn_ready)
            dve.wait_ge(zero_ready, 1)
            for k in range(DCONV):
                for g in range(GROUPS):
                    shifted = xi_pad[:, g, :, k:k + SEQ]
                    if k == 0:
                        dve.wait_ge(pad_ready, g + 1)
                        v_step.did(dve.tensor_scalar(conv[:, g, :, :], shifted, w.conv_w[:, 0:1], w.conv_b[:, 0:1],
                                                     ALU.mult, ALU.add))
                        continue
                    wait_back(v_step, dve, GROUPS - 1 - (g if k == DCONV - 1 else 0))
                    ins = dve.scalar_tensor_tensor(out=conv[:, g, :, :], in0=shifted, scalar=w.conv_w[:, k:k + 1],
                                                   in1=conv[:, g, :, :], op0=ALU.mult, op1=ALU.add)
                    if k < DCONV - 1:
                        v_step.did(ins)
                    else:
                        ins.then_inc(conv_ready, 1)
            for g in range(GROUPS):
                dve.wait_ge(tanh_ready, g + 1)
                dve.scalar_tensor_tensor(out=gate[:, g, :], in0=gate[:, g, :], scalar=1.0, in1=ps[3 + 2 * g][:, 0:COLS],
                                         op0=ALU.add, op1=ALU.mult).then_inc(gate_ready, 1)
            for g in range(GROUPS):
                dve.wait_ge(xt_ready, g + 1)
                dve.scalar_tensor_tensor(out=xi[:, g, :], in0=xi[:, g, :], scalar=1.0,
                                         in1=conv[:, g, :, :].rearrange("p b t -> p (b t)"), op0=ALU.add, op1=ALU.mult
                                         ).then_inc(xi_ready, 1)
            for g in range(GROUPS):
                dve.wait_ge(bcd_ps, g + 1)
                v_step.did(dve.tensor_copy(bc_parts[:, g, :], ps[g][0:96, 0:COLS]))
            for g in range(GROUPS):
                wait_back(v_step, dve, GROUPS - 1)
                v_step.did(dve.tensor_tensor(bc_rest[:, g, :], ps[g][0:96, 0:COLS], bc_parts[:, g, :], ALU.subtract))
            for g in range(GROUPS):
                wait_back(v_step, dve, GROUPS - 1)
                v_step.did(dve.tensor_copy(bc_mid[:, g, :], bc_rest[:, g, :]))
            for g in range(GROUPS):
                wait_back(v_step, dve, GROUPS - 1 - g)
                dve.tensor_copy(bc_parts[32:64, g, :], bc_mid[32:64, g, :])
                dve.tensor_tensor(bc_parts[64:96, g, :], bc_rest[64:96, g, :], bc_mid[64:96, g, :], ALU.subtract
                                  ).then_inc(parts_ready, 1)
            dve.wait_ge(soft_ready, 2 * GROUPS)
            for g in range(GROUPS):
                dve.tensor_tensor(dt[:, g, :], expo[:, g, :], rest[:, g, :], ALU.add).then_inc(dt_ready, 1)
            for g in range(GROUPS):
                dve.wait_ge(dt_ready, g + 1)
                v_step.did(dve.tensor_tensor(dtx[:, g, :], dt[:, g, :], xi[:, g, :], ALU.mult))
            v_step.wait(dve)
            for q in range(Q + 2):
                if q < Q:
                    g = q % GROUPS
                    dve.wait_ge(b_ps, q + 1)
                    if q >= 3:
                        dve.wait_ge(scanned, G * (q - 2))
                    dve.tensor_tensor(drive[:, q % 3, :, :].rearrange("p b t -> p (b t)"), ps[2 + q % 3][:, 0:COLS],
                                      dtx[:, g, :], ALU.mult).then_inc(drive_ready, 1)
                if 1 <= q <= Q:
                    s = q - 1
                    dve.wait_ge(decay_ready, s + 1)
                    dve.wait_ge(drive_ready, s + 1)
                    if s >= 3:
                        dve.wait_ge(prod_ready, s - 2)
                    for b in range(G):
                        dve.tensor_tensor_scan(state[:, s % 3, b, :], decay[:, s % 4, b, :], drive[:, s % 3, b, :],
                                               0.0, ALU.mult, ALU.add).then_inc(scanned, 1)
                if q >= 2:
                    s = q - 2
                    dve.wait_ge(scanned, G * (s + 1))
                    dve.wait_ge(c_ps, s + 1)
                    if s >= 3:
                        dve.wait_ge(y_sum, s - 2)
                    dve.tensor_tensor(prod[:, s % 3, :], ps[5 + s % 3][:, 0:COLS],
                                      state[:, s % 3, :, :].rearrange("p b t -> p (b t)"), ALU.mult
                                      ).then_inc(prod_ready, 1)
            for g in range(GROUPS):
                dve.wait_ge(y_sum, Q - GROUPS + g + 1)
                v_step.did(dve.scalar_tensor_tensor(out=y[:, g, :], in0=xi[:, g, :], scalar=w.D_ssm[:, 0:1],
                                                    in1=ps[g][:, 0:COLS], op0=ALU.mult, op1=ALU.add))
            dve.wait_ge(gate_ready, GROUPS)
            for g in range(GROUPS):
                wait_back(v_step, dve, GROUPS - 1 - g)
                dve.tensor_tensor(y[:, g, :], y[:, g, :], gate[:, g, :], ALU.mult).then_inc(y_ready, 1)
            for g in range(GROUPS):
                dve.wait_ge(mix_ps, g + 1)
                dve.wait_ge(xn_ready, g + 1)
                v_step.did(dve.tensor_tensor(tiles(w.xn, g), tiles(w.xn, g), ps[2 + g][0:TP, 0:U * D].rearrange(
                    "p (u n) -> p u n", u=U), ALU.add))
            v_step.wait(dve)
            norm(w.xn, mix, 1)
            gains(w.m_ln1_g, w.m_ln1_b, mix, lambda ins: ins.then_inc(mixed, 1), dve)
            dve.wait_ge(mixed, GROUPS)
            for g in range(GROUPS):
                dve.wait_ge(ffn_ready, g + 1)
                v_step.did(dve.tensor_tensor(tiles(w.xn, g), tiles(mix, g), tiles(ffn, g), ALU.add))
            v_step.wait(dve)
            norm(w.xn, w.xn, 2)
            gains(w.m_ln2_g, w.m_ln2_b, w.xn, v_step.did, dve)
            v_step.wait(dve)
            for g in range(GROUPS):
                v_step.did(dve.tensor_tensor(tiles(w.h, g), tiles(w.h, g), tiles(w.xn, g), ALU.add))
            v_step.wait(dve)

        return sems


def layer_memory(nc, ctx, layer):
    sems = []

    def sb(name, shape, dt=F32):
        return ctx.enter_context(nc.sbuf_tensor(f"{layer}_{name}", shape, dt))

    def sem(*names):
        new = [ctx.enter_context(nc.semaphore(f"{layer}_{n}")) for n in names]
        sems.extend(new)
        return new if len(new) > 1 else new[0]

    return sb, sem, sems


def per_group(*tensors):
    return [tuple(t[:, g * U:(g + 1) * U] if len(t.shape) == 2 else tiles(t, g) for t in tensors)
            for g in range(GROUPS)]


def find_first(dve, steps, code, code_max, hot, at_max):
    for g in range(GROUPS):
        wait_back(steps, dve, GROUPS - 1)
        steps.did(at_max(g))
    for g in range(GROUPS):
        wait_back(steps, dve, GROUPS - 1)
        steps.did(dve.tensor_reduce(code_max[g], code[g], X, ALU.max))
    for g in range(GROUPS):
        wait_back(steps, dve, GROUPS - 1)
        steps.did(dve.tensor_tensor(hot[g], code[g], wide(code_max[g], 8), ALU.is_equal))


def combine(dve, w, steps, gates, prod, y_ps, y_read, summed, banks):
    NT = GROUPS * U
    for i in range(NT + 1):
        if i < NT:
            dve.wait_ge(y_ps, i + 1)
            if i >= 2:
                dve.wait_ge(summed, i - 1)
            dve.tensor_tensor(prod[:, i % 2, :, :], w.psum[banks[i % len(banks)]][0:TP, :].rearrange(
                "p (e n) -> p e n", e=8), wide(gates[:, i, :], D), ALU.mult).then_inc(y_read, 1)
        if i >= 1:
            dve.wait_ge(y_read, i)
            dve.tensor_reduce(w.xn[:, i - 1, :], prod[:, (i - 1) % 2, :, :].rearrange("p e n -> p n e"), X, ALU.add
                              ).then_inc(summed, 1)
    for g in range(GROUPS):
        dve.wait_ge(summed, (g + 1) * U)
        steps.did(dve.tensor_tensor(tiles(w.h, g), tiles(w.h, g), tiles(w.xn, g), ALU.add))
    steps.wait(dve)


def ffn0(nc, d, w):
    NT = GROUPS * U
    with ExitStack() as ctx:
        sb, sem, sems = layer_memory(nc, ctx, "ffn0")
        squares, sums = sb("squares", [TP, NT, D]), sb("sums", [TP, NT])
        hid = sb("hid", [128, GROUPS, 2, COLS])
        best, code_max, total = sb("best", [TP, NT]), sb("code_max", [TP, NT]), sb("total", [TP, NT])
        z, code, hot, ex = (sb(n, [TP, NT, 8]) for n in ("z", "code", "hot", "ex"))
        prod = sb("prod", [TP, 2, 8, D])
        v_step = Steps(sem("v_step"))
        var_ready, rstd_ready, xn_ready, turned, xT_ready = sem("var", "rstd", "xn_ready", "turned", "xT_ready")
        h_ps, hid_ready, logit_ps, z_ready, ex_ready, y_ps, y_read, summed = sem(
            "h_ps", "hid_ready", "logit_ps", "z_ready", "ex_ready", "y_ps", "y_read", "summed")
        block = ctx.enter_context(nc.Block())
        ps = w.psum
        Y_BANKS = (4, 5, 6, 7)

        @block.gpsimd
        def _(pool):
            roots(pool, w, [s for s, in per_group(sums)], var_ready, rstd_ready, 0)

        @block.tensor
        def _(pe):
            for g in range(GROUPS):
                pe.wait_ge(xn_ready, g + 1)
                turn_tokens(pe, w, g, tiles(w.xn, g)).then_inc(turned, 1)
            for g in range(GROUPS):
                pe.wait_ge(xT_ready, g + 1)
                for c in range(2):
                    pe.matmul(ps[2 + 2 * g + c][:, 0:COLS], w.f0_W1[:, c * 128:(c + 1) * 128], w.xT[:, g, :],
                              start=True, stop=True).then_inc(h_ps, 1)
            for g in range(GROUPS):
                pe.wait_ge(hid_ready, 2 * g + 2)
                for u in range(U):
                    o = ps[g][0:TP, u * 8:(u + 1) * 8]
                    for c in range(2):
                        pe.matmul(o, hid[:, g, c, u * TP:(u + 1) * TP], w.f0_Wg[:, c, :], start=(c == 0), stop=False)
                    last = pe.matmul(o, w.ones_row[:, 0:TP], w.f0_bg[:, :], start=False, stop=True)
                last.then_inc(logit_ps, 1)
            for i in range(NT):
                g, u = i // U, i % U
                if i >= 4:
                    pe.wait_ge(y_read, i - 3)
                o = ps[Y_BANKS[i % 4]][0:TP, :]
                for c in range(2):
                    pe.matmul(o, hid[:, g, c, u * TP:(u + 1) * TP], w.f0_Wd[:, c, :, :].rearrange("p e n -> p (e n)"),
                              start=(c == 0), stop=False)
                pe.matmul(o, w.ones_row[:, 0:TP], w.f0_bd[:, :, :].rearrange("p e n -> p (e n)"), start=False, stop=True
                          ).then_inc(y_ps, 1)

        @block.scalar
        def _(act):
            act.preload_act_table(ACT.Gelu)
            for g in range(GROUPS):
                act.wait_ge(turned, g + 1)
                act.activation(w.xT[0:D, g, :], ps[g][0:D, 0:COLS], ACT.Copy).then_inc(xT_ready, 1)
            for g in range(GROUPS):
                for c in range(2):
                    act.wait_ge(h_ps, 2 * g + c + 1)
                    act.activation(hid[:, g, c, :], ps[2 + 2 * g + c][:, 0:COLS], ACT.Gelu).then_inc(hid_ready, 1)
            for g in range(GROUPS):
                act.wait_ge(z_ready, g + 1)
                act.activation(tiles(ex, g), tiles(z, g), ACT.Exp).then_inc(ex_ready, 1)

        @block.vector
        def _(dve):
            normalize(dve, v_step, per_group(w.h, w.xn, squares, sums), 1e-5, var_ready, rstd_ready, 0, ready=xn_ready)
            for g in range(GROUPS):
                dve.wait_ge(logit_ps, g + 1)
                logits = ps[g][0:TP, 0:U * 8].rearrange("p (u e) -> p u e", u=U)
                v_step.did(dve.tensor_reduce(best[:, g * U:(g + 1) * U], logits, X, ALU.max))
            for g in range(GROUPS):
                wait_back(v_step, dve, GROUPS - 1 - g)
                logits = ps[g][0:TP, 0:U * 8].rearrange("p (u e) -> p u e", u=U)
                dve.tensor_tensor(tiles(z, g), logits, wide(best[:, g * U:(g + 1) * U], 8), ALU.subtract
                                  ).then_inc(z_ready, 1)
            dve.wait_ge(z_ready, GROUPS)
            rank = each(w.rank[:, :], U)
            codes, hots = [tiles(code, g) for g in range(GROUPS)], [tiles(hot, g) for g in range(GROUPS)]
            find_first(dve, v_step, codes, [m for m, in per_group(code_max)], hots,
                       lambda g: dve.scalar_tensor_tensor(out=codes[g], in0=tiles(z, g), scalar=0.0, in1=rank,
                                                          op0=ALU.is_ge, op1=ALU.mult))
            for g in range(GROUPS):
                dve.wait_ge(ex_ready, g + 1)
                v_step.did(dve.tensor_reduce(total[:, g * U:(g + 1) * U], tiles(ex, g), X, ALU.add))
            for g in range(GROUPS):
                wait_back(v_step, dve, GROUPS - 1)
                v_step.did(dve.reciprocal(total[:, g * U:(g + 1) * U], total[:, g * U:(g + 1) * U]))
            for g in range(GROUPS):
                v_step.did(dve.tensor_tensor(hots[g], hots[g], tiles(ex, g), ALU.mult))
            for g in range(GROUPS):
                wait_back(v_step, dve, GROUPS - 1)
                v_step.did(dve.tensor_tensor(hots[g], hots[g], wide(total[:, g * U:(g + 1) * U], 8), ALU.mult))
            v_step.wait(dve)
            combine(dve, w, v_step, hot, prod, y_ps, y_read, summed, Y_BANKS)

        return sems


def ffn3(nc, d, w):
    NT = GROUPS * U
    with ExitStack() as ctx:
        sb, sem, sems = layer_memory(nc, ctx, "ffn3")
        squares, sums = sb("squares", [TP, NT, D]), sb("sums", [TP, NT])
        hid = sb("hid", [128, 8, GROUPS, COLS])
        best, code_max, total = sb("best", [TP, NT]), sb("code_max", [TP, NT]), sb("total", [TP, NT])
        z, z2, code, hot, hot2, ex = (sb(n, [TP, NT, 8]) for n in ("z", "z2", "code", "hot", "hot2", "ex"))
        prod = sb("prod", [TP, 2, 8, D])
        v_step = Steps(sem("v_step"))
        var_ready, rstd_ready, xn_ready, turned, xT_ready = sem("var", "rstd", "xn_ready", "turned", "xT_ready")
        h_ps, hid_ready, logit_ps, z_ready, ex_ready, y_ps, y_read, summed = sem(
            "h_ps", "hid_ready", "logit_ps", "z_ready", "ex_ready", "y_ps", "y_read", "summed")
        block = ctx.enter_context(nc.Block())
        ps = w.psum
        Y_BANKS = (6, 7)

        @block.gpsimd
        def _(pool):
            for i in range(2):
                roots(pool, w, [s for s, in per_group(sums)], var_ready, rstd_ready, i * GROUPS)

        @block.tensor
        def _(pe):
            for g in range(GROUPS):
                pe.wait_ge(xn_ready, g + 1)
                turn_tokens(pe, w, g, tiles(w.xn, g)).then_inc(turned, 1)
            for g in range(GROUPS):
                pe.wait_ge(xT_ready, g + 1)
                for u in range(U):
                    last = pe.matmul(ps[g][0:TP, u * 8:(u + 1) * 8], w.xT[:, g, u * TP:(u + 1) * TP], w.f3_Wr[:, :],
                                     start=True, stop=True)
                last.then_inc(logit_ps, 1)
            for q in range(8 * GROUPS):
                g, e = q // 8, q % 8
                if q >= 4:
                    pe.wait_ge(hid_ready, q - 3)
                pe.matmul(ps[2 + q % 4][:, 0:COLS], w.f3_W1[:, e, :], w.xT[:, g, :], start=True, stop=True
                          ).then_inc(h_ps, 1)
            for i in range(NT):
                g, u = i // U, i % U
                pe.wait_ge(hid_ready, 8 * g + 8)
                if i >= 2:
                    pe.wait_ge(y_read, i - 1)
                o = ps[Y_BANKS[i % 2]]
                pe.matmul(o[0:TP, :], w.ones_row[:, 0:TP], w.f3_b2[:, :, :].rearrange("p e n -> p (e n)"),
                          start=True, stop=False)
                for e in range(8):
                    last = pe.matmul(o[0:TP, e * D:(e + 1) * D], hid[:, e, g, u * TP:(u + 1) * TP], w.f3_W2[:, e, :],
                                     start=False, stop=(e == 7))
                last.then_inc(y_ps, 1)

        @block.scalar
        def _(act):
            act.preload_act_table(ACT.Gelu)
            for g in range(GROUPS):
                act.wait_ge(turned, g + 1)
                act.activation(w.xT[0:D, g, :], ps[g][0:D, 0:COLS], ACT.Identity, bias=w.f3_b[:, 0:1],
                               scale=w.f3_g[:, 0:1]).then_inc(xT_ready, 1)
            for q in range(8 * GROUPS):
                g, e = q // 8, q % 8
                act.wait_ge(h_ps, q + 1)
                act.activation(hid[:, e, g, :], ps[2 + q % 4][:, 0:COLS], ACT.Gelu).then_inc(hid_ready, 1)
            for g in range(GROUPS):
                act.wait_ge(z_ready, g + 1)
                act.activation(tiles(ex, g), tiles(z, g), ACT.Exp).then_inc(ex_ready, 1)

        @block.vector
        def _(dve):
            normalize(dve, v_step, per_group(w.h, w.xn, squares, sums), 1e-5, var_ready, rstd_ready, 0)
            v_step.wait(dve)
            normalize(dve, v_step, per_group(w.xn, w.xn, squares, sums), 1e-5, var_ready, rstd_ready, GROUPS,
                      ready=xn_ready)
            for g in range(GROUPS):
                dve.wait_ge(logit_ps, g + 1)
                logits = ps[g][0:TP, 0:U * 8].rearrange("p (u e) -> p u e", u=U)
                v_step.did(dve.tensor_reduce(best[:, g * U:(g + 1) * U], logits, X, ALU.max))
            for g in range(GROUPS):
                wait_back(v_step, dve, GROUPS - 1 - g)
                logits = ps[g][0:TP, 0:U * 8].rearrange("p (u e) -> p u e", u=U)
                dve.tensor_tensor(tiles(z, g), logits, wide(best[:, g * U:(g + 1) * U], 8), ALU.subtract
                                  ).then_inc(z_ready, 1)
            dve.wait_ge(z_ready, GROUPS)
            top_two(dve, v_step, w, z, z2, code, code_max, hot, hot2, best)
            for g in range(GROUPS):
                dve.wait_ge(ex_ready, g + 1)
                wait_back(v_step, dve, GROUPS - 1)
                v_step.did(dve.tensor_tensor(tiles(hot, g), tiles(hot, g), tiles(ex, g), ALU.mult))
            for g in range(GROUPS):
                wait_back(v_step, dve, GROUPS - 1)
                v_step.did(dve.tensor_reduce(total[:, g * U:(g + 1) * U], tiles(hot, g), X, ALU.add))
            for g in range(GROUPS):
                wait_back(v_step, dve, GROUPS - 1)
                v_step.did(dve.reciprocal(total[:, g * U:(g + 1) * U], total[:, g * U:(g + 1) * U]))
            for g in range(GROUPS):
                wait_back(v_step, dve, GROUPS - 1)
                v_step.did(dve.tensor_tensor(tiles(hot, g), tiles(hot, g), wide(total[:, g * U:(g + 1) * U], 8),
                                             ALU.mult))
            v_step.wait(dve)
            combine(dve, w, v_step, hot, prod, y_ps, y_read, summed, Y_BANKS)

        return sems


def top_two(dve, steps, w, z, z2, code, code_max, hot, hot2, best):
    rank = each(w.rank[:, :], U)
    codes = [tiles(code, g) for g in range(GROUPS)]
    maxima = [m for m, in per_group(code_max)]
    find_first(dve, steps, codes, maxima, [tiles(hot, g) for g in range(GROUPS)],
               lambda g: dve.scalar_tensor_tensor(out=codes[g], in0=tiles(z, g), scalar=0.0, in1=rank,
                                                  op0=ALU.is_ge, op1=ALU.mult))
    for g in range(GROUPS):
        wait_back(steps, dve, GROUPS - 1)
        steps.did(dve.scalar_tensor_tensor(out=tiles(z2, g), in0=tiles(hot, g), scalar=NEG, in1=tiles(z, g),
                                           op0=ALU.mult, op1=ALU.add))
    for g in range(GROUPS):
        wait_back(steps, dve, GROUPS - 1)
        steps.did(dve.tensor_reduce(best[:, g * U:(g + 1) * U], tiles(z2, g), X, ALU.max))
    for g in range(GROUPS):
        wait_back(steps, dve, GROUPS - 1)
        steps.did(dve.tensor_tensor(tiles(z2, g), tiles(z2, g), wide(best[:, g * U:(g + 1) * U], 8), ALU.is_ge))
    find_first(dve, steps, codes, maxima, [tiles(hot2, g) for g in range(GROUPS)],
               lambda g: dve.tensor_tensor(codes[g], tiles(z2, g), rank, ALU.mult))
    for g in range(GROUPS):
        wait_back(steps, dve, GROUPS - 1)
        steps.did(dve.tensor_tensor(tiles(hot, g), tiles(hot, g), tiles(hot2, g), ALU.add))


def attn1(nc, d, w):
    NT, NB = GROUPS * U, G * GROUPS
    W3 = 3 * TP
    with ExitStack() as ctx:
        sb, sem, sems = layer_memory(nc, ctx, "attn1")
        squares, sums = sb("squares", [TP, NT, D]), sb("sums", [TP, NT])
        below = sb("below", [128, 4, COLS])
        feat = sb("feat", [128, GROUPS, 4, COLS])
        vals = sb("vals", [TP, NT, 8, D + 1])
        probs = sb("probs", [TP, 2, 4, 2, W3])
        den = sb("den", [TP, 2, 8])
        prod = sb("prod", [TP, 2, 8, D])
        v_step = Steps(sem("v_step"))
        var_ready, rstd_ready, xn_ready, turned, xT_ready = sem("var", "rstd", "xn_ready", "turned", "xT_ready")
        kq_ps, below_ready, below_exp, feat_ready, v_ps, v_ready, ones_ready = sem(
            "kq_ps", "below_ready", "below_exp", "feat_ready", "v_ps", "v_ready", "ones_ready")
        s_ps, probs_ready, o_ps, den_ready, o_read, summed = sem(
            "s_ps", "probs_ready", "o_ps", "den_ready", "o_read", "summed")
        block = ctx.enter_context(nc.Block())
        ps = w.psum

        @block.gpsimd
        def _(pool):
            pool.memset(vals[:, :, :, D:D + 1], 1.0).then_inc(ones_ready, 1)
            pool.wait_ge(ones_ready, 1)
            roots(pool, w, [s for s, in per_group(sums)], var_ready, rstd_ready, 0)

        @block.tensor
        def _(pe):
            for g in range(GROUPS):
                pe.wait_ge(xn_ready, g + 1)
                turn_tokens(pe, w, g, tiles(w.xn, g)).then_inc(turned, 1)
            for g in range(GROUPS):
                pe.wait_ge(xT_ready, g + 1)
                if g:
                    pe.wait_ge(feat_ready, 4 * g)
                for c in range(4):
                    wt = (w.a1_Wk, w.a1_Wq)[c // 2][:, 4 * (c % 2):4 * (c % 2) + 4, :]
                    pe.matmul(ps[2 + c][:, 0:COLS], wt.rearrange("p h k -> p (h k)"), w.xT[0:D, g, :],
                              start=True, stop=True).then_inc(kq_ps, 1)
                for u in range(U):
                    i = g * U + u
                    if i >= 2:
                        pe.wait_ge(v_ready, i - 1)
                    pe.matmul(ps[6 + i % 2][0:TP, :], w.xT[0:D, g, u * TP:(u + 1) * TP],
                              w.a1_Wvo[:, :, :].rearrange("p h n -> p (h n)"), start=True, stop=True).then_inc(v_ps, 1)

            def scores(b):
                g, at = b // G, (b % G) * SEQ
                if b:
                    pe.wait_ge(probs_ready, 4 * b)
                for c in range(2):
                    for r in range(4):
                        rows = slice(32 * r, 32 * r + 32)
                        k, q = feat[rows, g, c, at:at + SEQ], feat[rows, g, 2 + c, at:at + SEQ]
                        o = ps[r][0:TP, c * W3:(c + 1) * W3]
                        pe.matmul(o[:, 0:SEQ], k[:, 0:TP], q, start=True, stop=True)
                        last = pe.matmul(o[:, SEQ:W3], k[:, TP:SEQ], q[:, TP:SEQ], start=True, stop=True)
                        if c:
                            last.then_inc(s_ps, 1)

            pe.wait_ge(feat_ready, 4 * GROUPS)
            pe.wait_ge(v_ready, NT)
            pe.wait_ge(xT_ready, GROUPS)
            scores(0)
            for b in range(NB):
                if b + 1 < NB:
                    scores(b + 1)
                pe.wait_ge(probs_ready, 4 * b + 4)
                for t in range(2):
                    if b:
                        pe.wait_ge(o_read, 2 * (b - 1) + t + 1)
                    for hd in range(8):
                        o = ps[4 + 2 * t + hd // 4][0:TP, (hd % 4) * (D + 1):(hd % 4 + 1) * (D + 1)]
                        pr = probs[:, b % 2, hd % 4, hd // 4, :]
                        last = pe.matmul(o, pr[:, t * TP:(t + 1) * TP], vals[:, 2 * b, hd, :], start=True, stop=(t == 0))
                        if t:
                            last = pe.matmul(o, pr[:, SEQ:W3], vals[:, 2 * b + 1, hd, :], start=False, stop=True)
                    last.then_inc(o_ps, 1)

        @block.scalar
        def _(act):
            act.preload_act_table(ACT.Exp)
            for g in range(GROUPS):
                act.wait_ge(turned, g + 1)
                act.activation(w.xT[0:D, g, :], ps[g][0:D, 0:COLS], ACT.Copy).then_inc(xT_ready, 1)
            for g in range(GROUPS):
                for c in range(4):
                    act.wait_ge(kq_ps, 4 * g + c + 1)
                    if g:
                        act.wait_ge(feat_ready, 4 * (g - 1) + c + 1)
                    act.activation(below[:, c, :], ps[2 + c][:, 0:COLS], ACT.Relu, scale=-1.0).then_inc(below_ready, 1)
                for c in range(4):
                    act.wait_ge(below_ready, 4 * g + c + 1)
                    act.activation(below[:, c, :], below[:, c, :], ACT.Exp, scale=-1.0).then_inc(below_exp, 1)
                for u in range(U):
                    i = g * U + u
                    act.wait_ge(v_ps, i + 1)
                    act.activation(vals[:, i, :, 0:D], ps[6 + i % 2][0:TP, :].rearrange("p (h n) -> p h n", h=8),
                                   ACT.Copy).then_inc(v_ready, 1)

        @block.vector
        def _(dve):
            normalize(dve, v_step, per_group(w.h, w.xn, squares, sums), 1e-5, var_ready, rstd_ready, 0, ready=xn_ready)
            for g in range(GROUPS):
                for c in range(4):
                    dve.wait_ge(below_exp, 4 * g + c + 1)
                    dve.scalar_tensor_tensor(out=feat[:, g, c, :], in0=ps[2 + c][:, 0:COLS], scalar=0.0,
                                             in1=below[:, c, :], op0=ALU.max, op1=ALU.add).then_inc(feat_ready, 1)

            def mask(b):
                for r in range(4):
                    dve.wait_ge(s_ps, 4 * b + r + 1)
                    if b >= 2:
                        dve.wait_ge(o_ps, 2 * (b - 1))
                    dve.tensor_tensor(probs[:, b % 2, r, :, :], ps[r][0:TP, 0:2 * W3].rearrange(
                        "p (c n) -> p c n", c=2), each(w.causal01[:, :], 2), ALU.mult).then_inc(probs_ready, 1)

            def finish(b):
                for t in range(2):
                    dve.wait_ge(o_ps, 2 * b + t + 1)
                    both = w.banks[0:TP, 4 + 2 * t:6 + 2 * t, 0:4 * (D + 1)].rearrange("p c (h n) -> p c h n", h=4)
                    v_step.did(dve.tensor_scalar(den[:, t, :].rearrange("p (c h) -> p c h", c=2), both[:, :, :, D],
                                                 1e-9, None, ALU.add))
                for t in range(2):
                    wait_back(v_step, dve, 1)
                    v_step.did(dve.reciprocal(den[:, t, :], den[:, t, :]))
                for t in range(2):
                    wait_back(v_step, dve, 1 - t)
                    if b:
                        dve.wait_ge(summed, 2 * (b - 1) + t + 1)
                    both = w.banks[0:TP, 4 + 2 * t:6 + 2 * t, 0:4 * (D + 1)].rearrange("p c (h n) -> p c h n", h=4)
                    scale = den[:, t, :].rearrange("p (c h) -> p c h", c=2).unsqueeze(3).broadcast_to([TP, 2, 4, D])
                    dve.tensor_tensor(prod[:, t, :, :].rearrange("p (c h) n -> p c h n", c=2), both[:, :, :, 0:D],
                                      scale, ALU.mult).then_inc(o_read, 1)
                for t in range(2):
                    dve.wait_ge(o_read, 2 * b + t + 1)
                    dve.tensor_reduce(w.xn[:, 2 * b + t, :], prod[:, t, :, :].rearrange("p h n -> p n h"), X, ALU.add
                                      ).then_inc(summed, 1)

            mask(0)
            for b in range(NB):
                if b + 1 < NB:
                    mask(b + 1)
                finish(b)
            for g in range(GROUPS):
                dve.wait_ge(summed, (g + 1) * U)
                v_step.did(dve.tensor_tensor(tiles(w.h, g), tiles(w.h, g), tiles(w.xn, g), ALU.add))
            v_step.wait(dve)

        return sems


def attn2(nc, d, w):
    NT, NB = GROUPS * U, G * GROUPS
    with ExitStack() as ctx:
        sb, sem, sems = layer_memory(nc, ctx, "attn2")
        squares, sums = sb("squares", [TP, NT, D]), sb("sums", [TP, NT])
        kv_sq = sb("kv_sq", [TP, 2, 16, D])
        kv_var = sb("kv_var", [TP, 3, 16])
        scale = sb("scale", [TP, 3, 8])
        keys = sb("keys", [TP, NT, 512])
        vals = sb("vals", [TP, NT, 512])
        dots = sb("dots", [128, 2, 4, 128])
        dots_o = sb("dots_o", [128, 2, 4, D])
        v_step = Steps(sem("v_step"))
        var_ready, rstd_ready, xn_ready, turned, xT_ready = sem("var", "rstd", "xn_ready", "turned", "xT_ready")
        kv_ps, sq_ready, k_ready, kv_var_ready, root_ready, v_ready, kv_sum, kv_scaled = sem(
            "kv_ps", "sq_ready", "k_ready", "kv_var_ready", "root_ready", "v_ready", "kv_sum", "kv_scaled")
        zeroed, dots_ps, dots_ready, do_ps, do_ready, m_ps, m_ready, out_ps, out_read = sem(
            "zeroed", "dots_ps", "dots_ready", "do_ps", "do_ready", "m_ps", "m_ready", "out_ps", "out_read")
        block = ctx.enter_context(nc.Block())
        ps = w.psum

        @block.gpsimd
        def _(pool):
            pool.memset(dots[:], 0.0).then_inc(zeroed, 1)
            pool.wait_ge(zeroed, 1)
            roots(pool, w, [s for s, in per_group(sums)], var_ready, rstd_ready, 0)
            for i in range(NT):
                pool.wait_ge(kv_scaled, i + 1)
                pool.tensor_tensor(scale[:, i % 3, :], scale[:, i % 3, :], w.neg_half[0:TP, 0:8], ALU.pow
                                   ).then_inc(root_ready, 1)

        @block.tensor
        def _(pe):
            for g in range(GROUPS):
                pe.wait_ge(xn_ready, g + 1)
                turn_tokens(pe, w, 6 + g, tiles(w.xn, g)).then_inc(turned, 1)
            for i in range(NT):
                g, u = i // U, i % U
                pe.wait_ge(xT_ready, g + 1)
                if i >= 3:
                    pe.wait_ge(k_ready, i - 2)
                    pe.wait_ge(v_ready, i - 2)
                for c, wt in enumerate((w.a2_kT, w.a2_vT)):
                    pe.matmul(ps[2 * (i % 3) + c][0:TP, :], w.xT[0:D, g, u * TP:(u + 1) * TP],
                              wt[:, :, :].rearrange("p h n -> p (h n)"), start=True, stop=True).then_inc(kv_ps, 1)
            for b in range(NB):
                pe.wait_ge(v_ready, 2 * b + 2)
                if b:
                    pe.wait_ge(dots_ready, b)
                for c in range(4):
                    at = slice(128 * c, 128 * c + 128)
                    for t in range(2):
                        last = pe.matmul(ps[6][:, at], vals[:, 2 * b + t, at], keys[:, 2 * b + t, at],
                                         start=(t == 0), stop=(t == 1))
                last.then_inc(dots_ps, 1)
                pe.wait_ge(dots_ready, b + 1)
                if b:
                    pe.wait_ge(out_read, b)
                for c in range(4):
                    last = pe.matmul(ps[7][:, c * D:(c + 1) * D], dots[:, b % 2, c, :], w.a2_woT[:, c, :],
                                     start=True, stop=True)
                last.then_inc(do_ps, 1)
                pe.wait_ge(do_ready, b + 1)
                for c in range(4):
                    last = pe.matmul(ps[7][0:D, 256:256 + D], w.a2_Wq[:, c, :], dots_o[:, b % 2, c, :],
                                     start=(c == 0), stop=(c == 3))
                last.then_inc(m_ps, 1)
                pe.wait_ge(m_ready, b + 1)
                for t in range(2):
                    at = (b % G) * SEQ + t * TP
                    last = pe.matmul(ps[7][0:TP, 320 + t * D:320 + (t + 1) * D], w.xT[:, b // G, at:at + TP],
                                     w.a2_M[:, b, :], start=True, stop=True)
                last.then_inc(out_ps, 1)

        @block.scalar
        def _(act):
            for g in range(GROUPS):
                act.wait_ge(turned, g + 1)
                act.activation(w.xT[0:D, g, :], ps[6 + g][0:D, 0:COLS], ACT.Copy).then_inc(xT_ready, 1)

            for i in range(NT):
                act.wait_ge(kv_ps, 2 * i + 2)
                if i >= 2:
                    act.wait_ge(kv_sum, i - 1)
                both = w.banks[0:TP, 2 * (i % 3):2 * (i % 3) + 2, :]
                act.activation(kv_sq[:, i % 2, :, :].rearrange("p (c h) n -> p c (h n)", c=2), both, ACT.Square
                               ).then_inc(sq_ready, 1)
                act.activation(keys[:, i, :], ps[2 * (i % 3)][0:TP, :], ACT.Copy).then_inc(k_ready, 1)
            act.wait_ge(zeroed, 1)
            for b in range(NB):
                act.wait_ge(dots_ps, b + 1)
                for half in range(2):
                    at = slice(half * D, half * D + D)
                    last = act.activation(dots[at, b % 2, :, at], ps[6][at, :].rearrange("p (c n) -> p c n", c=4)[:, :, at],
                                          ACT.Copy)
                last.then_inc(dots_ready, 1)
                act.wait_ge(m_ps, b + 1)
                act.activation(w.a2_M[0:D, b, :], ps[7][0:D, 256:256 + D], ACT.Copy, scale=1.0 / SEQ
                               ).then_inc(m_ready, 1)

        @block.vector
        def _(dve):
            normalize(dve, v_step, per_group(w.h, w.xn, squares, sums), 1e-5, var_ready, rstd_ready, 0, ready=xn_ready)
            for i in range(NT + 1):
                if i < NT:
                    dve.wait_ge(sq_ready, i + 1)
                    dve.tensor_reduce(kv_var[:, i % 3, :], kv_sq[:, i % 2, :, :], X, ALU.add).then_inc(kv_sum, 1)
                if i < NT:
                    dve.wait_ge(kv_sum, i + 1)
                    dve.tensor_scalar(kv_var[:, i % 3, :], kv_var[:, i % 3, :], 1.0 / D, 1e-5, ALU.mult, ALU.add
                                      ).then_inc(kv_var_ready, 1)
                if i:
                    dve.wait_ge(root_ready, i)
                    dve.tensor_tensor(vals[:, i - 1, :].rearrange("p (h n) -> p h n", h=8),
                                      ps[2 * ((i - 1) % 3) + 1][0:TP, :].rearrange("p (h n) -> p h n", h=8),
                                      wide(scale[:, (i - 1) % 3, :], D), ALU.mult).then_inc(v_ready, 1)
                if i < NT:
                    dve.wait_ge(kv_var_ready, i + 1)
                    dve.tensor_tensor(scale[:, i % 3, :], kv_var[:, i % 3, 0:8], kv_var[:, i % 3, 8:16], ALU.mult
                                      ).then_inc(kv_scaled, 1)
            for b in range(NB):
                dve.wait_ge(do_ps, b + 1)
                dve.tensor_copy(dots_o[:, b % 2, :, :], ps[7][:, 0:4 * D].rearrange("p (c n) -> p c n", c=4)
                                ).then_inc(do_ready, 1)
                dve.wait_ge(out_ps, b + 1)
                at = slice(2 * b, 2 * b + 2)
                dve.tensor_tensor(w.h[:, at, :], w.h[:, at, :], ps[7][0:TP, 320:320 + 2 * D].rearrange(
                    "p (t n) -> p t n", t=2), ALU.add).then_inc(out_read, 1)
            dve.wait_ge(out_read, NB)

        return sems


class Softmax:

    W3 = 3 * TP

    def __init__(self, w, steps_of, index, q_of, k_of, v_of, width, units, sems):
        self.w, self.steps_of, self.index = w, steps_of, index
        self.q_of, self.k_of, self.v_of, self.width, self.units = q_of, k_of, v_of, width, units
        (self.zeroed, self.max3_ready, self.max_ps, self.max_ready, self.maxT_ps, self.maxT_ready, self.s_ps, self.probs_ready, self.o_ps,
         self.o_read) = sems

    def banks(self, i):
        return 2 * (i % 3)

    def pe_scores(self, pe, i, b, rows, cols, transposed):
        w, W3 = self.w, self.W3
        for j, r in enumerate(rows):
            for k, c in enumerate(cols):
                o = w.psum[self.banks(i) + j][0:TP, k * W3:(k + 1) * W3]
                q, key = self.q_of(b, r, c), self.k_of(b, r, c)
                m = self.index(r, c)
                if not transposed:
                    parts = ((o[:, 0:TP], q[:, 0:TP], key[:, 0:TP], w.maskQ[:, TP:SEQ], None),
                             (o[:, TP:W3], q[:, TP:SEQ], key, w.maskQ[:, :], None))
                else:
                    parts = ((o[:, 0:SEQ], key[:, 0:TP], q, w.maskT[:, :], slice(0, SEQ)),
                             (o[:, SEQ:W3], key[:, TP:SEQ], q[:, TP:SEQ], w.maskT[:, 0:TP], slice(TP, SEQ)))
                for out, lhsT, rhs, mask, shift in parts:
                    pe.matmul(out, w.ident_b[:, :], mask, start=True, stop=False)
                    last = pe.matmul(out, lhsT, rhs, start=False, stop=(shift is None))
                    if shift is not None:
                        last = pe.matmul(out, w.sel_map[:, m, :], self.maxT[:, b, shift], start=False, stop=True)
        return last

    def pe_all(self, pe):
        S, NB = self.steps_of, self.units
        for b in range(NB):
            for s, (rows, cols) in enumerate(S):
                i = b * len(S) + s
                if i >= 3:
                    pe.wait_ge(self.max_ready, i - 2)
                self.pe_scores(pe, i, b, rows, cols, False).then_inc(self.max_ps, 1)
        for g in range(NB // 2):
            pe.wait_ge(self.max3_ready, g + 1)
            if g >= 2:
                pe.wait_ge(self.maxT_ready, g - 1)
            for u in range(4):
                last = pe.transpose(self.w.psum[6 + g % 2][0:96, u * TP:(u + 1) * TP], self.max3[:, g * 4 + u, :],
                                    self.w.ident[0:TP, 0:TP])
            last.then_inc(self.maxT_ps, 1)
        total = NB * len(S)
        for i in range(total + 2):
            if i < total:
                b, s = i // len(S), i % len(S)
                pe.wait_ge(self.maxT_ready, b // 2 + 1)
                if i >= 3:
                    pe.wait_ge(self.probs_ready, i - 2)
                elif i == 0:
                    pe.wait_ge(self.max_ready, total)
                self.pe_scores(pe, i, b, *S[s], True).then_inc(self.s_ps, 1)
            if i >= 2:
                self.pe_values(pe, i - 2)

    def pe_values(self, pe, i):
        S, W3 = self.steps_of, self.W3
        b, s = i // len(S), i % len(S)
        rows, cols = S[s]
        pe.wait_ge(self.probs_ready, i + 1)
        if s == 0:
            if b:
                pe.wait_ge(self.o_read, 2 * b)
            else:
                pe.wait_ge(self.maxT_ready, self.units // 2)
        for j, r in enumerate(rows):
            for k, c in enumerate(cols):
                m, pr = self.index(r, c), self.probs[:, i % 3, j, k * W3:(k + 1) * W3]
                v0, v1 = self.v_of(b, 0, r, c), self.v_of(b, 1, r, c)
                f = v0.shape[1]
                at = slice(m * f, (m + 1) * f)
                pe.matmul(self.w.psum[6][0:TP, at], pr[:, 0:TP], v0, start=True, stop=True)
                pe.matmul(self.w.psum[7][0:TP, at], pr[:, TP:SEQ], v0, start=True, stop=False)
                last = pe.matmul(self.w.psum[7][0:TP, at], pr[:, SEQ:W3], v1, start=False, stop=True)
        if s == len(S) - 1:
            last.then_inc(self.o_ps, 1)

    def act_all(self, act):
        S, NB = self.steps_of, self.units
        for i in range(NB * len(S)):
            act.wait_ge(self.s_ps, i + 1)
            if i >= 3 * len(S):
                act.wait_ge(self.o_ps, (i - 3) // len(S))
            act.activation(self.probs[:, i % 3, :, :], self.w.banks[0:TP, self.banks(i):self.banks(i) + 2, 0:2 * self.W3],
                           ACT.Exp).then_inc(self.probs_ready, 1)

    def dve_maxima(self, dve, out_of):
        S, NB = self.steps_of, self.units
        for b in range(NB):
            for s, (rows, cols) in enumerate(S):
                i = b * len(S) + s
                dve.wait_ge(self.max_ps, i + 1)
                both = self.w.banks[0:TP, self.banks(i):self.banks(i) + 2, 0:2 * self.W3].rearrange(
                    "p j (k n) -> p j k n", k=2)
                dve.tensor_reduce(out_of(b, 0, s), both[:, :, :, 0:TP], X, ALU.max)
                dve.tensor_reduce(out_of(b, 1, s), both[:, :, :, TP:], X, ALU.max).then_inc(self.max_ready, 1)

    def dve_shifts(self, dve, steps):
        n = self.width
        for g in range(self.units // 2):
            dve.wait_ge(self.max_ready, (g + 1) * 2 * len(self.steps_of))
            dve.wait_ge(self.zeroed, 1)
            some = self.maxima[:, g * 2:(g + 1) * 2, :, :].rearrange("p b t m -> p (b t) m")
            for i in range(3):
                last = dve.tensor_copy(self.max3[:, g * 4:(g + 1) * 4, 32 * i:32 * i + n], some)
            last.then_inc(self.max3_ready, 1)
        for g in range(self.units // 2):
            dve.wait_ge(self.maxT_ps, g + 1)
            ps, high = self.w.psum[6 + g % 2][0:96, 0:2 * SEQ], self.maxT[:, g * 2:(g + 1) * 2, :].rearrange(
                "p b n -> p (b n)")
            rest, mid = self.rest[:, :], self.mid[:, :]
            steps.did(dve.tensor_copy(high, ps))
            steps.wait(dve)
            steps.did(dve.tensor_tensor(rest, ps, high, ALU.subtract))
            steps.wait(dve)
            steps.did(dve.tensor_copy(mid, rest))
            steps.wait(dve)
            steps.did(dve.tensor_copy(high[32:64, :], mid[32:64, :]))
            dve.tensor_tensor(high[64:96, :], rest[64:96, :], mid[64:96, :], ALU.subtract).then_inc(self.maxT_ready, 1)
            dve.wait_ge(self.maxT_ready, g + 1)

    def memory(self, sb):
        NB = self.units
        self.maxima = sb("maxima", [TP, NB, 2, self.width])
        self.max3 = sb("max3", [TP, NB * 2, 96])
        self.maxT = sb("maxT", [96, NB, SEQ], BF16)
        self.rest = sb("maxT_rest", [96, 2 * SEQ])
        self.mid = sb("maxT_mid", [96, 2 * SEQ], BF16)
        self.probs = sb("probs", [TP, 3, 2, 2 * self.W3])


SM_SEMS = ("max3_zeroed", "max3_ready", "max_ps", "max_ready", "maxT_ps", "maxT_ready", "s_ps", "probs_ready", "o_ps", "o_read")


def ffn1(nc, d, w):
    NT, NB = GROUPS * U, G * GROUPS
    R = U * 4
    with ExitStack() as ctx:
        sb, sem, sems = layer_memory(nc, ctx, "ffn1")
        squares, sums = sb("squares", [TP, NT, D]), sb("sums", [TP, NT])
        sxT = sb("sxT", [D, GROUPS, COLS])
        sx, nonzero = sb("sx", [TP, NT, D]), sb("nonzero", [TP, NT, D])
        qf, kf = sb("qf", [128, GROUPS, 4, COLS]), sb("kf", [128, GROUPS, 4, COLS])
        vals = sb("vals", [TP, NT, 4, 17])
        den = sb("den", [TP, 2, 16])
        ov = sb("ov", [TP, NT, 256])
        ovT = sb("ovT", [128, 2, GROUPS, COLS])
        gs = sb("gs", [TP, NT, 16])
        gstat = sb("gstat", [TP, NT, 4])
        mixed = sb("mixed", [TP, NT, D])
        sums4 = sb("sums4", [TP, NT * 4])
        f_n, f_nz, hx = sb("f_n", [TP, NT, D]), sb("f_nz", [TP, NT, D]), sb("hx", [TP, NT, D])
        fg, fstat = sb("fg", [TP, NT, 4]), sb("fstat", [TP, NT])
        v_step = Steps(sem("v_step"))
        var_ready, rstd_ready, xn_ready, turned, xT_ready = sem("var", "rstd", "xn_ready", "turned", "xT_ready")
        ones_ready, sx_ps, sxT_ready, sx_tok, qk_ps, qk_read, v_ps, v_ready = sem(
            "ones_ready", "sx_ps", "sxT_ready", "sx_tok", "qk_ps", "qk_read", "v_ps", "v_ready")
        sx_read = sem("sx_read")
        ov_ready, ov_turned, ovT_ready, gate_ps, gz_ready, gex_ready = sem(
            "ov_ready", "ov_turned", "ovT_ready", "gate_ps", "gz_ready", "gex_ready")
        t_in, t_ps, t_ready, p_ps, fz_ready, fex_ready = sem("t_in", "t_ps", "t_ready", "p_ps", "fz_ready", "fex_ready")

        def of_feat(t):
            return lambda b, e, n: t[32 * e:32 * e + 32, b // G, n, (b % G) * SEQ:(b % G + 1) * SEQ]

        steps_of = [((0, 1), (0, 1)), ((2, 3), (0, 1)), ((0, 1), (2, 3)), ((2, 3), (2, 3))]
        sm = Softmax(w, steps_of, lambda e, n: 4 * n + e, of_feat(qf), of_feat(kf),
                     lambda b, t, e, n: vals[:, 2 * b + t, n, :], 16, NB, sem(*SM_SEMS))
        sm.memory(sb)
        block = ctx.enter_context(nc.Block())
        ps = w.psum

        def tok_ps(bank, n=D):
            return ps[bank][0:TP, 0:U * n].rearrange("p (u n) -> p u n", u=U)

        def rows4(t, g):
            return tiles(t, g).rearrange("p u (r n) -> p (u r) n", r=4)

        @block.gpsimd
        def _(pool):
            pool.memset(vals[:, :, :, 16:17], 1.0).then_inc(ones_ready, 1)
            pool.memset(sm.max3[:], 0.0).then_inc(sm.zeroed, 1)
            pool.wait_ge(ones_ready, 1)
            pool.wait_ge(sm.zeroed, 1)
            roots(pool, w, [s for s, in per_group(sums)], var_ready, rstd_ready, 0)
            for i in range(1, 3):
                roots(pool, w, [sums4[:, g * R:(g + 1) * R] for g in range(GROUPS)], var_ready, rstd_ready, i * GROUPS)

        @block.tensor
        def _(pe):
            for g in range(GROUPS):
                pe.wait_ge(xn_ready, g + 1)
                turn_tokens(pe, w, g, tiles(w.xn, g)).then_inc(turned, 1)
            for g in range(GROUPS):
                pe.wait_ge(xT_ready, g + 1)
                pe.matmul(ps[2 + g][0:D, 0:COLS], w.f1_hlT[:, :], w.xT[:, g, :], start=True, stop=True)
                for u in range(U):
                    last = pe.matmul(ps[4 + g][0:TP, u * D:(u + 1) * D], w.xT[:, g, u * TP:(u + 1) * TP],
                                     w.f1_hlT[:, :], start=True, stop=True)
                last.then_inc(sx_ps, 1)
            for g in range(GROUPS):
                pe.wait_ge(sxT_ready, g + 1)
                if g:
                    pe.wait_ge(v_ready, g)
                for u in range(U):
                    last = pe.matmul(ps[7][0:TP, u * D:(u + 1) * D], sxT[:, g, u * TP:(u + 1) * TP], w.f1_vT[:, :],
                                     start=True, stop=True)
                last.then_inc(v_ps, 1)
                for j in range(8):
                    i = 8 * g + j
                    if i < 3:
                        pe.wait_ge(sx_read, GROUPS)
                    if i >= 3:
                        pe.wait_ge(qk_read, i - 2)
                    wt = (w.f1_kT, w.f1_qT)[j % 2][:, j // 2, :]
                    pe.matmul(ps[4 + i % 3][:, 0:COLS], wt, sxT[:, g, :], start=True, stop=True).then_inc(qk_ps, 1)
            pe.wait_ge(qk_read, 8 * GROUPS)
            pe.wait_ge(v_ready, GROUPS)
            sm.pe_all(pe)
            for g in range(GROUPS):
                pe.wait_ge(ov_ready, (g + 1) * U)
                for c in range(2):
                    for u in range(U):
                        last = pe.transpose(ps[2 * g + c][:, u * TP:(u + 1) * TP],
                                            ov[:, g * U + u, c * 128:(c + 1) * 128], w.ident[0:TP, 0:TP])
                    last.then_inc(ov_turned, 1)
            for g in range(GROUPS):
                pe.wait_ge(ovT_ready, 2 * g + 2)
                for u in range(U):
                    o = ps[4 + g][0:TP, u * 16:(u + 1) * 16]
                    for c in range(2):
                        pe.matmul(o, ovT[:, c, g, u * TP:(u + 1) * TP], w.f1_gateT[:, c, :], start=(c == 0), stop=False)
                    last = pe.matmul(o, w.ones_row[:, 0:TP], w.f1_gate_b[:, :], start=False, stop=True)
                last.then_inc(gate_ps, 1)
            for i, (t, wt, n) in enumerate(((f_n, w.f1_fc1T[:, :], D), (hx, w.f1_fc2T[:, :], D),
                                            (mixed, w.f1_fgT[:, :], 4))):
                for g in range(GROUPS):
                    pe.wait_ge(t_in, i * GROUPS + g + 1)
                    turn_tokens(pe, w, g, tiles(t, g)).then_inc(t_ps, 1)
                for g in range(GROUPS):
                    pe.wait_ge(t_ready, i * GROUPS + g + 1)
                    for u in range(U):
                        last = pe.matmul(ps[2 + g][0:TP, u * n:(u + 1) * n],
                                         w.xT[0:wt.shape[0], g, u * TP:(u + 1) * TP], wt, start=True, stop=True)
                    last.then_inc(p_ps, 1)

        @block.scalar
        def _(act):
            act.preload_act_table(ACT.Exp)
            for g in range(GROUPS):
                act.wait_ge(turned, g + 1)
                act.activation(w.xT[0:D, g, :], ps[g][0:D, 0:COLS], ACT.Copy).then_inc(xT_ready, 1)
            for g in range(GROUPS):
                act.wait_ge(sx_ps, g + 1)
                act.activation(sxT[:, g, :], ps[2 + g][0:D, 0:COLS], ACT.Copy).then_inc(sxT_ready, 1)
            for g in range(GROUPS):
                act.wait_ge(v_ps, g + 1)
                act.activation(vals[:, g * U:(g + 1) * U, :, 0:16], ps[7][0:TP, 0:U * D].rearrange(
                    "p (u n k) -> p u n k", u=U, n=4), ACT.Copy).then_inc(v_ready, 1)
                for j in range(8):
                    i = 8 * g + j
                    act.wait_ge(qk_ps, i + 1)
                    act.activation((kf, qf)[j % 2][:, g, j // 2, :], ps[4 + i % 3][:, 0:COLS], ACT.Copy
                                   ).then_inc(qk_read, 1)
            sm.act_all(act)
            for g in range(GROUPS):
                for c in range(2):
                    act.wait_ge(ov_turned, 2 * g + c + 1)
                    act.activation(ovT[:, c, g, :], ps[2 * g + c][:, 0:COLS], ACT.Copy).then_inc(ovT_ready, 1)
            for g in range(GROUPS):
                act.wait_ge(gz_ready, g + 1)
                act.activation(tiles(gs, g), tiles(gs, g), ACT.Exp).then_inc(gex_ready, 1)
            for i in range(3):
                for g in range(GROUPS):
                    act.wait_ge(t_ps, i * GROUPS + g + 1)
                    act.activation(w.xT[0:D, g, :], ps[g][0:D, 0:COLS], ACT.Copy).then_inc(t_ready, 1)
            for g in range(GROUPS):
                act.wait_ge(fz_ready, g + 1)
                act.activation(tiles(fg, g), tiles(fg, g), ACT.Exp).then_inc(fex_ready, 1)

        @block.vector
        def _(dve):
            normalize(dve, v_step, per_group(w.h, w.xn, squares, sums), 1e-5, var_ready, rstd_ready, 0, ready=xn_ready)
            for g in range(GROUPS):
                dve.wait_ge(sx_ps, g + 1)
                dve.tensor_copy(tiles(sx, g), tok_ps(4 + g)).then_inc(sx_read, 1)
            dve.wait_ge(sx_read, GROUPS)
            v_step.did(dve.tensor_scalar(nonzero[:, :, :], sx[:, :, :], 0.0, None, ALU.not_equal))
            for n in range(4):
                dve.copy_predicated(w.resid[:, :, n, :], w.in_first[:, :, n, :], sx[:, 2 * n:2 * n + 2, 16 * n:16 * n + 16])

            def out_of(b, t, s):
                rows, cols = steps_of[s]
                return sm.maxima[:, b, t, :].rearrange("p (n e) -> p e n", e=4)[:, rows[0]:rows[0] + 2, cols[0]:cols[0] + 2]

            sm.dve_maxima(dve, out_of)
            sm.dve_shifts(dve, v_step)
            v_step.wait(dve)
            for b in range(NB):
                for t in range(2):
                    dve.wait_ge(sm.o_ps, b + 1)
                    out = ps[6 + t][0:TP, 0:16 * 17].rearrange("p (m k) -> p m k", m=16)
                    v_step.did(dve.reciprocal(den[:, t, :], out[:, :, 16]))
                for t in range(2):
                    wait_back(v_step, dve, 1 - t)
                    i = 2 * b + t
                    out = ps[6 + t][0:TP, 0:16 * 17].rearrange("p (m k) -> p m k", m=16)
                    dve.tensor_tensor(ov[:, i, :].rearrange("p (m k) -> p m k", m=16), out[:, :, 0:16],
                                      wide(den[:, t, :], 16), ALU.mult).then_inc(sm.o_read, 1)
                for t in range(2):
                    i = 2 * b + t
                    dve.wait_ge(sm.o_read, i + 1)
                    parts = ov[:, i, :].rearrange("p (n e k) -> p n e k", n=4, e=4)
                    nz = nonzero[:, i, :].rearrange("p (n k) -> p n k", n=4).unsqueeze(2).broadcast_to([TP, 4, 4, 16])
                    dve.tensor_tensor(parts, parts, nz, ALU.mult).then_inc(ov_ready, 1)
            for g in range(GROUPS):
                dve.wait_ge(gate_ps, g + 1)
                v_step.did(dve.tensor_reduce(tiles(gstat, g), tok_ps(4 + g, 16).rearrange("p u (n e) -> p u n e", n=4),
                                             X, ALU.max))
            for g in range(GROUPS):
                wait_back(v_step, dve, GROUPS - 1 - g)
                dve.tensor_tensor(tiles(gs, g).rearrange("p u (n e) -> p (u n) e", n=4),
                                  ps[4 + g][0:TP, 0:U * 16].rearrange("p (r e) -> p r e", e=4),
                                  wide(tiles(gstat, g).rearrange("p u n -> p (u n)"), 4), ALU.subtract
                                  ).then_inc(gz_ready, 1)
            for g in range(GROUPS):
                dve.wait_ge(gex_ready, g + 1)
                v_step.did(dve.tensor_reduce(tiles(gstat, g), tiles(gs, g).rearrange("p u (n e) -> p u n e", n=4),
                                             X, ALU.add))
            for g in range(GROUPS):
                wait_back(v_step, dve, GROUPS - 1)
                v_step.did(dve.reciprocal(tiles(gstat, g), tiles(gstat, g)))
            for g in range(GROUPS):
                wait_back(v_step, dve, GROUPS - 1)
                four = tiles(gs, g).rearrange("p u (n e) -> p (u n) e", n=4)
                v_step.did(dve.tensor_tensor(four, four, wide(tiles(gstat, g).rearrange("p u n -> p (u n)"), 4), ALU.mult))
            for g in range(GROUPS):
                wait_back(v_step, dve, GROUPS - 1)
                dve.wait_ge(ov_turned, 2 * g + 2)
                part = tiles(ov, g).rearrange("p u (m k) -> p (u m) k", m=16)
                v_step.did(dve.tensor_tensor(part, part, wide(tiles(gs, g).rearrange("p u m -> p (u m)"), 16), ALU.mult))
            for g in range(GROUPS):
                wait_back(v_step, dve, GROUPS - 1)
                v_step.did(dve.tensor_reduce(rows4(mixed, g), tiles(ov, g).rearrange(
                    "p u (n e k) -> p (u n) k e", n=4, e=4), X, ALU.add))
            for g in range(GROUPS):
                wait_back(v_step, dve, GROUPS - 1)
                both = tiles(mixed, g).rearrange("p (b t) n -> p b (t n)", t=2)
                v_step.did(dve.tensor_tensor(both, both, each(w.resid[:, :, :, :].rearrange("p t n k -> p (t n k)"), G),
                                             ALU.add))
            v_step.wait(dve)

            def heads_norm(src, dst, i, gain, bias):
                normalize(dve, v_step, [(rows4(src, g), rows4(dst, g), rows4(squares, g), sums4[:, g * R:(g + 1) * R])
                                        for g in range(GROUPS)], 1e-8, var_ready, rstd_ready, i * GROUPS)
                for vec, op in ((gain, ALU.mult), (bias, ALU.add)):
                    for g in range(GROUPS):
                        wait_back(v_step, dve, GROUPS - 1)
                        v_step.did(dve.tensor_tensor(rows4(dst, g), rows4(dst, g), each(vec[:, :], R), op))
                v_step.wait(dve)

            heads_norm(mixed, f_n, 1, w.f1_ln_g, w.f1_ln_b)
            for g in range(GROUPS):
                dve.tensor_scalar(tiles(f_nz, g), tiles(f_n, g), 0.0, None, ALU.not_equal).then_inc(t_in, 1)
            dve.wait_ge(t_in, GROUPS)
            for g in range(GROUPS):
                dve.wait_ge(p_ps, g + 1)
                dve.scalar_tensor_tensor(out=tiles(hx, g), in0=tok_ps(2 + g), scalar=0.0, in1=tiles(f_nz, g),
                                         op0=ALU.max, op1=ALU.mult).then_inc(t_in, 1)
            for g in range(GROUPS):
                dve.wait_ge(p_ps, GROUPS + g + 1)
                v_step.did(dve.tensor_tensor(tiles(mixed, g), tok_ps(2 + g), tiles(f_nz, g), ALU.mult))
            for g in range(GROUPS):
                wait_back(v_step, dve, GROUPS - 1)
                v_step.did(dve.tensor_tensor(tiles(mixed, g), tiles(mixed, g), tiles(f_n, g), ALU.add))
            v_step.wait(dve)
            heads_norm(mixed, mixed, 2, w.f1_fn_g, w.f1_fn_b)
            for g in range(GROUPS):
                dve.sem_inc(t_in, 1)
            for g in range(GROUPS):
                dve.wait_ge(p_ps, 2 * GROUPS + g + 1)
                v_step.did(dve.tensor_reduce(fstat[:, g * U:(g + 1) * U], tok_ps(2 + g, 4), X, ALU.max))
            for g in range(GROUPS):
                wait_back(v_step, dve, GROUPS - 1 - g)
                dve.tensor_tensor(tiles(fg, g), tok_ps(2 + g, 4), wide(fstat[:, g * U:(g + 1) * U], 4), ALU.subtract
                                  ).then_inc(fz_ready, 1)
            for g in range(GROUPS):
                dve.wait_ge(fex_ready, g + 1)
                v_step.did(dve.tensor_reduce(fstat[:, g * U:(g + 1) * U], tiles(fg, g), X, ALU.add))
            for g in range(GROUPS):
                wait_back(v_step, dve, GROUPS - 1)
                v_step.did(dve.reciprocal(fstat[:, g * U:(g + 1) * U], fstat[:, g * U:(g + 1) * U]))
            for g in range(GROUPS):
                wait_back(v_step, dve, GROUPS - 1)
                v_step.did(dve.tensor_tensor(tiles(fg, g), tiles(fg, g), wide(fstat[:, g * U:(g + 1) * U], 4), ALU.mult))
            for g in range(GROUPS):
                wait_back(v_step, dve, GROUPS - 1)
                v_step.did(dve.tensor_tensor(rows4(mixed, g), rows4(mixed, g), wide(tiles(fg, g).rearrange(
                    "p u n -> p (u n)"), 16), ALU.mult))
            for g in range(GROUPS):
                wait_back(v_step, dve, GROUPS - 1)
                v_step.did(dve.tensor_tensor(tiles(w.h, g), tiles(w.h, g), tiles(mixed, g), ALU.add))
            v_step.wait(dve)

        return sems


def ffn2(nc, d, w):
    NT = GROUPS * U
    with ExitStack() as ctx:
        sb, sem, sems = layer_memory(nc, ctx, "ffn2")
        squares, sums = sb("squares", [TP, NT, D]), sb("sums", [TP, NT])
        rn = sb("rn", [TP, NT, D])
        by_cos, by_sin = sb("by_cos", [128, 2, COLS]), sb("by_sin", [128, 2, COLS])
        qf, kf = sb("qf", [128, GROUPS, COLS]), sb("kf", [128, GROUPS, COLS])
        vals = sb("vals", [TP, NT, 2, 17])
        den = sb("den", [TP, 2, 8])
        act1 = sb("act1", [85, 3, COLS])
        hh = sb("hh", [85, 16, GROUPS, COLS])
        best, code_max, total = sb("best", [TP, NT]), sb("code_max", [TP, NT]), sb("total", [TP, NT])
        z, z2, code, hot, hot2, ex = (sb(n, [TP, NT, 8]) for n in ("z", "z2", "code", "hot", "hot2", "ex"))
        prod = sb("prod", [TP, 2, 8, D])
        v_step = Steps(sem("v_step"))
        var_ready, rstd_ready, turn_in, turned, xT_ready = sem("var", "rstd", "turn_in", "turned", "xT_ready")
        ones_ready, qk_ps, rope_read, qk_ready, v_ps, v_ready, att_ps = sem(
            "ones_ready", "qk_ps", "rope_read", "qk_ready", "v_ps", "v_ready", "att_ps")
        h_ps, silu_ready, hh_ready, logit_ps, z_ready, ex_ready, y_ps, y_read, summed = sem(
            "h_ps", "silu_ready", "hh_ready", "logit_ps", "z_ready", "ex_ready", "y_ps", "y_read", "summed")

        def of_feat(t):
            return lambda g, hd, c: t[32 * hd:32 * hd + 32, g, c * SEQ:(c + 1) * SEQ]

        steps_of = [((0, 1), (0, 1)), ((2, 3), (0, 1))]
        sm = Softmax(w, steps_of, lambda hd, c: 4 * c + hd, of_feat(qf), of_feat(kf),
                     lambda g, t, hd, c: vals[:, g * U + 2 * c + t, hd // 2, :], 8, GROUPS, sem(*SM_SEMS))
        sm.memory(sb)
        block = ctx.enter_context(nc.Block())
        ps = w.psum
        Y_BANKS = (6, 7)

        def tok_ps(bank, n=D):
            return ps[bank][0:TP, 0:U * n].rearrange("p (u n) -> p u n", u=U)

        @block.gpsimd
        def _(pool):
            pool.memset(vals[:, :, :, 16:17], 1.0).then_inc(ones_ready, 1)
            pool.memset(sm.max3[:], 0.0).then_inc(sm.zeroed, 1)
            pool.wait_ge(ones_ready, 1)
            pool.wait_ge(sm.zeroed, 1)
            for i in range(3):
                roots(pool, w, [s for s, in per_group(sums)], var_ready, rstd_ready, i * GROUPS)

        @block.tensor
        def _(pe):
            def turn(i, src):
                for g in range(GROUPS):
                    pe.wait_ge(turn_in, i * GROUPS + g + 1)
                    turn_tokens(pe, w, 6 + g, tiles(src, g)).then_inc(turned, 1)

            turn(0, rn)
            for g in range(GROUPS):
                pe.wait_ge(xT_ready, g + 1)
                for j in range(4):
                    if g:
                        pe.wait_ge(rope_read, 4 * (g - 1) + j + 1)
                    pe.matmul(ps[j][:, 0:COLS], (w.f2_qT, w.f2_kT)[j // 2][:, j % 2, :], w.xT[0:D, g, :],
                              start=True, stop=True).then_inc(qk_ps, 1)
                for u in range(U):
                    last = pe.matmul(ps[4 + g][0:TP, u * 32:(u + 1) * 32], w.xT[0:D, g, u * TP:(u + 1) * TP], w.f2_vT[:, :],
                                     start=True, stop=True)
                last.then_inc(v_ps, 1)
            pe.wait_ge(qk_ready, 2 * GROUPS)
            pe.wait_ge(v_ready, GROUPS)
            sm.pe_all(pe)
            pe.wait_ge(sm.o_read, 2 * GROUPS)
            turn(1, rn)
            for g in range(GROUPS):
                pe.wait_ge(xT_ready, GROUPS + g + 1)
                for u in range(U):
                    last = pe.matmul(ps[g][0:TP, u * D:(u + 1) * D], w.xT[0:D, g, u * TP:(u + 1) * TP], w.f2_oT[:, :],
                                     start=True, stop=True)
                last.then_inc(att_ps, 1)
            turn(2, rn)
            for g in range(GROUPS):
                pe.wait_ge(xT_ready, 2 * GROUPS + g + 1)
                for u in range(U):
                    last = pe.matmul(ps[g][0:TP, u * 8:(u + 1) * 8], w.xT[0:D, g, u * TP:(u + 1) * TP],
                                     w.f2_routerT[:, :], start=True, stop=True)
                last.then_inc(logit_ps, 1)
            for q in range(16 * GROUPS):
                g, j = q // 16, q % 16
                if q >= 2:
                    pe.wait_ge(silu_ready, q - 1)
                    pe.wait_ge(hh_ready, q - 1)
                for i, wt in enumerate((w.f2_w1T, w.f2_w3T)):
                    pe.matmul(ps[2 + 2 * (q % 2) + i][0:85, 0:COLS], wt[:, j, :], w.xT[0:D, g, :], start=True, stop=True
                              ).then_inc(h_ps, 1)
            for i in range(NT):
                g, u = i // U, i % U
                pe.wait_ge(hh_ready, 16 * (g + 1))
                if i >= 2:
                    pe.wait_ge(y_read, i - 1)
                for j in range(16):
                    last = pe.matmul(ps[Y_BANKS[i % 2]][0:TP, (j // 2) * D:(j // 2 + 1) * D],
                                     hh[:, j, g, u * TP:(u + 1) * TP], w.f2_w2T[:, j, :],
                                     start=(j % 2 == 0), stop=(j % 2 == 1))
                last.then_inc(y_ps, 1)

        @block.scalar
        def _(act):
            def turn(i):
                for g in range(GROUPS):
                    act.wait_ge(turned, i * GROUPS + g + 1)
                    act.activation(w.xT[0:D, g, :], ps[6 + g][0:D, 0:COLS], ACT.Copy).then_inc(xT_ready, 1)

            act.preload_act_table(ACT.Exp)
            turn(0)
            for g in range(GROUPS):
                act.wait_ge(v_ps, g + 1)
                act.activation(vals[:, g * U:(g + 1) * U, :, 0:16], ps[4 + g][0:TP, 0:U * 32].rearrange(
                    "p (u n k) -> p u n k", u=U, n=2), ACT.Copy).then_inc(v_ready, 1)
            sm.act_all(act)
            turn(1)
            act.preload_act_table(ACT.Silu)
            turn(2)
            for q in range(16 * GROUPS):
                act.wait_ge(h_ps, 2 * q + 1)
                if q >= 3:
                    act.wait_ge(hh_ready, q - 2)
                act.activation(act1[:, q % 3, :], ps[2 + 2 * (q % 2)][0:85, 0:COLS], ACT.Silu).then_inc(silu_ready, 1)
            for g in range(GROUPS):
                act.wait_ge(z_ready, g + 1)
                act.activation(tiles(ex, g), tiles(z, g), ACT.Exp).then_inc(ex_ready, 1)

        @block.vector
        def _(dve):
            def rms(i):
                normalize(dve, v_step, per_group(w.xn, rn, squares, sums), 1e-6, var_ready, rstd_ready, i * GROUPS,
                          centre=False, ready=turn_in)

            normalize(dve, v_step, per_group(w.h, w.xn, squares, sums), 1e-5, var_ready, rstd_ready, 0)
            v_step.wait(dve)
            rms(1)
            for g in range(GROUPS):
                for j in range(4):
                    dve.wait_ge(qk_ps, 4 * g + j + 1)
                    part, table = ((by_cos, w.rope_cos), (by_sin, w.rope_sin))[j % 2]
                    if g:
                        dve.wait_ge(qk_ready, 2 * (g - 1) + j // 2 + 1)
                    dve.tensor_tensor(part[:, j // 2, :].rearrange("p (b t) -> p b t", b=G),
                                      ps[j][:, 0:COLS].rearrange("p (b t) -> p b t", b=G), each(table[:, :], G), ALU.mult
                                      ).then_inc(rope_read, 1)
                for j in range(2):
                    dve.wait_ge(rope_read, 4 * g + 2 * j + 2)
                    dve.tensor_tensor((qf, kf)[j][:, g, :], by_cos[:, j, :], by_sin[:, j, :], ALU.add
                                      ).then_inc(qk_ready, 1)

            def out_of(g, t, s):
                rows, cols = steps_of[s]
                return sm.maxima[:, g, t, :].rearrange("p (c h) -> p h c", h=4)[:, rows[0]:rows[0] + 2, :]

            sm.dve_maxima(dve, out_of)
            sm.dve_shifts(dve, v_step)
            for g in range(GROUPS):
                dve.wait_ge(sm.o_ps, g + 1)
                for t in range(2):
                    out = ps[6 + t][0:TP, 0:8 * 17].rearrange("p (m k) -> p m k", m=8)
                    v_step.did(dve.reciprocal(den[:, t, :], out[:, :, 16]))
                for t in range(2):
                    wait_back(v_step, dve, 1 - t)
                    out = ps[6 + t][0:TP, 0:8 * 17].rearrange("p (c h k) -> p c h k", c=2, h=4)
                    scale = den[:, t, :].rearrange("p (c h) -> p c h", c=2).unsqueeze(3).broadcast_to([TP, 2, 4, 16])
                    dve.tensor_tensor(rn[:, g * U + t:(g + 1) * U:2, :].rearrange("p c (h k) -> p c h k", h=4),
                                      out[:, :, :, 0:16], scale, ALU.mult).then_inc(sm.o_read, 1)
                dve.wait_ge(sm.o_read, 2 * g + 2)
                dve.sem_inc(turn_in, 1)
            for g in range(GROUPS):
                dve.wait_ge(att_ps, g + 1)
                v_step.did(dve.tensor_tensor(tiles(w.xn, g), tiles(w.xn, g), tok_ps(g), ALU.add))
            v_step.wait(dve)
            rms(2)
            for g in range(GROUPS):
                v_step.did(dve.tensor_tensor(tiles(w.h, g), tiles(w.h, g), tiles(w.xn, g), ALU.add))
            for g in range(GROUPS):
                dve.wait_ge(logit_ps, g + 1)
                v_step.did(dve.tensor_reduce(best[:, g * U:(g + 1) * U], tok_ps(g, 8), X, ALU.max))
            for g in range(GROUPS):
                wait_back(v_step, dve, GROUPS - 1 - g)
                dve.tensor_tensor(tiles(z, g), tok_ps(g, 8), wide(best[:, g * U:(g + 1) * U], 8), ALU.subtract
                                  ).then_inc(z_ready, 1)
            dve.wait_ge(z_ready, GROUPS)
            for q in range(16 * GROUPS):
                dve.wait_ge(h_ps, 2 * q + 2)
                dve.wait_ge(silu_ready, q + 1)
                dve.tensor_tensor(hh[:, q % 16, q // 16, :], act1[:, q % 3, :], ps[3 + 2 * (q % 2)][0:85, 0:COLS], ALU.mult
                                  ).then_inc(hh_ready, 1)
            top_two(dve, v_step, w, z, z2, code, code_max, hot, hot2, best)

            def over_groups(f, back=GROUPS - 1):
                for g in range(GROUPS):
                    wait_back(v_step, dve, back)
                    v_step.did(f(g, total[:, g * U:(g + 1) * U]))

            dve.wait_ge(ex_ready, GROUPS)
            over_groups(lambda g, t: dve.tensor_reduce(t, tiles(ex, g), X, ALU.add))
            over_groups(lambda g, t: dve.reciprocal(t, t))
            over_groups(lambda g, t: dve.tensor_tensor(tiles(ex, g), tiles(ex, g), wide(t, 8), ALU.mult))
            over_groups(lambda g, t: dve.tensor_tensor(tiles(hot, g), tiles(hot, g), tiles(ex, g), ALU.mult))
            over_groups(lambda g, t: dve.tensor_reduce(t, tiles(hot, g), X, ALU.add))
            over_groups(lambda g, t: dve.tensor_scalar(t, t, 1e-9, None, ALU.add))
            over_groups(lambda g, t: dve.reciprocal(t, t))
            over_groups(lambda g, t: dve.tensor_tensor(tiles(hot, g), tiles(hot, g), wide(t, 8), ALU.mult))
            v_step.wait(dve)
            combine(dve, w, v_step, hot, prod, y_ps, y_read, summed, Y_BANKS)

        return sems


def attn3(nc, d, w):
    NT, NB = GROUPS * U, G * GROUPS
    STEPS = 2 * U
    ALL = GROUPS * STEPS
    PHI = (1.0 + math.sqrt(5.0)) / 2.0
    C1, C2 = PHI * math.sqrt(2.0) * 51.85, math.pi / PHI
    TURN = C1 / (2.0 * math.pi)
    HALF_PI = math.pi / 2.0
    BELOW_2PI = 6.2831845
    with ExitStack() as ctx:
        sb, sem, sems = layer_memory(nc, ctx, "attn3")
        sums = sb("sums", [TP, NT])
        qf, kf = sb("qf", [128, GROUPS, 4, COLS]), sb("kf", [128, GROUPS, 4, COLS])
        vals = sb("vals", [TP, NT, 512])
        step = [2, 2, SEQ]
        mag, low = sb("mag", [TP, 2] + step), sb("low", [TP, 2] + step)
        squares = low[:, 0, :, :, :].rearrange("p a c n -> p (a c n)")[:, 0:NT * D].rearrange("p (i n) -> p i n", n=D)
        z, frac, damp = (sb(n, [TP, STEPS] + step) for n in ("z", "frac", "damp"))
        cosine = sb("cosine", [TP, 2] + step)
        peak, total = sb("peak", [TP, STEPS, 4]), sb("total", [TP, STEPS, 4])
        half_pi = sb("half_pi", [TP, 1])
        aT = sb("aT", [TP, 2, 2, 4 * TP])
        v_step = Steps(sem("v_step"))
        var_ready, rstd_ready, xn_ready, turned, xT_ready = sem("var", "rstd", "xn_ready", "turned", "xT_ready")
        const_ready, q_ps, q_ready, k_ps, k_ready, v_ps, v_ready = sem(
            "const_ready", "q_ps", "q_ready", "k_ps", "k_ready", "v_ps", "v_ready")
        s_ps, mag_ready, low_ready, frac_ready, three_ready, above_ready, held_ready, filtered, peak_ready, shift_ready = sem(
            "s_ps", "mag_ready", "low_ready", "frac_ready", "three_ready", "above_ready", "held_ready", "filtered", "peak_ready", "shift_ready")
        exp_ready, recip_ready, z_ready, turns_ready, rest_ready, square_ready, damp_ready = sem(
            "exp_ready", "recip_ready", "z_ready", "turns_ready", "rest_ready", "square_ready", "damp_ready")
        sin_ready, cos_ready, prod_ready, sum_ready, a_ready, aT_ps, aT_ready, used, o_read = sem(
            "sin_ready", "cos_ready", "prod_ready", "sum_ready", "a_ready", "aT_ps", "aT_ready", "used", "o_read")
        block = ctx.enter_context(nc.Block())
        ps = w.psum

        def scores_of(j):
            b = 2 * (j % 2)
            return w.banks[0:TP, b:b + 2, 0:2 * SEQ].rearrange("p a (c n) -> p a c n", c=2)

        def q_bank(i):
            return 4 if i >= 4 or i % 2 else 2

        def flat(t, j):
            return t[:, j, :, :, :].rearrange("p a c n -> p (a c n)")

        @block.gpsimd
        def _(pool):
            pool.memset(half_pi[:, :], HALF_PI).then_inc(const_ready, 1)
            pool.wait_ge(const_ready, 1)
            roots(pool, w, [s for s, in per_group(sums)], var_ready, rstd_ready, 0)

            def remainder(j):
                pool.wait_ge(three_ready, j + 1)
                pool.tensor_tensor(flat(mag, j % 2), flat(mag, j % 2), flat(low, j % 2), ALU.subtract
                                   ).then_inc(frac_ready, 1)

            def square(j):
                i = j % STEPS
                pool.wait_ge(z_ready, j + 1)
                pool.tensor_tensor(flat(damp, i), flat(z, i), flat(z, i), ALU.mult).then_inc(square_ready, 1)

            def product(j):
                i = j % STEPS
                pool.wait_ge(sin_ready, j + 1)
                pool.wait_ge(damp_ready, j + 1)
                pool.tensor_tensor(flat(damp, i), flat(frac, i), flat(damp, i), ALU.mult).then_inc(prod_ready, 1)

            for t in range(STEPS + 3):
                if t < STEPS:
                    remainder(t)
                if t >= 3:
                    square(t - 3)
                    pool.wait_ge(turns_ready, t - 2)
                    pool.tensor_tensor(flat(frac, t - 3), flat(z, t - 3), flat(frac, t - 3), ALU.subtract
                                       ).then_inc(rest_ready, 1)
            for g in range(1, GROUPS):
                for t in range(STEPS + 2):
                    if t >= 2:
                        remainder(g * STEPS + t - 2)
                    if t < STEPS:
                        product((g - 1) * STEPS + t)
                for i in range(STEPS):
                    square(g * STEPS + i)
            for i in range(STEPS):
                product((GROUPS - 1) * STEPS + i)

        @block.tensor
        def _(pe):
            for g in range(GROUPS):
                pe.wait_ge(xn_ready, g + 1)
                turn_tokens(pe, w, g, tiles(w.xn, g)).then_inc(turned, 1)

            def queries_keys(i):
                g, c = i // 4, i % 4
                pe.wait_ge(xT_ready, g + 1)
                if i == 2 or i == 3:
                    pe.wait_ge(q_ready, i - 1)
                    pe.wait_ge(k_ready, i - 1)
                elif i >= 4:
                    pe.wait_ge(q_ready, i)
                    pe.wait_ge(k_ready, i)
                for wt, bank, done in ((w.a3_Wq, q_bank(i), q_ps), (w.a3_Wk, q_bank(i) + 1, k_ps)):
                    pe.matmul(ps[bank][:, 0:COLS], wt[:, 2 * c:2 * c + 2, :].rearrange("p h k -> p (h k)"),
                              w.xT[:, g, :], start=True, stop=True).then_inc(done, 1)

            def values(i):
                if i >= 2:
                    pe.wait_ge(v_ready, i - 1)
                pe.matmul(ps[6 + i % 2][0:TP, :], w.xT[:, i // U, i % U * TP:(i % U + 1) * TP],
                          w.a3_Wvo[:, :, :].rearrange("p h n -> p (h n)"), start=True, stop=True).then_inc(v_ps, 1)

            def turn_weights(j):
                i = j % STEPS
                pe.wait_ge(a_ready, j + 1)
                if j:
                    pe.wait_ge(aT_ready, j)
                for par in range(2):
                    for c in range(2):
                        for t in range(2):
                            last = pe.transpose(ps[4 + par][0:TP, (2 * c + t) * TP:(2 * c + t + 1) * TP],
                                                frac[:, i, par, c, t * TP:(t + 1) * TP], w.ident[0:TP, 0:TP])
                last.then_inc(aT_ps, 1)

            def weigh(j):
                tile, pair = j // 2, j % 2
                o = ps[6 + tile % 2][0:TP, 0:D]
                if pair == 0:
                    if tile >= 2:
                        pe.wait_ge(o_read, tile - 1)
                    pe.matmul(o, w.ones_row[:, 0:TP], w.a3_bo[:, :], start=True, stop=False)
                pe.wait_ge(aT_ready, j + 1)
                for par in range(2):
                    for c in range(2):
                        hd = 2 * (2 * pair + c) + par
                        for t in range(2):
                            stop = pair == 1 and par == 1 and c == 1 and t == 1
                            last = pe.matmul(o, aT[:, j % 2, par, (2 * c + t) * TP:(2 * c + t + 1) * TP],
                                             vals[:, 2 * (tile // 2) + t, hd * D:(hd + 1) * D], start=False, stop=stop)
                last.then_inc(used, 1)

            def scores(j):
                g, tile, pair = j // STEPS, j // 2, j % 2
                if j >= 2:
                    pe.wait_ge(filtered, j - 1)
                at, keys = (tile % U) * TP, (tile % U) // 2 * SEQ
                for par in range(2):
                    rows = slice(64 * par, 64 * par + 64)
                    for c in range(2):
                        last = pe.matmul(ps[2 * (j % 2) + par][0:TP, c * SEQ:(c + 1) * SEQ],
                                         qf[rows, g, 2 * pair + c, at:at + TP],
                                         kf[rows, g, 2 * pair + c, keys:keys + SEQ], start=True, stop=True)
                last.then_inc(s_ps, 1)

            for i in range(4):
                queries_keys(i)
            pe.wait_ge(q_ready, 4)
            pe.wait_ge(k_ready, 4)
            for t in range(STEPS):
                scores(t)
                if t < 4:
                    for i in range(4 + t, 4 * GROUPS, 4):
                        queries_keys(i)
                else:
                    for i in range(2 * (t - 4), NT, 8):
                        values(i)
                        values(i + 1)
            pe.wait_ge(v_ready, NT)
            pe.wait_ge(q_ready, 4 * GROUPS)
            pe.wait_ge(k_ready, 4 * GROUPS)
            for j in range(ALL + 1):
                if j + STEPS < ALL:
                    scores(j + STEPS)
                if j < ALL:
                    turn_weights(j)
                if j:
                    weigh(j - 1)

        @block.scalar
        def _(act):
            for g in range(GROUPS):
                act.wait_ge(turned, g + 1)
                act.activation(w.xT[0:D, g, :], ps[g][0:D, 0:COLS], ACT.Copy).then_inc(xT_ready, 1)

            def keys(i):
                act.wait_ge(k_ps, i + 1)
                act.activation(kf[:, i // 4, i % 4, :], ps[q_bank(i) + 1][:, 0:COLS], ACT.Copy).then_inc(k_ready, 1)

            def values(i):
                act.wait_ge(v_ps, i + 1)
                act.activation(vals[:, i, :], ps[6 + i % 2][0:TP, :], ACT.Copy, scale=1.0 / TURN).then_inc(v_ready, 1)

            for i in range(4):
                keys(i)
            act.wait_ge(const_ready, 1)

            def size(j):
                act.wait_ge(s_ps, j + 1)
                if j >= 2:
                    act.wait_ge(held_ready, j - 1)
                act.activation(mag[:, j % 2, :, :, :], scores_of(j), ACT.Abs, scale=1618.0 / 8.0).then_inc(mag_ready, 1)

            def exponentials(j):
                i = j % STEPS
                act.wait_ge(shift_ready, j + 1)
                for m in range(4):
                    head = z[:, i, m // 2, m % 2, :]
                    last = act.activation(head, head, ACT.Exp, scale=0.125, bias=peak[:, i, m:m + 1],
                                          accum_out=total[:, i, m:m + 1])
                last.then_inc(exp_ready, 1)

            def damping(j):
                i = j % STEPS
                act.wait_ge(square_ready, j + 1)
                act.activation(flat(damp, i), flat(damp, i), ACT.Exp, scale=-1.0 / (TURN * TURN * PHI)
                               ).then_inc(damp_ready, 1)

            def waves(j):
                i = j % STEPS
                act.wait_ge(rest_ready, j + 1)
                act.activation(flat(frac, i), flat(frac, i), ACT.Sin, scale=BELOW_2PI).then_inc(sin_ready, 1)
                if j >= 2:
                    act.wait_ge(sum_ready, j - 1)
                act.activation(flat(cosine, j % 2), flat(z, i), ACT.Sin, scale=-C2 / TURN, bias=half_pi[:, 0:1]
                               ).then_inc(cos_ready, 1)

            def copy_turned(j):
                act.wait_ge(aT_ps, j + 1)
                if j >= 2:
                    act.wait_ge(used, j - 1)
                act.activation(aT[:, j % 2, :, :], w.banks[0:TP, 4:6, 0:4 * TP], ACT.Copy).then_inc(aT_ready, 1)

            act.preload_act_table(ACT.Exp)
            for t in range(STEPS + 4):
                if t < STEPS:
                    size(t)
                    if t < 4:
                        for i in range(4 + t, 4 * GROUPS, 4):
                            keys(i)
                if 1 <= t <= STEPS:
                    exponentials(t - 1)
                if 4 <= t < STEPS:
                    for i in range(2 * (t - 4), NT, 8):
                        values(i)
                        values(i + 1)
                if t >= 4:
                    damping(t - 4)
            for g in range(1, GROUPS + 1):
                act.preload_act_table(ACT.Sin)
                for t in range(STEPS + 3):
                    if g < GROUPS and 2 <= t < STEPS + 2:
                        size(g * STEPS + t - 2)
                    if t < STEPS:
                        waves((g - 1) * STEPS + t)
                    if t >= 3:
                        copy_turned((g - 1) * STEPS + t - 3)
                if g < GROUPS:
                    act.preload_act_table(ACT.Exp)
                    for t in range(STEPS + 2):
                        if t < STEPS:
                            exponentials(g * STEPS + t)
                        if t >= 2:
                            damping(g * STEPS + t - 2)

        @block.vector
        def _(dve):
            normalize(dve, v_step, per_group(w.h, w.xn, squares, sums), 1e-5, var_ready, rstd_ready, 0, ready=xn_ready)

            def queries(i):
                dve.wait_ge(q_ps, i + 1)
                dve.tensor_copy(qf[:, i // 4, i % 4, :], ps[q_bank(i)][:, 0:COLS]).then_inc(q_ready, 1)

            for i in range(4):
                queries(i)

            def add_out(tile):
                dve.wait_ge(used, 2 * tile + 2)
                dve.tensor_tensor(w.h[:, tile, :], w.h[:, tile, :], ps[6 + tile % 2][0:TP, 0:D], ALU.add
                                  ).then_inc(o_read, 1)

            def stage(j, s):
                g, i = j // STEPS, j % STEPS
                y, lo, f = flat(mag, j % 2), flat(low, j % 2), flat(z, i)
                y4, lo4, f4 = mag[:, j % 2, :, :, :], low[:, j % 2, :, :, :], z[:, i, :, :, :]
                heads = f4.rearrange("p a c n -> p (a c) n")
                if s == 0:
                    dve.wait_ge(mag_ready, j + 1)
                    dve.tensor_scalar(lo, y, 1.0 / 3.0, MAGIC, ALU.mult, ALU.add).then_inc(low_ready, 1)
                elif s == 1:
                    dve.wait_ge(low_ready, j + 1)
                    dve.tensor_scalar(lo, lo, -MAGIC, 3.0, ALU.add, ALU.mult).then_inc(three_ready, 1)
                elif s == 2:
                    dve.wait_ge(frac_ready, j + 1)
                    dve.scalar_tensor_tensor(out=lo4, in0=y4, scalar=0.0, in1=scores_of(j), op0=ALU.is_ge,
                                             op1=ALU.mult).then_inc(above_ready, 1)
                elif s == 9:
                    dve.wait_ge(above_ready, j + 1)
                    dve.scalar_tensor_tensor(out=lo, in0=y, scalar=1.0, in1=lo, op0=ALU.is_lt,
                                             op1=ALU.mult).then_inc(held_ready, 1)
                elif s == 3:
                    dve.wait_ge(held_ready, j + 1)
                    dve.scalar_tensor_tensor(out=f4, in0=lo4, scalar=1.0 / PHI - 1.0, in1=scores_of(j), op0=ALU.mult,
                                             op1=ALU.add).then_inc(filtered, 1)
                elif s == 4:
                    dve.wait_ge(filtered, j + 1)
                    dve.tensor_reduce(peak[:, i, :], heads, X, ALU.max).then_inc(peak_ready, 1)
                elif s == 5:
                    dve.wait_ge(peak_ready, j + 1)
                    dve.tensor_scalar(peak[:, i, :], peak[:, i, :], -0.125, None, ALU.mult).then_inc(shift_ready, 1)
                elif s == 6:
                    dve.wait_ge(exp_ready, j + 1)
                    dve.reciprocal(total[:, i, :], total[:, i, :]).then_inc(recip_ready, 1)
                elif s == 7:
                    dve.wait_ge(recip_ready, j + 1)
                    dve.scalar_tensor_tensor(out=heads, in0=heads, scalar=TURN, in1=wide(total[:, i, :], SEQ),
                                             op0=ALU.mult, op1=ALU.mult).then_inc(z_ready, 1)
                elif s == 10:
                    dve.wait_ge(turns_ready, j + 1)
                    dve.tensor_tensor(flat(frac, i), f, flat(frac, i), ALU.subtract).then_inc(rest_ready, 1)
                else:
                    dve.wait_ge(z_ready, j + 1)
                    if g:
                        dve.wait_ge(aT_ps, j - STEPS + 1)
                    dve.tensor_scalar(flat(frac, i), f, MAGIC, -MAGIC, ALU.add, ALU.add).then_inc(turns_ready, 1)

            def sum_up(j):
                i = j % STEPS
                dve.wait_ge(prod_ready, j + 1)
                dve.wait_ge(cos_ready, j + 1)
                dve.tensor_tensor(flat(damp, i), flat(damp, i), flat(cosine, j % 2), ALU.add).then_inc(sum_ready, 1)

            def times_weight(j):
                i = j % STEPS
                dve.wait_ge(sum_ready, j + 1)
                dve.tensor_tensor(flat(frac, i), flat(damp, i), flat(z, i), ALU.mult).then_inc(a_ready, 1)

            for t in range(STEPS + 3):
                for s, behind in ((8, 3), (0, 0), (4, 1), (1, 0), (5, 1), (6, 2), (2, 0), (7, 2), (9, 0), (3, 0)):
                    if 0 <= t - behind < STEPS:
                        stage(t - behind, s)
                    if s == 0 and t < 4:
                        for i in range(4 + t, 4 * GROUPS, 4):
                            queries(i)
            for g in range(1, GROUPS + 1):
                for t in range(STEPS + 3):
                    now, before = g * STEPS + t - 2, (g - 1) * STEPS + t - 1
                    filtering, peaks = g < GROUPS and 2 <= t < STEPS + 2, g < GROUPS and 3 <= t < STEPS + 3
                    weighing = 1 <= t <= STEPS
                    if filtering:
                        stage(now, 0)
                    if peaks:
                        stage(now - 1, 4)
                    if filtering:
                        stage(now, 1)
                    if peaks:
                        stage(now - 1, 5)
                    if weighing:
                        sum_up(before)
                    if filtering:
                        stage(now, 2)
                    if weighing:
                        times_weight(before)
                    if filtering:
                        stage(now, 9)
                    if t % 2 == 1 and before >= 4 and 3 <= t <= STEPS + 1:
                        add_out((before - 4) // 2)
                    if filtering:
                        stage(now, 3)
                if g < GROUPS:
                    for t in range(STEPS + 2):
                        for s, behind in ((8, 1), (6, 0), (10, 2), (7, 0)):
                            if 0 <= t - behind < STEPS:
                                stage(g * STEPS + t - behind, s)
            add_out(NT - 1)
            dve.wait_ge(o_read, NT)

        return sems


def early_fusion(nc, d, out):
    w = Core()
    with ExitStack() as ctx:
        allocate(nc, ctx, w)
        loaded_p = ctx.enter_context(nc.semaphore("loaded_p"))
        stored = ctx.enter_context(nc.semaphore("stored"))

        def clear(sems):
            for s in sems:
                nc.sync.sem_clear(s)
            nc.all_engine_barrier()

        clear(load_weights(nc, d, w, loaded_p))
        with nc.Fori(0, PASSES) as p:
            clear(tok(nc, d, w, p))
            for layer in LAYERS:
                clear(layer(nc, d, w))
            store(nc, w, p, out, stored)
            clear([stored])


def store(nc, w, p, out, stored):
    NB = G * GROUPS
    with nc.Block() as block:
        @block.sync
        def _(sp):
            sp.dma_start(out[bass.ds(p * NB, NB)].rearrange("b (t q) n -> q (b t) n", t=2), w.h[:, :, :]
                         ).then_inc(stored, 16)
            sp.wait_ge(stored, 16)

        @block.gpsimd
        def _(pool):
            pool.memset(w.in_first[:], 0)


LAYERS = [mamba, ffn0, attn1, ffn1, attn2, ffn2, attn3, ffn3]


def constants():
    t = np.arange(TP)
    seen = (t[:, None] <= t[None, :])
    sel_bc = np.zeros((96, 2 * NST, 128), np.float32)
    for part in range(3):
        for n in range(2 * NST):
            sel_bc[32 * part + n, n, :] = 1.0
    sel_map = np.zeros((96, 16, TP), np.float32)
    for m in range(16):
        sel_map[m:96:32, m, :] = -1.0
    hd = 16
    inv_freq = 1.0 / 10000.0 ** (np.arange(0, hd, 2, dtype=np.float32) / hd)
    freqs = np.outer(np.arange(SEQ, dtype=np.float32), inv_freq)
    emb = np.concatenate([freqs, freqs], axis=-1)
    cos, sin = np.zeros((128, SEQ), np.float32), np.zeros((128, SEQ), np.float32)
    for n in range(4):
        cos[32 * n:32 * n + 16] = np.cos(emb).T
        sin[32 * n:32 * n + 16] = np.sin(emb).T
        sin[32 * n:32 * n + 8] *= -1.0
    return {
        "c_ident": np.eye(128, dtype=np.float32),
        "c_causal01": np.concatenate([seen, np.ones_like(seen), seen], 1).astype(np.float32),
        "c_maskT": np.concatenate([np.where(seen, 0.0, NEG), np.zeros((TP, TP))], 1).astype(np.float32),
        "c_maskQ": np.concatenate([np.zeros((TP, TP)), np.where(seen.T, 0.0, NEG)], 1).astype(np.float32),
        "c_rank": np.tile(8.0 - np.arange(8, dtype=np.float32), (TP, 1)),
        "c_sel_bc": sel_bc, "c_sel_map": sel_map,
        "c_row_half": (np.arange(IMG)[:, None] // PATCH % 2 == np.arange(2)).astype(np.float32),
        "c_rope_cos": cos, "c_rope_sin": sin,
    }


def kernel(**inputs):
    import concourse.bacc as bacc
    from concourse.bass_utils import run_bass_kernel_spmd

    nc = bacc.Bacc("TRN2", target_bir_lowering=False, num_devices=1)
    arrays, d = {}, {}
    for name, a in {**inputs, **constants()}.items():
        a = np.ascontiguousarray(a)
        arrays[name + "_dram"] = a
        d[name] = nc.dram_tensor(name + "_dram", a.shape, mybir.dt.from_np(a.dtype), kind="ExternalInput").ap()
    out = nc.dram_tensor("out_dram", (B, SEQ, D), F32, kind="ExternalOutput").ap()
    early_fusion(nc, d, out)
    r = run_bass_kernel_spmd(nc, [arrays], core_ids=[0])
    return r.results[0]["out_dram"]
```

```python
import math
from contextlib import ExitStack

import numpy as np

import concourse.bass as bass
from concourse import mybir

F32 = mybir.dt.float32
BF16 = mybir.dt.bfloat16
I32 = mybir.dt.int32
U32 = mybir.dt.uint32
ALU = mybir.AluOpType
ACT = mybir.ActivationFunctionType
X = mybir.AxisListType.X

B = 8
PATCH, IMG_C, IMG = 16, 3, 96
GRID = IMG // PATCH
N_IMG = GRID * GRID
N_TXT = 128
SEQ = N_IMG + N_TXT
TP = SEQ // 2
D = 64
G = 2
U = 2 * G
COLS = G * SEQ
GROUPS = 2
PASSES = B // (G * GROUPS)
PDIM = PATCH * PATCH * IMG_C
KC = PDIM // 128
DI, NST, DTR, DCONV = 128, 16, 16, 4
HID2 = 8 * 170
CHUNKS2 = [min(128, HID2 - at) for at in range(0, HID2, 128)]
NEG = -float(2.0 ** 100)
MAGIC = 12582912.0
BANK = 512


class Steps:

    def __init__(self, sem):
        self.sem, self.n = sem, 0

    def did(self, ins):
        ins.then_inc(self.sem, 1)
        self.n += 1

    def wait(self, eng):
        eng.wait_ge(self.sem, self.n)


class Core:
    pass


def wide(ap, n):
    return ap.unsqueeze(2).broadcast_to([ap.shape[0], ap.shape[1], n])


def each(ap, n):
    return ap.unsqueeze(1).broadcast_to([ap.shape[0], n, ap.shape[1]])


def allocate(nc, ctx, w):

    def sb(name, shape, dt=F32):
        return ctx.enter_context(nc.sbuf_tensor(name, shape, dt))

    w.banks = ctx.enter_context(nc.psum_tensor("banks", [128, 8, BANK], F32))
    w.psum = [w.banks[:, i, :] for i in range(8)]
    NT = GROUPS * U
    w.h = sb("h", [TP, NT, D])
    w.xT = sb("xT", [D + 1, GROUPS, COLS])
    w.xn = sb("xn", [TP, NT, D])
    w.resid = sb("resid", [TP, 2, 4, 16])
    w.in_first = sb("in_first", [TP, 2, 4, 16], U32)
    w.ident = sb("ident", [128, 128])
    w.ident_b = sb("ident_b", [TP, TP], BF16)
    w.causal01 = sb("causal01", [TP, 3 * TP])
    w.maskT = sb("maskT", [TP, SEQ], BF16)
    w.maskQ = sb("maskQ", [TP, SEQ], BF16)
    w.rank = sb("rank", [TP, 8])
    w.sel_bc = sb("sel_bc", [96, 2 * NST, 128], BF16)
    w.rope_cos = sb("rope_cos", [128, SEQ])
    w.rope_sin = sb("rope_sin", [128, SEQ])
    w.ones_row = sb("ones_row", [1, 128])
    w.neg_half = sb("neg_half", [128, 64])
    w.img_tok = sb("img_tok", [N_IMG, B, D])
    w.inT = sb("inT", [D + 1, 2 * DI])
    w.conv_w = sb("conv_w", [DI, DCONV])
    w.conv_b = sb("conv_b", [DI, 1])
    w.xp_dtT = sb("xp_dtT", [DI, DTR])
    w.xp_bcT = sb("xp_bcT", [DI, 3, 2 * NST])
    w.dtT = sb("dtT", [DTR, DI])
    w.dt_b = sb("dt_b", [DI, 1])
    w.A = sb("A", [DI, NST])
    w.D_ssm = sb("D_ssm", [DI, 1])
    w.outT = sb("outT", [DI, D])
    w.out_b = sb("out_b", [1, D])
    w.m_ln1_g = sb("m_ln1_g", [TP, D])
    w.m_ln1_b = sb("m_ln1_b", [TP, D])
    w.m_ln2_g = sb("m_ln2_g", [TP, D])
    w.m_ln2_b = sb("m_ln2_b", [TP, D])
    w.fc1T = sb("fc1T", [D + 1, 256])
    w.fc2T = sb("fc2T", [128, 2, D])
    w.fc2_b = sb("fc2_b", [1, D])
    w.f0_W1 = sb("f0_W1", [D + 1, 256])
    w.f0_Wg = sb("f0_Wg", [128, 2, 8])
    w.f0_bg = sb("f0_bg", [1, 8])
    w.f0_Wd = sb("f0_Wd", [128, 2, 8, D])
    w.a1_Wk = sb("a1_Wk", [D, 8, 32])
    w.a1_Wq = sb("a1_Wq", [D, 8, 32])
    w.a1_Wvo = sb("a1_Wvo", [D, 8, D])
    w.f1_hlT = sb("f1_hlT", [D + 1, D])
    w.f1_qkT = sb("f1_qkT", [D, 4, 128])
    w.f1_vT = sb("f1_vT", [D, D])
    w.f1_gateT = sb("f1_gateT", [128, 2, 16])
    w.f1_gate_b = sb("f1_gate_b", [1, 16])
    w.f1_fc1T = sb("f1_fc1T", [D + 1, D])
    w.f1_fc2T = sb("f1_fc2T", [D + 1, D])
    w.f1_ln_g = sb("f1_ln_g", [TP, 16])
    w.f1_ln_b = sb("f1_ln_b", [TP, 16])
    w.f1_fn_g = sb("f1_fn_g", [TP, 16])
    w.f1_fn_b = sb("f1_fn_b", [TP, 16])
    w.f1_fgT = sb("f1_fgT", [D, 4])
    w.a2_Wq = sb("a2_Wq", [128, 4, D])
    w.a2_kT = sb("a2_kT", [D, 8, D])
    w.a2_vT = sb("a2_vT", [D, 8, D])
    w.a2_woT = sb("a2_woT", [128, 4, D])
    w.a2_M = sb("a2_M", [D + 1, G * GROUPS, D])
    w.f2_ln1 = sb("f2_ln1", [D, 1])
    w.f2_ln2 = sb("f2_ln2", [D, 1])
    w.f2_qkT = sb("f2_qkT", [D, 2, 128])
    w.f2_vT = sb("f2_vT", [D, 32])
    w.f2_oT = sb("f2_oT", [D, D])
    w.f2_routerT = sb("f2_routerT", [D, 8])
    w.f2_w1T = sb("f2_w1T", [D, HID2])
    w.f2_w3T = sb("f2_w3T", [D, HID2])
    w.f2_w2T = sb("f2_w2T", [128, len(CHUNKS2), D])
    w.sel_expert = sb("sel_expert", [96, HID2], BF16)
    w.a3_Wq = sb("a3_Wq", [D + 1, 8, D])
    w.a3_Wk = sb("a3_Wk", [D + 1, 8, D])
    w.a3_Wvo = sb("a3_Wvo", [D + 1, 8, D])
    w.a3_bo = sb("a3_bo", [1, D])
    w.f3_g = sb("f3_g", [D, 1])
    w.f3_b = sb("f3_b", [D, 1])
    w.f3_Wr = sb("f3_Wr", [D + 1, 8])
    w.f3_W1 = sb("f3_W1", [D + 1, 8, 128])
    w.f3_W2 = sb("f3_W2", [128, 8, D])
    w.bias3 = sb("bias3", [3, 2, 8 * D], BF16)
    w.ones3 = sb("ones3", [3, 128], BF16)


def load_weights(nc, d, w, loaded_p):
    with ExitStack() as ctx:
        def sb(name, shape, dt=F32):
            return ctx.enter_context(nc.sbuf_tensor(name, shape, dt))

        sems = []

        def sem(name):
            sems.append(ctx.enter_context(nc.semaphore(name)))
            return sems[-1]

        n_tok = sb("n_tok", [D, IMG_C, PATCH, PATCH])
        image = sb("image", [IMG_C * PATCH, B, GRID, IMG])
        tokT = sb("tokT", [IMG_C * PATCH, PATCH, D])
        img_featT = sb("img_featT", [D, B, N_IMG])
        tok_b = sb("tok_b", [1, D])
        n_in = sb("n_in", [128, 2, D])
        n_xp = sb("n_xp", [DTR + 2 * NST, DI])
        n_dt = sb("n_dt", [DI, DTR])
        n_out = sb("n_out", [D, DI])
        n_fc1 = sb("n_fc1", [128, 2, D])
        n_fc2 = sb("n_fc2", [D, 256])
        n_Wv1 = sb("n_Wv1", [D, 8, D])
        a1_WvT, a1_Wo = sb("a1_WvT", [128, 4, D]), sb("a1_Wo", [128, 4, D])
        a3_WvT, a3_Wo = sb("a3_WvT", [128, 4, D + 1]), sb("a3_Wo", [128, 4, D])
        n_hl = sb("n_hl", [D, D])
        n_q = sb("n_q", [128, 320])
        n_v = sb("n_v", [D, D])
        n_f1 = sb("n_f1", [D, D])
        n_f2 = sb("n_f2", [D, D])
        n_gate = sb("n_gate", [16, 256])
        n_fg = sb("n_fg", [4, D])
        n_kv = sb("n_kv", [128, 8, D])
        n_wo2 = sb("n_wo2", [D, 512])
        n_q2 = sb("n_q2", [128, 2, D])
        n_v2 = sb("n_v2", [32, D])
        n_o2 = sb("n_o2", [D, D])
        n_r2 = sb("n_r2", [8, D])
        n_w1 = sb("n_w1", [128, len(CHUNKS2), D])
        n_w3 = sb("n_w3", [128, len(CHUNKS2), D])
        n_sel_expert = sb("n_sel_expert", [96, HID2])
        n_w2 = sb("n_w2", [D, 8, 170])
        n_Wv3 = sb("n_Wv3", [D + 1, 8, D])
        n_sel_bc = sb("n_sel_bc", [96, 2 * NST, 128])
        n_maskT, n_maskQ = sb("n_maskT", [TP, SEQ]), sb("n_maskQ", [TP, SEQ])
        n_bias, bias_high = sb("n_bias", [3, 2, 8 * D]), sb("bias_high", [3, 2, 8 * D], BF16)
        less = sb("less", [3, 2])
        mean_k = sb("mean_k", [D, 2, 8])
        a_pos = sb("a_pos", [DI, NST])

        zeroed, loaded_s, to_turn_in, to_narrow_in = map(sem, ("zeroed", "loaded_s", "to_turn_in", "to_narrow_in"))
        turned, copied_v, copied_a = sem("turned"), sem("copied_v"), sem("copied_a")
        vo_done, decay_exp, centred = sem("vo_done"), sem("decay_exp"), sem("centred")

        image_in, tok_in, tok_turned, tok_copied, tok_ps, feat_ready, img_turned, img_ready = map(
            sem, ("image_in", "tok_in", "tok_turned", "tok_copied", "tok_ps", "feat_ready", "img_turned", "img_ready"))
        bias_split = sem("bias_split")
        turns = [(n_in[:, c, :], w.inT[0:D, c * 128:(c + 1) * 128]) for c in range(2)]
        turns += [(n_xp[:, :], None)]
        XP = len(turns) - 1
        turns += [(n_dt[:, :], w.dtT[:, :]), (n_out[:, :], w.outT[:, :])]
        turns += [(n_fc1[:, c, :], w.fc1T[0:D, c * 128:(c + 1) * 128]) for c in range(2)]
        turns += [(n_fc2[:, c * 128:(c + 1) * 128], w.fc2T[:, c, :]) for c in range(2)]
        turns += [(n_Wv1[:, 2 * c:2 * c + 2, :].rearrange("p a b -> p (a b)"), a1_WvT[:, c, :]) for c in range(4)]
        turns += [(n_hl[:, :], w.f1_hlT[0:D, :])]
        turns += [(n_fg[:, :], w.f1_fgT[:, :])]
        for c in range(4):
            turns += [(n_kv[:, c, :], w.a2_kT[:, 2 * c:2 * c + 2, :].rearrange("p a b -> p (a b)")),
                      (n_kv[:, 4 + c, :], w.a2_vT[:, 2 * c:2 * c + 2, :].rearrange("p a b -> p (a b)")),
                      (n_wo2[:, c * 128:(c + 1) * 128], w.a2_woT[:, c, :])]
        turns += [(n_v2[:, :], w.f2_vT[:, :]), (n_o2[:, :], w.f2_oT[:, :]), (n_r2[:, :], w.f2_routerT[:, :])]
        w2_flat = n_w2[:, :, :].rearrange("p e f -> p (e f)")
        for c, rows in enumerate(CHUNKS2):
            at = slice(128 * c, 128 * c + rows)
            turns += [(n_w1[0:rows, c, :], w.f2_w1T[:, at]), (n_w3[0:rows, c, :], w.f2_w3T[:, at]),
                      (w2_flat[:, at], w.f2_w2T[0:rows, c, :])]
        turns += [(n_Wv3[:, 2 * c:2 * c + 2, :].rearrange("p a b -> p (a b)"), a3_WvT[:, c, :]) for c in range(4)]
        n_plain = len(turns) // 4
        turns += [(n_q[:, n * D:(n + 1) * D], w.f1_qkT[:, n, :]) for n in range(4)]
        turns += [(n_v[:, :], w.f1_vT[:, :]), (n_f1[:, :], w.f1_fc1T[0:D, :]), (n_f2[:, :], w.f1_fc2T[0:D, :])]
        turns += [(n_gate[:, c * 128:(c + 1) * 128], w.f1_gateT[:, c, :]) for c in range(2)]
        turns += [(n_q2[:, c, :], w.f2_qkT[:, c, :]) for c in range(2)]
        fours = [turns[i:i + 4] for i in range(0, len(turns), 4)]
        assert XP < 4

        def slot(i, j, rows, cols):
            return w.psum[i % 6][0:rows, j * 128:j * 128 + cols]

        block = ctx.enter_context(nc.Block())
        row = lambda ap: ap.rearrange("(a n) -> a n", a=1)
        col = lambda ap: ap.rearrange("(n a) -> n a", a=1)
        spread = lambda ap, p: row(ap).broadcast_to([p, ap.shape[0]])

        embedding = [(n_tok[:, :, :, :].rearrange("p a b c -> p (a b c)"), d["L0_tok_W"]),
                     (w.ident[:, :], d["c_ident"]), (tok_b[:, :], row(d["L0_tok_b"]))]
        to_narrow = [(n_sel_bc[:, :, :], d["c_sel_bc"]), (n_sel_expert[:, :], d["c_sel_expert"]),
                     (n_maskT[:, :], d["c_maskT"]), (n_maskQ[:, :], d["c_maskQ"])]
        to_turn = [
            (n_in[:, :, :], d["L0_attn_in_proj_w"].rearrange("(c p) k -> p c k", p=128)),
            (n_xp[:, :], d["L0_attn_x_proj_w"]),
            (n_dt[:, :], d["L0_attn_dt_proj_w"]),
            (n_out[:, :], d["L0_attn_out_proj_w"]),
            (n_fc1[:, :, :], d["L0_attn_fc1_w"].rearrange("(c p) k -> p c k", p=128)),
            (n_fc2[:, :], d["L0_attn_fc2_w"]),
            (n_Wv1[:, :, :], d["L1_attn_Wvs"].rearrange("h p k -> p h k")),
            (n_hl[:, :], d["L1_ffn_hl_w"].rearrange("n o k -> (n o) k")),
            (n_fg[:, :], d["L1_ffn_fgate_w"]),
            (n_kv[:, :, :], d["L2_attn_w_qkv"][512:1536, :].rearrange("(c p) k -> p c k", p=128)),
            (n_wo2[:, :], d["L2_attn_w_out"]),
            (n_v2[:, :], d["L2_ffn_wv"]),
            (n_o2[:, :], d["L2_ffn_wo"]),
            (n_r2[:, :], d["L2_ffn_router_w"]),
            (n_w2[:, :, :], d["L2_ffn_w2"].rearrange("e p f -> p e f")),
            (n_Wv3[0:D, :, :], d["L3_attn_Wv"].rearrange("p (h k) -> p h k", h=8)),
            (n_Wv3[D:D + 1, :, :], row(d["L3_attn_bv"]).rearrange("a (h k) -> a h k", h=8)),
        ]
        direct = [
            (w.inT[D:D + 1, :], row(d["L0_attn_in_proj_b"])),
            (w.conv_w[:, :], d["L0_attn_conv_w"]),
            (w.conv_b[:, :], col(d["L0_attn_conv_b"])),
            (w.dt_b[:, :], col(d["L0_attn_dt_proj_b"])),
            (w.A[:, :], d["L0_attn_A_log"]),
            (w.D_ssm[:, :], col(d["L0_attn_D_ssm"])),
            (w.out_b[:, :], row(d["L0_attn_out_proj_b"])),
            (w.fc1T[D:D + 1, :], row(d["L0_attn_fc1_b"])),
            (w.fc2_b[:, :], row(d["L0_attn_fc2_b"])),
            (w.f0_W1[0:D, :], d["L0_ffn_W1"]),
            (w.f0_W1[D:D + 1, :], row(d["L0_ffn_b1"])),
            (w.f0_Wg[:, :, :], d["L0_ffn_Wg"].rearrange("(c p) e -> p c e", p=128)),
            (w.f0_bg[:, :], row(d["L0_ffn_bg"])),
            (w.f0_Wd[:, 0, :, :], d["L0_ffn_Wd"][:, 0:128, :].rearrange("e p n -> p e n")),
            (w.f0_Wd[:, 1, :, :], d["L0_ffn_Wd"][:, 128:256, :].rearrange("e p n -> p e n")),
            (n_bias[:, 0, :], row(d["L0_ffn_bd"].rearrange("e n -> (e n)")).broadcast_to([3, 8 * D])),
            (w.a1_Wk[:, :, :], d["L1_attn_Wks"].rearrange("h p k -> p h k")),
            (w.a1_Wq[:, :, :], d["L1_attn_Wqs"].rearrange("h p k -> p h k")),
            (a1_Wo[:, :, :], d["L1_attn_Wo"].rearrange("(c a) p k -> (a p) c k", a=2)),
            (w.f1_hlT[D:D + 1, :], d["L1_ffn_hl_b"].rearrange("(a n) o -> a (n o)", a=1)),
            (w.f1_gate_b[:, :], d["L1_ffn_gate_b"].rearrange("(a n) o -> a (n o)", a=1)),
            (w.a2_Wq[:, :, :], d["L2_attn_w_qkv"][0:512, :].rearrange("(c p) k -> p c k", p=128)),
            (w.f2_ln1[:, :], col(d["L2_ffn_ln1_w"])),
            (w.f2_ln2[:, :], col(d["L2_ffn_ln2_w"])),
            (w.a3_Wq[0:D, :, :], d["L3_attn_Wq"].rearrange("p (h k) -> p h k", h=8)),
            (w.a3_Wk[0:D, :, :], d["L3_attn_Wk"].rearrange("p (h k) -> p h k", h=8)),
            (w.a3_Wq[D:D + 1, :, :], row(d["L3_attn_bq"]).rearrange("a (h k) -> a h k", h=8)),
            (w.a3_Wk[D:D + 1, :, :], row(d["L3_attn_bk"]).rearrange("a (h k) -> a h k", h=8)),
            (a3_Wo[:, :, :], d["L3_attn_Wo"].rearrange("(c p) k -> p c k", p=128)),
            (w.a3_bo[:, :], row(d["L3_attn_bo"])),
            (w.f3_g[:, :], col(d["L3_ffn_gamma"])),
            (w.f3_b[:, :], col(d["L3_ffn_beta"])),
            (w.f3_Wr[0:D, :], d["L3_ffn_Wr"]),
            (w.f3_Wr[D:D + 1, :], row(d["L3_ffn_br"])),
            (w.f3_W1[0:D, :, :], d["L3_ffn_W1"].rearrange("e p n -> p e n")),
            (w.f3_W1[D:D + 1, :, :], d["L3_ffn_b1"].rearrange("(a e) n -> a e n", a=1)),
            (w.f3_W2[:, :, :], d["L3_ffn_W2"].rearrange("e p n -> p e n")),
            (n_bias[:, 1, :], row(d["L3_ffn_b2"].rearrange("e n -> (e n)")).broadcast_to([3, 8 * D])),
            (less[:, :], d["c_less"]),
            (w.causal01[:, :], d["c_causal01"]),
            
            (w.rank[:, :], d["c_rank"]),
            (w.rope_cos[:, :], d["c_rope_cos"]),
            (w.rope_sin[:, :], d["c_rope_sin"]),
        ]
        for a, n, k in ((w.m_ln1_g, "L0_attn_ln1_g", D), (w.m_ln1_b, "L0_attn_ln1_b", D),
                        (w.m_ln2_g, "L0_attn_ln2_g", D), (w.m_ln2_b, "L0_attn_ln2_b", D),
                        (w.f1_ln_g, "L1_ffn_ln_g", 16), (w.f1_ln_b, "L1_ffn_ln_b", 16),
                        (w.f1_fn_g, "L1_ffn_fnorm_g", 16), (w.f1_fn_b, "L1_ffn_fnorm_b", 16)):
            direct.append((a[:, :], spread(d[n], TP)))
        whole = 128 * (HID2 // 128)
        for tile, name in ((n_w1, "L2_ffn_w1"), (n_w3, "L2_ffn_w3")):
            flat = d[name].rearrange("e f k -> (e f) k")
            to_turn += [(tile[:, 0:whole // 128, :], flat[0:whole].rearrange("(c p) k -> p c k", p=128)),
                        (tile[0:HID2 - whole, whole // 128, :], flat[whole:HID2])]
        for b in range(G * GROUPS):
            direct.append((w.a2_M[D:D + 1, b, :], row(d["L2_attn_b_out"])))
        for n in range(4):
            direct.append((w.f1_fc1T[D:D + 1, 16 * n:16 * n + 16], row(d["L1_ffn_fc1_b"])))
            direct.append((w.f1_fc2T[D:D + 1, 16 * n:16 * n + 16], row(d["L1_ffn_fc2_b"])))

        sparse = []
        for e in range(4):
            dst = n_q[32 * e:32 * e + 16, :].rearrange("p (n c) -> p n c", c=80)[:, :, 0:16]
            sparse.append((dst, d["L1_ffn_wq"][:, e, :, :].rearrange("n o k -> o n k")))
        dst = n_q[16:32, :].rearrange("p (n c) -> p n c", c=80)[:, :, 0:16]
        sparse.append((dst, d["L1_ffn_wk"].rearrange("n o k -> o n k")))
        for n in range(4):
            at = slice(16 * n, 16 * n + 16)
            sparse += [(n_v[at, at], d["L1_ffn_wv"][n]), (n_f1[at, at], d["L1_ffn_fc1_w"]),
                       (n_f2[at, at], d["L1_ffn_fc2_w"]),
                       (n_gate[4 * n:4 * n + 4, 64 * n:64 * n + 64], d["L1_ffn_gate_w"][n])]
            sparse += [(n_q2[32 * n:32 * n + 16, 0, :], d["L2_ffn_wq"][16 * n:16 * n + 16, :]),
                       (n_q2[32 * n:32 * n + 8, 1, :], d["L2_ffn_wq"][16 * n + 8:16 * n + 16, :]),
                       (n_q2[32 * n + 8:32 * n + 16, 1, :], d["L2_ffn_wq"][16 * n:16 * n + 8, :])]
        for n in range(2):
            at, m = 32 * n + 16, 16 * n
            sparse += [(n_q2[at:at + 16, 0, :], d["L2_ffn_wk"][m:m + 16, :]),
                       (n_q2[at:at + 8, 1, :], d["L2_ffn_wk"][m + 8:m + 16, :]),
                       (n_q2[at + 8:at + 16, 1, :], d["L2_ffn_wk"][m:m + 8, :])]
        zero = [n_q, n_v, n_f1, n_f2, n_gate, n_q2]
        rest = [(w.ones_row[:, :], 1.0), (w.ones3[:, :], 1.0), (w.neg_half[:, :], -0.5), (w.in_first[:], 1), (w.resid[:], 0.0),
                (w.xT[D:D + 1, :, :], 1.0)]

        def all_loaded(eng):
            eng.wait_ge(to_turn_in, 16 * len(to_turn))
            eng.wait_ge(to_narrow_in, 16 * len(to_narrow))
            eng.wait_ge(loaded_s, 16 * len(direct))
            eng.wait_ge(loaded_p, 16 * len(sparse))

        @block.sync
        def _(sp):
            for dst, src in embedding:
                sp.dma_start(dst, src).then_inc(tok_in, 16)
            for c in range(IMG_C):
                for y in range(GRID):
                    sp.dma_start(image[PATCH * c:PATCH * (c + 1), :, y, :],
                                 d["x"][:, c, PATCH * y:PATCH * (y + 1), :].rearrange("b r q -> r b q")
                                 ).then_inc(image_in, 16)
            for dst, src in to_turn:
                sp.dma_start(dst, src).then_inc(to_turn_in, 16)
            for dst, src in to_narrow:
                sp.dma_start(dst, src).then_inc(to_narrow_in, 16)
            for dst, src in direct:
                sp.dma_start(dst, src).then_inc(loaded_s, 16)
            sp.wait_ge(loaded_s, 16 * len(direct))

        @block.gpsimd
        def _(pool):
            for t in zero:
                pool.memset(t[:], 0.0).then_inc(zeroed, 1)
            for i, (t, value) in enumerate(rest):
                pool.wait_ge(zeroed, len(zero) + i)
                pool.memset(t, value).then_inc(zeroed, 1)
            pool.wait_ge(zeroed, len(zero) + len(rest))
            for dst, src in sparse:
                pool.dma_start(dst, src).then_inc(loaded_p, 16)
            pool.wait_ge(loaded_p, 16 * len(sparse))

        @block.tensor
        def _(pe):
            pe.wait_ge(tok_in, 16 * len(embedding))
            for k in range(PATCH):
                last = pe.transpose(w.psum[6 + k // 8][0:IMG_C * PATCH, (k % 8) * D:(k % 8 + 1) * D],
                                    n_tok[:, :, :, k].rearrange("p c r -> p (c r)"), w.ident[0:D, 0:D])
                if k % 8 == 7:
                    last.then_inc(tok_turned, 1)
            pe.wait_ge(tok_copied, 2)
            pe.wait_ge(image_in, 16 * IMG_C * GRID)
            for k in range(PATCH):
                last = pe.matmul(w.psum[0][0:D, 0:B * N_IMG], tokT[:, k, :], image[:, :, :, k::PATCH],
                                 start=(k == 0), stop=(k == PATCH - 1))
            last.then_inc(tok_ps, 1)
            pe.wait_ge(feat_ready, 1)
            pe.wait_ge(zeroed, len(zero) + len(rest))
            for b in range(B):
                o = w.psum[1][0:N_IMG, b * D:(b + 1) * D]
                pe.matmul(o, img_featT[:, b, :], w.ident[0:D, 0:D], start=True, stop=False)
                last = pe.matmul(o, w.ones_row[:, 0:N_IMG], tok_b[:, :], start=False, stop=True)
            last.then_inc(img_turned, 1)
            pe.wait_ge(img_ready, 1)
            pe.wait_ge(to_turn_in, 16 * len(to_turn))
            for i, four in enumerate(fours):
                if i == n_plain:
                    pe.wait_ge(loaded_p, 16 * len(sparse))
                if i >= 6:
                    pe.wait_ge(copied_v if i % 2 == 0 else copied_a, (i - 6) // 2 + 1)
                for j, (src, _) in enumerate(four):
                    r, c = src.shape
                    last = pe.transpose(slot(i, j, c, r), src, w.ident[0:r, 0:r])
                last.then_inc(turned, 1)
            pe.wait_ge(copied_v, (len(fours) + 1) // 2)
            pe.wait_ge(copied_a, len(fours) // 2)
            all_loaded(pe)
            for i, (vT, wo) in enumerate(((a1_WvT, a1_Wo), (a3_WvT, a3_Wo))):
                rows = vT.shape[2]
                for hd in range(8):
                    at = slice(64 * (hd % 2), 64 * (hd % 2) + 64)
                    last = pe.matmul(w.psum[2 * i + hd % 2][0:rows, hd // 2 * D:(hd // 2 + 1) * D], vT[at, hd // 2, :],
                                     wo[at, hd // 2, :], start=True, stop=True)
                last.then_inc(vo_done, 1)

        @block.vector
        def _(dve):
            for i in range(2):
                dve.wait_ge(tok_turned, i + 1)
                dve.tensor_copy(tokT[:, 8 * i:8 * i + 8, :], w.psum[6 + i][0:IMG_C * PATCH, :].rearrange(
                    "p (k n) -> p k n", k=8)).then_inc(tok_copied, 1)
            dve.wait_ge(tok_ps, 1)
            dve.tensor_copy(img_featT[:, :, :], w.psum[0][0:D, 0:B * N_IMG].rearrange("p (b t) -> p b t", b=B)
                            ).then_inc(feat_ready, 1)
            dve.wait_ge(img_turned, 1)
            dve.tensor_copy(w.img_tok[:, :, :], w.psum[1][0:N_IMG, :].rearrange("p (b n) -> p b n", b=B)
                            ).then_inc(img_ready, 1)
            for i in range(0, len(fours), 2):
                dve.wait_ge(turned, i + 1)
                for j, (src, dst) in enumerate(fours[i]):
                    r, c = src.shape
                    if 4 * i + j == XP:
                        dve.tensor_copy(w.xp_dtT[:, :], slot(i, j, c, r)[:, 0:DTR])
                        ins = dve.tensor_copy(w.xp_bcT[:, :, :], each(slot(i, j, c, r)[:, DTR:r], 3))
                    else:
                        ins = dve.tensor_copy(dst, slot(i, j, c, r))
                ins.then_inc(copied_v, 1)
            dve.wait_ge(copied_v, (len(fours) + 1) // 2)
            dve.wait_ge(copied_a, len(fours) // 2)
            all_loaded(dve)
            for i, t in enumerate((w.a2_kT, w.a2_vT)):
                dve.tensor_reduce(mean_k[:, i, :], t[:, :, :], X, ALU.add).then_inc(centred, 1)
            for i, t in enumerate((w.a2_kT, w.a2_vT)):
                dve.wait_ge(centred, i + 1)
                dve.scalar_tensor_tensor(out=t[:, :, :], in0=wide(mean_k[:, i, :], D), scalar=1.0 / D,
                                         in1=t[:, :, :], op0=ALU.mult, op1=ALU.subtract, reverse1=True)
            dve.tensor_scalar(w.inT[:, DI:2 * DI], w.inT[:, DI:2 * DI], 0.5, None, ALU.mult)
            dve.tensor_scalar(w.conv_w[:, :], w.conv_w[:, :], 0.5, None, ALU.mult)
            dve.tensor_scalar(w.conv_b[:, :], w.conv_b[:, :], 0.5, None, ALU.mult)
            f1_q = w.f1_qkT[:, :, :].rearrange("p n (r c) -> p n r c", c=32)[:, :, :, 0:16]
            f2_q = w.f2_qkT[:, :, :].rearrange("p n (r c) -> p n r c", c=32)[:, :, :, 0:16]
            f2_k = w.f2_qkT[:, :, :].rearrange("p n (r c) -> p n r c", c=32)[:, :, :, 16:32]
            dve.tensor_scalar(f1_q, f1_q, 4.0, None, ALU.mult)
            dve.tensor_scalar(f2_q, f2_q, w.f2_ln1[:, 0:1], 0.25, ALU.mult, ALU.mult)
            dve.tensor_scalar(f2_k, f2_k, w.f2_ln1[:, 0:1], None, ALU.mult)
            dve.tensor_scalar(w.f2_vT[:, :], w.f2_vT[:, :], w.f2_ln1[:, 0:1], None, ALU.mult)
            for t in (w.f2_w1T, w.f2_w3T):
                dve.tensor_scalar(t[:, :], t[:, :], w.f2_ln2[:, 0:1], None, ALU.mult)
            dve.tensor_scalar(w.f2_routerT[:, :], w.f2_routerT[:, :], w.f2_ln2[:, 0:1], None, ALU.mult)
            for p in range(2):
                if p:
                    dve.wait_ge(bias_split, 2)
                dve.tensor_copy(bias_high[:, :, :], n_bias[:, :, :]).then_inc(bias_split, 1)
                dve.wait_ge(bias_split, 2 * p + 1)
                dve.scalar_tensor_tensor(out=n_bias[:, :, :], in0=bias_high[:, :, :], scalar=less[:, p:p + 1],
                                         in1=n_bias[:, :, :], op0=ALU.mult, op1=ALU.add).then_inc(bias_split, 1)
            dve.wait_ge(bias_split, 4)
            dve.tensor_copy(w.bias3[:, :, :], n_bias[:, :, :])
            dve.wait_ge(decay_exp, 1)
            dve.tensor_scalar(w.A[:, :], a_pos[:, :], -1.0, None, ALU.mult)
            dve.wait_ge(vo_done, 2)
            for i, (t, rows) in enumerate(((w.a1_Wvo, D), (w.a3_Wvo, D + 1))):
                for odd in range(2):
                    dve.tensor_copy(t[:, odd:8:2, :], w.psum[2 * i + odd][0:rows, 0:4 * D].rearrange(
                        "p (h n) -> p h n", h=4))

        @block.scalar
        def _(act):
            for i in range(1, len(fours), 2):
                act.wait_ge(turned, i + 1)
                for j, (src, dst) in enumerate(fours[i]):
                    r, c = src.shape
                    ins = act.activation(dst, slot(i, j, c, r), ACT.Copy)
                ins.then_inc(copied_a, 1)
            act.wait_ge(to_narrow_in, 16 * len(to_narrow))
            act.wait_ge(tok_in, 16 * len(embedding))
            for dst, src in ((w.sel_bc[:, :, :], n_sel_bc[:, :, :]), (w.sel_expert[:, :], n_sel_expert[:, :]),
                             (w.maskT[:, :], n_maskT[:, :]), (w.maskQ[:, :], n_maskQ[:, :]),
                             (w.ident_b[:, :], w.ident[0:TP, 0:TP])):
                act.activation(dst, src, ACT.Copy)
            all_loaded(act)
            act.activation(a_pos[:, :], w.A[:, :], ACT.Exp).then_inc(decay_exp, 1)

        return sems


def wait_back(steps, eng, back):
    eng.wait_ge(steps.sem, steps.n - back)


def normalize(dve, steps, groups, eps, var_ready, rstd_ready, base, centre=True, ready=None):
    back = len(groups) - 1
    f = groups[0][0].shape[2]
    if centre:
        for src, dst, squares, sums in groups:
            steps.did(dve.tensor_reduce(sums, src, X, ALU.add))
        for src, dst, squares, sums in groups:
            wait_back(steps, dve, back)
            steps.did(dve.scalar_tensor_tensor(out=dst, in0=wide(sums, f), scalar=1.0 / f, in1=src,
                                               op0=ALU.mult, op1=ALU.subtract, reverse1=True))
    for src, dst, squares, sums in groups:
        if centre:
            wait_back(steps, dve, back)
        x = dst if centre else src
        steps.did(dve.tensor_tensor(squares, x, x, ALU.mult))
    for src, dst, squares, sums in groups:
        wait_back(steps, dve, back)
        steps.did(dve.tensor_reduce(sums, squares, X, ALU.add))
    for i, (src, dst, squares, sums) in enumerate(groups):
        wait_back(steps, dve, back - i)
        dve.tensor_scalar(sums, sums, 1.0 / f, eps, ALU.mult, ALU.add).then_inc(var_ready, 1)
    for i, (src, dst, squares, sums) in enumerate(groups):
        dve.wait_ge(rstd_ready, base + i + 1)
        ins = dve.tensor_tensor(dst, dst if centre else src, wide(sums, f), ALU.mult)
        if ready is None:
            steps.did(ins)
        else:
            ins.then_inc(ready, 1)


def roots(pool, w, all_sums, var_ready, rstd_ready, base):
    for i, sums in enumerate(all_sums):
        pool.wait_ge(var_ready, base + i + 1)
        half = w.neg_half[0:sums.shape[0], 0:sums.shape[1]]
        pool.tensor_tensor(sums, sums, half, ALU.pow).then_inc(rstd_ready, 1)


def tiles(t, g):
    return t[:, g * U:(g + 1) * U, :]


def turn_tokens(pe, w, bank, src):
    f = src.shape[2]
    for u in range(U):
        last = pe.transpose(w.psum[bank][0:f, u * TP:(u + 1) * TP], src[:, u, :], w.ident[0:TP, 0:TP])
    return last


def tok(nc, d, w, p):
    NB = G * GROUPS
    with ExitStack() as ctx:
        text_in, placed = ctx.enter_context(nc.semaphore("text_in")), ctx.enter_context(nc.semaphore("placed"))
        block = ctx.enter_context(nc.Block())

        @block.sync
        def _(sp):
            txt = d["txt"][bass.ds(p * NB, NB)]
            sp.dma_start(w.h[N_IMG:TP, 0:2 * NB:2, :], txt[:, 0:TP - N_IMG].rearrange("b t k -> t b k")
                         ).then_inc(text_in, 16)
            sp.dma_start(w.h[:, 1:2 * NB:2, :], txt[:, TP - N_IMG:N_TXT].rearrange("b t k -> t b k")
                         ).then_inc(text_in, 16)
            sp.wait_ge(text_in, 32)

        @block.vector
        def _(dve):
            dve.tensor_copy(w.h[0:N_IMG, 0:2 * NB:2, :], w.img_tok[:, bass.ds(p * NB, NB), :]).then_inc(placed, 1)
            dve.wait_ge(placed, 1)

        return text_in, placed


def mamba(nc, d, w):
    Q = NST * GROUPS
    with ExitStack() as ctx:
        def sb(name, shape, dt=F32):
            return ctx.enter_context(nc.sbuf_tensor(name, shape, dt))

        sems = []

        def sem(name):
            sems.append(ctx.enter_context(nc.semaphore(name)))
            return sems[-1]

        NT = GROUPS * U
        squares = sb("squares", [TP, NT, D])
        sums = sb("sums", [TP, NT])
        xi_pad = sb("xi_pad", [DI, GROUPS, G, DCONV - 1 + SEQ])
        conv = sb("conv", [DI, GROUPS, G, SEQ])
        xi = sb("xi", [DI, GROUPS, COLS])
        gate = sb("gate", [DI, GROUPS, COLS])
        dt_low = sb("dt_low", [DTR, GROUPS, COLS])
        expo = sb("expo", [DI, GROUPS, COLS])
        rest = sb("rest", [DI, GROUPS, COLS])
        dt = sb("dt", [DI, GROUPS, COLS])
        dtx = sb("dtx", [DI, GROUPS, COLS])
        bc_parts = sb("bc_parts", [96, GROUPS, COLS], BF16)
        bc_rest = sb("bc_rest", [96, GROUPS, COLS])
        bc_mid = sb("bc_mid", [96, GROUPS, COLS], BF16)
        decay = sb("decay", [DI, 4, G, SEQ])
        spread_b = sb("spread_b", [DI, 3, COLS])
        drive = sb("drive", [DI, 3, G, SEQ])
        state = sb("state", [DI, 3, G, SEQ])
        prod = sb("prod", [DI, 3, COLS])
        y = sb("y", [DI, GROUPS, COLS])
        mix = sb("mix", [TP, NT, D])
        hid = sb("hid", [128, GROUPS, 2, COLS])
        ffn = sb("ffn", [TP, NT, D])

        v_step, a_step = Steps(sem("v_step")), Steps(sem("a_step"))
        var_ready, rstd_ready, xn_ready, turned, xT_ready = map(sem, ("var", "rstd", "xn_ready", "turned", "xT_ready"))
        xz_ps, pad_ready, gate_ready, conv_ready, xi_ready = map(
            sem, ("xz", "pad_ready", "gate_ready", "conv_ready", "xi_ready"))
        bcd_ps, low_ready, dt_ps, soft_ready, dt_ready, parts_ready = map(
            sem, ("bcd", "low_ready", "dt_ps", "soft_ready", "dt_ready", "parts_ready"))
        b_ps, c_ps, decay_ready, drive_ready, scanned, prod_ready, y_sum = map(
            sem, ("b_ps", "c_ps", "decay_ready", "drive_ready", "scanned", "prod_ready", "y_sum"))
        y_ready, mix_ps, mixed, y_turned, yT_ready, fc1_ps, hid_ready, fc2_ps, ffn_ready = map(
            sem, ("y_ready", "mix_ps", "mixed", "y_turned", "yT_ready", "fc1_ps", "hid_ready", "fc2_ps", "ffn_ready"))
        zero_ready, tanh_ready, xt_ready, dtx_ready, b_ready = map(
            sem, ("zero_ready", "tanh_ready", "xt_ready", "dtx_ready", "b_ready"))
        block = ctx.enter_context(nc.Block())
        ps = w.psum

        @block.gpsimd
        def _(pool):
            pool.memset(xi_pad[:, :, :, 0:DCONV - 1], 0.0).then_inc(zero_ready, 1)
            pool.memset(decay[:, :, :, 0:1], 0.0).then_inc(zero_ready, 1)
            pool.wait_ge(zero_ready, 2)
            def norm_roots(i):
                roots(pool, w, [sums[:, g * U:(g + 1) * U] for g in range(GROUPS)], var_ready, rstd_ready, i * GROUPS)

            norm_roots(0)
            for q in range(Q):
                pool.wait_ge(dtx_ready, q % GROUPS + 1 if q < GROUPS else GROUPS)
                pool.wait_ge(b_ready, q + 1)
                if q >= 3:
                    pool.wait_ge(scanned, G * (q - 2))
                pool.tensor_tensor(drive[:, q % 3, :, :].rearrange("p b t -> p (b t)"), spread_b[:, q % 3, :],
                                   dtx[:, q % GROUPS, :], ALU.mult).then_inc(drive_ready, 1)
            norm_roots(1)
            norm_roots(2)

        @block.tensor
        def _(pe):
            for g in range(GROUPS):
                pe.wait_ge(xn_ready, g + 1)
                turn_tokens(pe, w, g, tiles(w.xn, g)).then_inc(turned, 1)
            for g in range(GROUPS):
                pe.wait_ge(xT_ready, g + 1)
                for c in range(2):
                    pe.matmul(ps[2 + 2 * g + c][:, 0:COLS], w.inT[:, c * DI:(c + 1) * DI], w.xT[:, g, :],
                              start=True, stop=True).then_inc(xz_ps, 1)
            for g in range(GROUPS):
                pe.wait_ge(xi_ready, g + 1)
                pe.matmul(ps[g][0:96, 0:COLS], w.xp_bcT[:, :, :].rearrange("p a b -> p (a b)"), xi[:, g, :],
                          start=True, stop=True)
                pe.matmul(ps[6 + g][0:DTR, 0:COLS], w.xp_dtT[:, :], xi[:, g, :], start=True, stop=True
                          ).then_inc(bcd_ps, 1)
            for g in range(GROUPS):
                pe.wait_ge(low_ready, g + 1)
                pe.matmul(ps[2 + g][:, 0:COLS], w.dtT[:, :], dt_low[:, g, :], start=True, stop=True
                          ).then_inc(dt_ps, 1)

            def product_b(q):
                if q >= 3:
                    pe.wait_ge(b_ready, q - 2)
                pe.matmul(ps[2 + q % 3][:, 0:COLS], w.sel_bc[:, q // GROUPS, :], bc_parts[:, q % GROUPS, :],
                          start=True, stop=True).then_inc(b_ps, 1)

            def product_c(q):
                if q >= 3:
                    pe.wait_ge(prod_ready, q - 2)
                pe.matmul(ps[5 + q % 3][:, 0:COLS], w.sel_bc[:, NST + q // GROUPS, :], bc_parts[:, q % GROUPS, :],
                          start=True, stop=True).then_inc(c_ps, 1)

            pe.wait_ge(parts_ready, GROUPS)
            pe.wait_ge(gate_ready, GROUPS)
            pe.wait_ge(soft_ready, 2 * GROUPS)
            for q in range(3):
                product_b(q)
            product_c(0)
            for t in range(Q + 2):
                if t + 3 < Q:
                    product_b(t + 3)
                if t + 1 < Q:
                    product_c(t + 1)
                if t >= 2:
                    q = t - 2
                    pe.wait_ge(prod_ready, q + 1)
                    pe.matmul(ps[q % GROUPS][:, 0:COLS], w.ident[:, :], prod[:, q % 3, :], start=(q < GROUPS),
                              stop=(q >= Q - GROUPS)).then_inc(y_sum, 1)
            for g in range(GROUPS):
                pe.wait_ge(y_ready, g + 1)
                for u in range(U):
                    o = ps[2 + g][0:TP, u * D:(u + 1) * D]
                    pe.matmul(o, w.ones_row[:, 0:TP], w.out_b[:, :], start=True, stop=False)
                    last = pe.matmul(o, y[:, g, u * TP:(u + 1) * TP], w.outT[:, :], start=False, stop=True)
                last.then_inc(mix_ps, 1)
            for g in range(GROUPS):
                pe.wait_ge(mixed, g + 1)
                turn_tokens(pe, w, 4 + g, tiles(mix, g)).then_inc(y_turned, 1)
            for g in range(GROUPS):
                pe.wait_ge(yT_ready, g + 1)
                for c in range(2):
                    pe.matmul(ps[[0, 1, 6, 7][2 * g + c]][:, 0:COLS], w.fc1T[:, c * 128:(c + 1) * 128], w.xT[:, g, :],
                              start=True, stop=True).then_inc(fc1_ps, 1)
            for g in range(GROUPS):
                pe.wait_ge(hid_ready, 2 * g + 2)
                for u in range(U):
                    o = ps[2 + g][0:TP, u * D:(u + 1) * D]
                    for c in range(2):
                        pe.matmul(o, hid[:, g, c, u * TP:(u + 1) * TP], w.fc2T[:, c, :], start=(c == 0), stop=False)
                    last = pe.matmul(o, w.ones_row[:, 0:TP], w.fc2_b[:, :], start=False, stop=True)
                last.then_inc(fc2_ps, 1)

        @block.scalar
        def _(act):
            act.preload_act_table(ACT.Tanh)
            for g in range(GROUPS):
                act.wait_ge(turned, g + 1)
                act.activation(w.xT[0:D, g, :], ps[g][0:D, 0:COLS], ACT.Copy).then_inc(xT_ready, 1)
            for g in range(GROUPS):
                act.wait_ge(xz_ps, 2 * g + 1)
                act.activation(xi_pad[:, g, :, DCONV - 1:], ps[2 + 2 * g][:, 0:COLS].rearrange("p (b t) -> p b t", b=G),
                               ACT.Copy).then_inc(pad_ready, 1)
                act.wait_ge(xz_ps, 2 * g + 2)
                act.activation(gate[:, g, :], ps[3 + 2 * g][:, 0:COLS], ACT.Tanh).then_inc(tanh_ready, 1)
            for g in range(GROUPS):
                act.wait_ge(conv_ready, g + 1)
                act.activation(xi[:, g, :], conv[:, g, :, :].rearrange("p b t -> p (b t)"), ACT.Tanh
                               ).then_inc(xt_ready, 1)
            for g in range(GROUPS):
                act.wait_ge(bcd_ps, g + 1)
                act.activation(dt_low[:, g, :], ps[6 + g][0:DTR, 0:COLS], ACT.Copy).then_inc(low_ready, 1)
            act.preload_act_table_set("natural_log_exp_and_others")
            for g in range(GROUPS):
                act.wait_ge(dt_ps, g + 1)
                a_step.did(act.activation(expo[:, g, :], ps[2 + g][:, 0:COLS], ACT.Abs, bias=w.dt_b[:, 0:1]))
                act.activation(rest[:, g, :], ps[2 + g][:, 0:COLS], ACT.Relu, bias=w.dt_b[:, 0:1]).then_inc(soft_ready, 1)
            for g in range(GROUPS):
                wait_back(a_step, act, GROUPS - 1)
                a_step.did(act.activation(expo[:, g, :], expo[:, g, :], ACT.Exp, scale=-1.0))
            for g in range(GROUPS):
                wait_back(a_step, act, GROUPS - 1 - g)
                act.activation(expo[:, g, :], expo[:, g, :], ACT.Ln, bias=1.0).then_inc(soft_ready, 1)
            act.wait_ge(zero_ready, 2)
            for q in range(Q):
                n, g = q // GROUPS, q % GROUPS
                if q < GROUPS:
                    act.wait_ge(dt_ready, g + 1)
                if q >= 4:
                    act.wait_ge(scanned, G * (q - 3))
                act.activation(decay[:, q % 4, :, 1:], dt[:, g, :].rearrange("p (b t) -> p b t", b=G)[:, :, 1:],
                               ACT.Exp, scale=w.A[:, n:n + 1]).then_inc(decay_ready, 1)
                act.wait_ge(b_ps, q + 1)
                if q >= 3:
                    act.wait_ge(drive_ready, q - 2)
                act.activation(spread_b[:, q % 3, :], ps[2 + q % 3][:, 0:COLS], ACT.Copy).then_inc(b_ready, 1)
            for g in range(GROUPS):
                act.wait_ge(y_turned, g + 1)
                act.activation(w.xT[0:D, g, :], ps[4 + g][0:D, 0:COLS], ACT.Copy).then_inc(yT_ready, 1)
            for g in range(GROUPS):
                for c in range(2):
                    act.wait_ge(fc1_ps, 2 * g + c + 1)
                    act.activation(hid[:, g, c, :], ps[[0, 1, 6, 7][2 * g + c]][:, 0:COLS], ACT.Gelu
                                   ).then_inc(hid_ready, 1)
            for g in range(GROUPS):
                act.wait_ge(fc2_ps, g + 1)
                act.activation(tiles(ffn, g), ps[2 + g][0:TP, 0:U * D].rearrange("p (u n) -> p u n", u=U), ACT.Gelu
                               ).then_inc(ffn_ready, 1)

        @block.vector
        def _(dve):
            def norm(src, dst, i, ready=None):
                normalize(dve, v_step, [(tiles(src, g), tiles(dst, g), tiles(squares, g), sums[:, g * U:(g + 1) * U])
                                        for g in range(GROUPS)], 1e-5, var_ready, rstd_ready, i * GROUPS,
                          ready=ready)

            def gains(gain, bias, t, did):
                for g in range(GROUPS):
                    wait_back(v_step, dve, GROUPS - 1)
                    v_step.did(dve.tensor_tensor(tiles(t, g), tiles(t, g), each(gain[:, :], U), ALU.mult))
                for g in range(GROUPS):
                    wait_back(v_step, dve, GROUPS - 1 - g)
                    ins = dve.tensor_tensor(tiles(t, g), tiles(t, g), each(bias[:, :], U), ALU.add)
                    did(ins)

            norm(w.h, w.xn, 0, ready=xn_ready)
            dve.wait_ge(zero_ready, 1)
            for k in range(DCONV):
                for g in range(GROUPS):
                    shifted = xi_pad[:, g, :, k:k + SEQ]
                    if k == 0:
                        dve.wait_ge(pad_ready, g + 1)
                        v_step.did(dve.tensor_scalar(conv[:, g, :, :], shifted, w.conv_w[:, 0:1], w.conv_b[:, 0:1],
                                                     ALU.mult, ALU.add))
                        continue
                    wait_back(v_step, dve, GROUPS - 1 - (g if k == DCONV - 1 else 0))
                    ins = dve.scalar_tensor_tensor(out=conv[:, g, :, :], in0=shifted, scalar=w.conv_w[:, k:k + 1],
                                                   in1=conv[:, g, :, :], op0=ALU.mult, op1=ALU.add)
                    if k < DCONV - 1:
                        v_step.did(ins)
                    else:
                        ins.then_inc(conv_ready, 1)
            for g in range(GROUPS):
                dve.wait_ge(tanh_ready, g + 1)
                dve.scalar_tensor_tensor(out=gate[:, g, :], in0=gate[:, g, :], scalar=1.0, in1=ps[3 + 2 * g][:, 0:COLS],
                                         op0=ALU.add, op1=ALU.mult).then_inc(gate_ready, 1)
            for g in range(GROUPS):
                dve.wait_ge(xt_ready, g + 1)
                dve.scalar_tensor_tensor(out=xi[:, g, :], in0=xi[:, g, :], scalar=1.0,
                                         in1=conv[:, g, :, :].rearrange("p b t -> p (b t)"), op0=ALU.add, op1=ALU.mult
                                         ).then_inc(xi_ready, 1)
            for g in range(GROUPS):
                dve.wait_ge(bcd_ps, g + 1)
                v_step.did(dve.tensor_copy(bc_parts[:, g, :], ps[g][0:96, 0:COLS]))
            for g in range(GROUPS):
                wait_back(v_step, dve, GROUPS - 1)
                v_step.did(dve.tensor_tensor(bc_rest[:, g, :], ps[g][0:96, 0:COLS], bc_parts[:, g, :], ALU.subtract))
            for g in range(GROUPS):
                wait_back(v_step, dve, GROUPS - 1)
                v_step.did(dve.tensor_copy(bc_mid[:, g, :], bc_rest[:, g, :]))
            for g in range(GROUPS):
                wait_back(v_step, dve, GROUPS - 1 - g)
                dve.tensor_copy(bc_parts[32:64, g, :], bc_mid[32:64, g, :])
                dve.tensor_tensor(bc_parts[64:96, g, :], bc_rest[64:96, g, :], bc_mid[64:96, g, :], ALU.subtract
                                  ).then_inc(parts_ready, 1)
            dve.wait_ge(soft_ready, 2 * GROUPS)
            for g in range(GROUPS):
                dve.tensor_tensor(dt[:, g, :], expo[:, g, :], rest[:, g, :], ALU.add).then_inc(dt_ready, 1)
            for g in range(GROUPS):
                dve.wait_ge(dt_ready, g + 1)
                dve.tensor_tensor(dtx[:, g, :], dt[:, g, :], xi[:, g, :], ALU.mult).then_inc(dtx_ready, 1)
            for q in range(Q + 2):
                if 1 <= q <= Q:
                    s = q - 1
                    dve.wait_ge(decay_ready, s + 1)
                    dve.wait_ge(drive_ready, s + 1)
                    if s >= 3:
                        dve.wait_ge(prod_ready, s - 2)
                    for b in range(G):
                        dve.tensor_tensor_scan(state[:, s % 3, b, :], decay[:, s % 4, b, :], drive[:, s % 3, b, :],
                                               0.0, ALU.mult, ALU.add).then_inc(scanned, 1)
                if q >= 2:
                    s = q - 2
                    dve.wait_ge(scanned, G * (s + 1))
                    dve.wait_ge(c_ps, s + 1)
                    if s >= 3:
                        dve.wait_ge(y_sum, s - 2)
                    dve.tensor_tensor(prod[:, s % 3, :], ps[5 + s % 3][:, 0:COLS],
                                      state[:, s % 3, :, :].rearrange("p b t -> p (b t)"), ALU.mult
                                      ).then_inc(prod_ready, 1)
            for g in range(GROUPS):
                dve.wait_ge(y_sum, Q - GROUPS + g + 1)
                v_step.did(dve.scalar_tensor_tensor(out=y[:, g, :], in0=xi[:, g, :], scalar=w.D_ssm[:, 0:1],
                                                    in1=ps[g][:, 0:COLS], op0=ALU.mult, op1=ALU.add))
            dve.wait_ge(gate_ready, GROUPS)
            for g in range(GROUPS):
                wait_back(v_step, dve, GROUPS - 1 - g)
                dve.tensor_tensor(y[:, g, :], y[:, g, :], gate[:, g, :], ALU.mult).then_inc(y_ready, 1)
            for g in range(GROUPS):
                dve.wait_ge(mix_ps, g + 1)
                dve.wait_ge(xn_ready, g + 1)
                v_step.did(dve.tensor_tensor(tiles(w.xn, g), tiles(w.xn, g), ps[2 + g][0:TP, 0:U * D].rearrange(
                    "p (u n) -> p u n", u=U), ALU.add))
            v_step.wait(dve)
            norm(w.xn, mix, 1)
            gains(w.m_ln1_g, w.m_ln1_b, mix, lambda ins: ins.then_inc(mixed, 1))
            dve.wait_ge(mixed, GROUPS)
            for g in range(GROUPS):
                dve.wait_ge(ffn_ready, g + 1)
                v_step.did(dve.tensor_tensor(tiles(w.xn, g), tiles(mix, g), tiles(ffn, g), ALU.add))
            v_step.wait(dve)
            norm(w.xn, w.xn, 2)
            gains(w.m_ln2_g, w.m_ln2_b, w.xn, v_step.did)
            v_step.wait(dve)
            for g in range(GROUPS):
                v_step.did(dve.tensor_tensor(tiles(w.h, g), tiles(w.h, g), tiles(w.xn, g), ALU.add))
            v_step.wait(dve)

        return sems


def layer_memory(nc, ctx, layer):
    sems = []

    def sb(name, shape, dt=F32):
        return ctx.enter_context(nc.sbuf_tensor(f"{layer}_{name}", shape, dt))

    def sem(*names):
        new = [ctx.enter_context(nc.semaphore(f"{layer}_{n}")) for n in names]
        sems.extend(new)
        return new if len(new) > 1 else new[0]

    return sb, sem, sems


def per_group(*tensors):
    return [tuple(t[:, g * U:(g + 1) * U] if len(t.shape) == 2 else tiles(t, g) for t in tensors)
            for g in range(GROUPS)]


def find_first(dve, steps, code, code_max, hot, at_max):
    for g in range(GROUPS):
        wait_back(steps, dve, GROUPS - 1)
        steps.did(at_max(g))
    for g in range(GROUPS):
        wait_back(steps, dve, GROUPS - 1)
        steps.did(dve.tensor_reduce(code_max[g], code[g], X, ALU.max))
    for g in range(GROUPS):
        wait_back(steps, dve, GROUPS - 1)
        steps.did(dve.tensor_tensor(hot[g], code[g], wide(code_max[g], 8), ALU.is_equal))


def combine(dve, w, steps, gates, prod, y_ps, y_read, summed, banks):
    NT = GROUPS * U
    for i in range(NT + 1):
        if i < NT:
            dve.wait_ge(y_ps, i + 1)
            if i >= 2:
                dve.wait_ge(summed, i - 1)
            dve.tensor_tensor(prod[:, i % 2, :, :], w.psum[banks[i % len(banks)]][0:TP, :].rearrange(
                "p (e n) -> p e n", e=8), wide(gates[:, i, :], D), ALU.mult).then_inc(y_read, 1)
        if i >= 1:
            dve.wait_ge(y_read, i)
            dve.tensor_reduce(w.xn[:, i - 1, :], prod[:, (i - 1) % 2, :, :].rearrange("p e n -> p n e"), X, ALU.add
                              ).then_inc(summed, 1)
    for g in range(GROUPS):
        dve.wait_ge(summed, (g + 1) * U)
        steps.did(dve.tensor_tensor(tiles(w.h, g), tiles(w.h, g), tiles(w.xn, g), ALU.add))
    steps.wait(dve)


def ffn0(nc, d, w):
    NT = GROUPS * U
    with ExitStack() as ctx:
        sb, sem, sems = layer_memory(nc, ctx, "ffn0")
        squares, sums = sb("squares", [TP, NT, D]), sb("sums", [TP, NT])
        hid = sb("hid", [128, GROUPS, 2, COLS])
        best, code_max, total = sb("best", [TP, NT]), sb("code_max", [TP, NT]), sb("total", [TP, NT])
        z, code, hot, ex = (sb(n, [TP, NT, 8]) for n in ("z", "code", "hot", "ex"))
        prod = sb("prod", [TP, 2, 8, D])
        v_step = Steps(sem("v_step"))
        var_ready, rstd_ready, xn_ready, turned, xT_ready = sem("var", "rstd", "xn_ready", "turned", "xT_ready")
        h_ps, hid_ready, logit_ps, z_ready, ex_ready, y_ps, y_read, summed = sem(
            "h_ps", "hid_ready", "logit_ps", "z_ready", "ex_ready", "y_ps", "y_read", "summed")
        block = ctx.enter_context(nc.Block())
        ps = w.psum
        Y_BANKS = (4, 5, 6, 7)

        @block.gpsimd
        def _(pool):
            roots(pool, w, [s for s, in per_group(sums)], var_ready, rstd_ready, 0)

        @block.tensor
        def _(pe):
            for g in range(GROUPS):
                pe.wait_ge(xn_ready, g + 1)
                turn_tokens(pe, w, g, tiles(w.xn, g)).then_inc(turned, 1)
            for g in range(GROUPS):
                pe.wait_ge(xT_ready, g + 1)
                for c in range(2):
                    pe.matmul(ps[2 + 2 * g + c][:, 0:COLS], w.f0_W1[:, c * 128:(c + 1) * 128], w.xT[:, g, :],
                              start=True, stop=True).then_inc(h_ps, 1)
            for g in range(GROUPS):
                pe.wait_ge(hid_ready, 2 * g + 2)
                for u in range(U):
                    o = ps[g][0:TP, u * 8:(u + 1) * 8]
                    for c in range(2):
                        pe.matmul(o, hid[:, g, c, u * TP:(u + 1) * TP], w.f0_Wg[:, c, :], start=(c == 0), stop=False)
                    last = pe.matmul(o, w.ones_row[:, 0:TP], w.f0_bg[:, :], start=False, stop=True)
                last.then_inc(logit_ps, 1)
            for i in range(NT):
                g, u = i // U, i % U
                if i >= 4:
                    pe.wait_ge(y_read, i - 3)
                o = ps[Y_BANKS[i % 4]][0:TP, :]
                for c in range(2):
                    pe.matmul(o, hid[:, g, c, u * TP:(u + 1) * TP], w.f0_Wd[:, c, :, :].rearrange("p e n -> p (e n)"),
                              start=(c == 0), stop=False)
                pe.matmul(o, w.ones3[:, 0:TP], w.bias3[:, 0, :], start=False, stop=True
                          ).then_inc(y_ps, 1)

        @block.scalar
        def _(act):
            act.preload_act_table(ACT.Gelu)
            for g in range(GROUPS):
                act.wait_ge(turned, g + 1)
                act.activation(w.xT[0:D, g, :], ps[g][0:D, 0:COLS], ACT.Copy).then_inc(xT_ready, 1)
            for g in range(GROUPS):
                for c in range(2):
                    act.wait_ge(h_ps, 2 * g + c + 1)
                    act.activation(hid[:, g, c, :], ps[2 + 2 * g + c][:, 0:COLS], ACT.Gelu).then_inc(hid_ready, 1)
            for g in range(GROUPS):
                act.wait_ge(z_ready, g + 1)
                act.activation(tiles(ex, g), tiles(z, g), ACT.Exp).then_inc(ex_ready, 1)

        @block.vector
        def _(dve):
            normalize(dve, v_step, per_group(w.h, w.xn, squares, sums), 1e-5, var_ready, rstd_ready, 0, ready=xn_ready)
            for g in range(GROUPS):
                dve.wait_ge(logit_ps, g + 1)
                logits = ps[g][0:TP, 0:U * 8].rearrange("p (u e) -> p u e", u=U)
                v_step.did(dve.tensor_reduce(best[:, g * U:(g + 1) * U], logits, X, ALU.max))
            for g in range(GROUPS):
                wait_back(v_step, dve, GROUPS - 1 - g)
                logits = ps[g][0:TP, 0:U * 8].rearrange("p (u e) -> p u e", u=U)
                dve.tensor_tensor(tiles(z, g), logits, wide(best[:, g * U:(g + 1) * U], 8), ALU.subtract
                                  ).then_inc(z_ready, 1)
            dve.wait_ge(z_ready, GROUPS)
            rank = each(w.rank[:, :], U)
            codes, hots = [tiles(code, g) for g in range(GROUPS)], [tiles(hot, g) for g in range(GROUPS)]
            find_first(dve, v_step, codes, [m for m, in per_group(code_max)], hots,
                       lambda g: dve.scalar_tensor_tensor(out=codes[g], in0=tiles(z, g), scalar=0.0, in1=rank,
                                                          op0=ALU.is_ge, op1=ALU.mult))
            for g in range(GROUPS):
                dve.wait_ge(ex_ready, g + 1)
                v_step.did(dve.tensor_reduce(total[:, g * U:(g + 1) * U], tiles(ex, g), X, ALU.add))
            for g in range(GROUPS):
                wait_back(v_step, dve, GROUPS - 1)
                v_step.did(dve.reciprocal(total[:, g * U:(g + 1) * U], total[:, g * U:(g + 1) * U]))
            for g in range(GROUPS):
                v_step.did(dve.tensor_tensor(hots[g], hots[g], tiles(ex, g), ALU.mult))
            for g in range(GROUPS):
                wait_back(v_step, dve, GROUPS - 1)
                v_step.did(dve.tensor_tensor(hots[g], hots[g], wide(total[:, g * U:(g + 1) * U], 8), ALU.mult))
            v_step.wait(dve)
            combine(dve, w, v_step, hot, prod, y_ps, y_read, summed, Y_BANKS)

        return sems


def ffn3(nc, d, w):
    NT = GROUPS * U
    with ExitStack() as ctx:
        sb, sem, sems = layer_memory(nc, ctx, "ffn3")
        squares, sums = sb("squares", [TP, NT, D]), sb("sums", [TP, NT])
        hid = sb("hid", [128, 8, GROUPS, COLS])
        best, code_max, total = sb("best", [TP, NT]), sb("code_max", [TP, NT]), sb("total", [TP, NT])
        z, z2, code, hot, hot2, ex = (sb(n, [TP, NT, 8]) for n in ("z", "z2", "code", "hot", "hot2", "ex"))
        prod = sb("prod", [TP, 2, 8, D])
        v_step = Steps(sem("v_step"))
        var_ready, rstd_ready, xn_ready, turned, xT_ready = sem("var", "rstd", "xn_ready", "turned", "xT_ready")
        h_ps, hid_ready, logit_ps, z_ready, ex_ready, y_ps, y_read, summed = sem(
            "h_ps", "hid_ready", "logit_ps", "z_ready", "ex_ready", "y_ps", "y_read", "summed")
        block = ctx.enter_context(nc.Block())
        ps = w.psum
        Y_BANKS = (6, 7)

        @block.gpsimd
        def _(pool):
            for i in range(2):
                roots(pool, w, [s for s, in per_group(sums)], var_ready, rstd_ready, i * GROUPS)

        @block.tensor
        def _(pe):
            for g in range(GROUPS):
                pe.wait_ge(xn_ready, g + 1)
                turn_tokens(pe, w, g, tiles(w.xn, g)).then_inc(turned, 1)
            for g in range(GROUPS):
                pe.wait_ge(xT_ready, g + 1)
                for u in range(U):
                    last = pe.matmul(ps[g][0:TP, u * 8:(u + 1) * 8], w.xT[:, g, u * TP:(u + 1) * TP], w.f3_Wr[:, :],
                                     start=True, stop=True)
                last.then_inc(logit_ps, 1)
            for q in range(8 * GROUPS):
                g, e = q // 8, q % 8
                if q >= 4:
                    pe.wait_ge(hid_ready, q - 3)
                pe.matmul(ps[2 + q % 4][:, 0:COLS], w.f3_W1[:, e, :], w.xT[:, g, :], start=True, stop=True
                          ).then_inc(h_ps, 1)
            for i in range(NT):
                g, u = i // U, i % U
                pe.wait_ge(hid_ready, 8 * g + 8)
                if i >= 2:
                    pe.wait_ge(y_read, i - 1)
                o = ps[Y_BANKS[i % 2]]
                pe.matmul(o[0:TP, :], w.ones3[:, 0:TP], w.bias3[:, 1, :], start=True, stop=False)
                for e in range(8):
                    last = pe.matmul(o[0:TP, e * D:(e + 1) * D], hid[:, e, g, u * TP:(u + 1) * TP], w.f3_W2[:, e, :],
                                     start=False, stop=(e == 7))
                last.then_inc(y_ps, 1)

        @block.scalar
        def _(act):
            act.preload_act_table(ACT.Gelu)
            for g in range(GROUPS):
                act.wait_ge(turned, g + 1)
                act.activation(w.xT[0:D, g, :], ps[g][0:D, 0:COLS], ACT.Identity, bias=w.f3_b[:, 0:1],
                               scale=w.f3_g[:, 0:1]).then_inc(xT_ready, 1)
            for q in range(8 * GROUPS):
                g, e = q // 8, q % 8
                act.wait_ge(h_ps, q + 1)
                act.activation(hid[:, e, g, :], ps[2 + q % 4][:, 0:COLS], ACT.Gelu).then_inc(hid_ready, 1)
            for g in range(GROUPS):
                act.wait_ge(z_ready, g + 1)
                act.activation(tiles(ex, g), tiles(z, g), ACT.Exp).then_inc(ex_ready, 1)

        @block.vector
        def _(dve):
            normalize(dve, v_step, per_group(w.h, w.xn, squares, sums), 1e-5, var_ready, rstd_ready, 0)
            v_step.wait(dve)
            normalize(dve, v_step, per_group(w.xn, w.xn, squares, sums), 1e-5, var_ready, rstd_ready, GROUPS,
                      ready=xn_ready)
            for g in range(GROUPS):
                dve.wait_ge(logit_ps, g + 1)
                logits = ps[g][0:TP, 0:U * 8].rearrange("p (u e) -> p u e", u=U)
                v_step.did(dve.tensor_reduce(best[:, g * U:(g + 1) * U], logits, X, ALU.max))
            for g in range(GROUPS):
                wait_back(v_step, dve, GROUPS - 1 - g)
                logits = ps[g][0:TP, 0:U * 8].rearrange("p (u e) -> p u e", u=U)
                dve.tensor_tensor(tiles(z, g), logits, wide(best[:, g * U:(g + 1) * U], 8), ALU.subtract
                                  ).then_inc(z_ready, 1)
            dve.wait_ge(z_ready, GROUPS)
            top_two(dve, v_step, w, z, z2, code, code_max, hot, hot2, best)
            for g in range(GROUPS):
                dve.wait_ge(ex_ready, g + 1)
                wait_back(v_step, dve, GROUPS - 1)
                v_step.did(dve.tensor_tensor(tiles(hot, g), tiles(hot, g), tiles(ex, g), ALU.mult))
            for g in range(GROUPS):
                wait_back(v_step, dve, GROUPS - 1)
                v_step.did(dve.tensor_reduce(total[:, g * U:(g + 1) * U], tiles(hot, g), X, ALU.add))
            for g in range(GROUPS):
                wait_back(v_step, dve, GROUPS - 1)
                v_step.did(dve.reciprocal(total[:, g * U:(g + 1) * U], total[:, g * U:(g + 1) * U]))
            for g in range(GROUPS):
                wait_back(v_step, dve, GROUPS - 1)
                v_step.did(dve.tensor_tensor(tiles(hot, g), tiles(hot, g), wide(total[:, g * U:(g + 1) * U], 8),
                                             ALU.mult))
            v_step.wait(dve)
            combine(dve, w, v_step, hot, prod, y_ps, y_read, summed, Y_BANKS)

        return sems


def top_two(dve, steps, w, z, z2, code, code_max, hot, hot2, best):
    rank = each(w.rank[:, :], U)
    codes = [tiles(code, g) for g in range(GROUPS)]
    maxima = [m for m, in per_group(code_max)]
    find_first(dve, steps, codes, maxima, [tiles(hot, g) for g in range(GROUPS)],
               lambda g: dve.scalar_tensor_tensor(out=codes[g], in0=tiles(z, g), scalar=0.0, in1=rank,
                                                  op0=ALU.is_ge, op1=ALU.mult))
    for g in range(GROUPS):
        wait_back(steps, dve, GROUPS - 1)
        steps.did(dve.scalar_tensor_tensor(out=tiles(z2, g), in0=tiles(hot, g), scalar=NEG, in1=tiles(z, g),
                                           op0=ALU.mult, op1=ALU.add))
    for g in range(GROUPS):
        wait_back(steps, dve, GROUPS - 1)
        steps.did(dve.tensor_reduce(best[:, g * U:(g + 1) * U], tiles(z2, g), X, ALU.max))
    for g in range(GROUPS):
        wait_back(steps, dve, GROUPS - 1)
        steps.did(dve.tensor_tensor(tiles(z2, g), tiles(z2, g), wide(best[:, g * U:(g + 1) * U], 8), ALU.is_ge))
    find_first(dve, steps, codes, maxima, [tiles(hot2, g) for g in range(GROUPS)],
               lambda g: dve.tensor_tensor(codes[g], tiles(z2, g), rank, ALU.mult))
    for g in range(GROUPS):
        wait_back(steps, dve, GROUPS - 1)
        steps.did(dve.tensor_tensor(tiles(hot, g), tiles(hot, g), tiles(hot2, g), ALU.add))


def attn1(nc, d, w):
    NT, NB = GROUPS * U, G * GROUPS
    W3 = 3 * TP
    with ExitStack() as ctx:
        sb, sem, sems = layer_memory(nc, ctx, "attn1")
        squares, sums = sb("squares", [TP, NT, D]), sb("sums", [TP, NT])
        below = sb("below", [128, 4, COLS])
        feat = sb("feat", [128, GROUPS, 4, COLS])
        vals = sb("vals", [TP, NT, 8, D + 1])
        probs = sb("probs", [TP, 2, 4, 2, W3])
        den = sb("den", [TP, 2, 8])
        prod = sb("prod", [TP, 2, 8, D])
        v_step = Steps(sem("v_step"))
        var_ready, rstd_ready, xn_ready, turned, xT_ready = sem("var", "rstd", "xn_ready", "turned", "xT_ready")
        kq_ps, below_ready, below_exp, feat_ready, v_ps, v_ready, ones_ready = sem(
            "kq_ps", "below_ready", "below_exp", "feat_ready", "v_ps", "v_ready", "ones_ready")
        s_ps, probs_ready, o_ps, o_read, summed = sem("s_ps", "probs_ready", "o_ps", "o_read", "summed")
        block = ctx.enter_context(nc.Block())
        ps = w.psum

        @block.gpsimd
        def _(pool):
            pool.memset(vals[:, :, :, D:D + 1], 1.0).then_inc(ones_ready, 1)
            pool.wait_ge(ones_ready, 1)
            roots(pool, w, [s for s, in per_group(sums)], var_ready, rstd_ready, 0)

        @block.tensor
        def _(pe):
            for g in range(GROUPS):
                pe.wait_ge(xn_ready, g + 1)
                turn_tokens(pe, w, g, tiles(w.xn, g)).then_inc(turned, 1)
            for g in range(GROUPS):
                pe.wait_ge(xT_ready, g + 1)
                if g:
                    pe.wait_ge(feat_ready, 4 * g)
                for c in range(4):
                    wt = (w.a1_Wk, w.a1_Wq)[c // 2][:, 4 * (c % 2):4 * (c % 2) + 4, :]
                    pe.matmul(ps[2 + c][:, 0:COLS], wt.rearrange("p h k -> p (h k)"), w.xT[0:D, g, :],
                              start=True, stop=True).then_inc(kq_ps, 1)
                for u in range(U):
                    i = g * U + u
                    if i >= 2:
                        pe.wait_ge(v_ready, i - 1)
                    pe.matmul(ps[6 + i % 2][0:TP, :], w.xT[0:D, g, u * TP:(u + 1) * TP],
                              w.a1_Wvo[:, :, :].rearrange("p h n -> p (h n)"), start=True, stop=True).then_inc(v_ps, 1)

            def scores(b):
                g, at = b // G, (b % G) * SEQ
                if b:
                    pe.wait_ge(probs_ready, 4 * b)
                for c in range(2):
                    for r in range(4):
                        rows = slice(32 * r, 32 * r + 32)
                        k, q = feat[rows, g, c, at:at + SEQ], feat[rows, g, 2 + c, at:at + SEQ]
                        o = ps[r][0:TP, c * W3:(c + 1) * W3]
                        pe.matmul(o[:, 0:SEQ], k[:, 0:TP], q, start=True, stop=True)
                        last = pe.matmul(o[:, SEQ:W3], k[:, TP:SEQ], q[:, TP:SEQ], start=True, stop=True)
                        if c:
                            last.then_inc(s_ps, 1)

            pe.wait_ge(feat_ready, 4 * GROUPS)
            pe.wait_ge(v_ready, NT)
            pe.wait_ge(xT_ready, GROUPS)
            scores(0)
            for b in range(NB):
                if b + 1 < NB:
                    scores(b + 1)
                pe.wait_ge(probs_ready, 4 * b + 4)
                for t in range(2):
                    if b:
                        pe.wait_ge(o_read, 2 * (b - 1) + t + 1)
                    for hd in range(8):
                        o = ps[4 + 2 * t + hd // 4][0:TP, (hd % 4) * (D + 1):(hd % 4 + 1) * (D + 1)]
                        pr = probs[:, b % 2, hd % 4, hd // 4, :]
                        last = pe.matmul(o, pr[:, t * TP:(t + 1) * TP], vals[:, 2 * b, hd, :], start=True, stop=(t == 0))
                        if t:
                            last = pe.matmul(o, pr[:, SEQ:W3], vals[:, 2 * b + 1, hd, :], start=False, stop=True)
                    last.then_inc(o_ps, 1)

        @block.scalar
        def _(act):
            act.preload_act_table(ACT.Exp)
            for g in range(GROUPS):
                act.wait_ge(turned, g + 1)
                act.activation(w.xT[0:D, g, :], ps[g][0:D, 0:COLS], ACT.Copy).then_inc(xT_ready, 1)
            for g in range(GROUPS):
                for c in range(4):
                    act.wait_ge(kq_ps, 4 * g + c + 1)
                    if g:
                        act.wait_ge(feat_ready, 4 * (g - 1) + c + 1)
                    act.activation(below[:, c, :], ps[2 + c][:, 0:COLS], ACT.Relu, scale=-1.0).then_inc(below_ready, 1)
                for c in range(4):
                    act.wait_ge(below_ready, 4 * g + c + 1)
                    act.activation(below[:, c, :], below[:, c, :], ACT.Exp, scale=-1.0).then_inc(below_exp, 1)
                for u in range(U):
                    i = g * U + u
                    act.wait_ge(v_ps, i + 1)
                    act.activation(vals[:, i, :, 0:D], ps[6 + i % 2][0:TP, :].rearrange("p (h n) -> p h n", h=8),
                                   ACT.Copy).then_inc(v_ready, 1)

        @block.vector
        def _(dve):
            normalize(dve, v_step, per_group(w.h, w.xn, squares, sums), 1e-5, var_ready, rstd_ready, 0, ready=xn_ready)
            for g in range(GROUPS):
                for c in range(4):
                    dve.wait_ge(below_exp, 4 * g + c + 1)
                    dve.scalar_tensor_tensor(out=feat[:, g, c, :], in0=ps[2 + c][:, 0:COLS], scalar=0.0,
                                             in1=below[:, c, :], op0=ALU.max, op1=ALU.add).then_inc(feat_ready, 1)

            def mask(b):
                for r in range(4):
                    dve.wait_ge(s_ps, 4 * b + r + 1)
                    if b >= 2:
                        dve.wait_ge(o_ps, 2 * (b - 1))
                    dve.tensor_tensor(probs[:, b % 2, r, :, :], ps[r][0:TP, 0:2 * W3].rearrange(
                        "p (c n) -> p c n", c=2), each(w.causal01[:, :], 2), ALU.mult).then_inc(probs_ready, 1)

            def finish(b):
                for t in range(2):
                    dve.wait_ge(o_ps, 2 * b + t + 1)
                    both = w.banks[0:TP, 4 + 2 * t:6 + 2 * t, 0:4 * (D + 1)].rearrange("p c (h n) -> p c h n", h=4)
                    v_step.did(dve.tensor_scalar(den[:, t, :].rearrange("p (c h) -> p c h", c=2), both[:, :, :, D],
                                                 1e-9, None, ALU.add))
                for t in range(2):
                    wait_back(v_step, dve, 1)
                    v_step.did(dve.reciprocal(den[:, t, :], den[:, t, :]))
                for t in range(2):
                    wait_back(v_step, dve, 1 - t)
                    if b:
                        dve.wait_ge(summed, 2 * (b - 1) + t + 1)
                    both = w.banks[0:TP, 4 + 2 * t:6 + 2 * t, 0:4 * (D + 1)].rearrange("p c (h n) -> p c h n", h=4)
                    scale = den[:, t, :].rearrange("p (c h) -> p c h", c=2).unsqueeze(3).broadcast_to([TP, 2, 4, D])
                    dve.tensor_tensor(prod[:, t, :, :].rearrange("p (c h) n -> p c h n", c=2), both[:, :, :, 0:D],
                                      scale, ALU.mult).then_inc(o_read, 1)
                for t in range(2):
                    dve.wait_ge(o_read, 2 * b + t + 1)
                    dve.tensor_reduce(w.xn[:, 2 * b + t, :], prod[:, t, :, :].rearrange("p h n -> p n h"), X, ALU.add
                                      ).then_inc(summed, 1)

            mask(0)
            for b in range(NB):
                if b + 1 < NB:
                    mask(b + 1)
                finish(b)
            for g in range(GROUPS):
                dve.wait_ge(summed, (g + 1) * U)
                v_step.did(dve.tensor_tensor(tiles(w.h, g), tiles(w.h, g), tiles(w.xn, g), ALU.add))
            v_step.wait(dve)

        return sems


def attn2(nc, d, w):
    NT, NB = GROUPS * U, G * GROUPS
    with ExitStack() as ctx:
        sb, sem, sems = layer_memory(nc, ctx, "attn2")
        squares, sums = sb("squares", [TP, NT, D]), sb("sums", [TP, NT])
        kv_sq = sb("kv_sq", [TP, 2, 16, D])
        kv_var = sb("kv_var", [TP, 3, 16])
        scale = sb("scale", [TP, 3, 8])
        keys = sb("keys", [TP, NT, 512])
        vals = sb("vals", [TP, NT, 512])
        dots = sb("dots", [128, NB, 4, 128])
        dots_o = sb("dots_o", [128, NB, 4, D])
        v_step = Steps(sem("v_step"))
        var_ready, rstd_ready, xn_ready, turned, xT_ready = sem("var", "rstd", "xn_ready", "turned", "xT_ready")
        kv_ps, sq_ready, k_ready, kv_var_ready, root_ready, v_ready, kv_sum, kv_scaled = sem(
            "kv_ps", "sq_ready", "k_ready", "kv_var_ready", "root_ready", "v_ready", "kv_sum", "kv_scaled")
        zeroed, dots_ps, dots_ready, do_ps, do_ready, m_ps, m_ready, out_ps, out_read = sem(
            "zeroed", "dots_ps", "dots_ready", "do_ps", "do_ready", "m_ps", "m_ready", "out_ps", "out_read")
        block = ctx.enter_context(nc.Block())
        ps = w.psum
        BANKS = (6, 7, 4, 5)

        @block.gpsimd
        def _(pool):
            pool.memset(dots[:], 0.0).then_inc(zeroed, 1)
            pool.wait_ge(zeroed, 1)
            roots(pool, w, [s for s, in per_group(sums)], var_ready, rstd_ready, 0)
            for i in range(NT):
                pool.wait_ge(kv_scaled, i + 1)
                pool.tensor_tensor(scale[:, i % 3, :], scale[:, i % 3, :], w.neg_half[0:TP, 0:8], ALU.pow
                                   ).then_inc(root_ready, 1)

        @block.tensor
        def _(pe):
            for g in range(GROUPS):
                pe.wait_ge(xn_ready, g + 1)
                turn_tokens(pe, w, 6 + g, tiles(w.xn, g)).then_inc(turned, 1)
            for i in range(NT):
                g, u = i // U, i % U
                pe.wait_ge(xT_ready, g + 1)
                if i >= 3:
                    pe.wait_ge(k_ready, i - 2)
                    pe.wait_ge(v_ready, i - 2)
                for c, wt in enumerate((w.a2_kT, w.a2_vT)):
                    pe.matmul(ps[2 * (i % 3) + c][0:TP, :], w.xT[0:D, g, u * TP:(u + 1) * TP],
                              wt[:, :, :].rearrange("p h n -> p (h n)"), start=True, stop=True).then_inc(kv_ps, 1)
            for b in range(NB):
                pe.wait_ge(v_ready, 2 * b + 2)
                pe.wait_ge(k_ready, 2 * b + 2)
                for c in range(4):
                    at = slice(128 * c, 128 * c + 128)
                    for t in range(2):
                        last = pe.matmul(ps[BANKS[b]][:, at], vals[:, 2 * b + t, at], keys[:, 2 * b + t, at],
                                         start=(t == 0), stop=(t == 1))
                last.then_inc(dots_ps, 1)
            for b in range(NB):
                pe.wait_ge(dots_ready, b + 1)
                for c in range(4):
                    last = pe.matmul(ps[BANKS[b]][:, c * D:(c + 1) * D], dots[:, b, c, :], w.a2_woT[:, c, :],
                                     start=True, stop=True)
                last.then_inc(do_ps, 1)
            for b in range(NB):
                pe.wait_ge(do_ready, b + 1)
                for c in range(4):
                    last = pe.matmul(ps[BANKS[b]][0:D, 256:256 + D], w.a2_Wq[:, c, :], dots_o[:, b, c, :],
                                     start=(c == 0), stop=(c == 3))
                last.then_inc(m_ps, 1)
            for b in range(NB):
                pe.wait_ge(m_ready, b + 1)
                for t in range(2):
                    at = (b % G) * SEQ + t * TP
                    last = pe.matmul(ps[BANKS[b]][0:TP, 320 + t * D:320 + (t + 1) * D], w.xT[:, b // G, at:at + TP],
                                     w.a2_M[:, b, :], start=True, stop=True)
                last.then_inc(out_ps, 1)

        @block.scalar
        def _(act):
            for g in range(GROUPS):
                act.wait_ge(turned, g + 1)
                act.activation(w.xT[0:D, g, :], ps[6 + g][0:D, 0:COLS], ACT.Copy).then_inc(xT_ready, 1)

            for i in range(NT):
                act.wait_ge(kv_ps, 2 * i + 2)
                if i >= 2:
                    act.wait_ge(kv_sum, i - 1)
                both = w.banks[0:TP, 2 * (i % 3):2 * (i % 3) + 2, :]
                act.activation(kv_sq[:, i % 2, :, :].rearrange("p (c h) n -> p c (h n)", c=2), both, ACT.Square
                               ).then_inc(sq_ready, 1)
                act.activation(keys[:, i, :], ps[2 * (i % 3)][0:TP, :], ACT.Copy).then_inc(k_ready, 1)
            act.wait_ge(zeroed, 1)
            for b in range(NB):
                act.wait_ge(dots_ps, b + 1)
                for half in range(2):
                    at = slice(half * D, half * D + D)
                    last = act.activation(dots[at, b, :, at], ps[BANKS[b]][at, :].rearrange(
                        "p (c n) -> p c n", c=4)[:, :, at], ACT.Copy)
                last.then_inc(dots_ready, 1)
            for b in range(NB):
                act.wait_ge(m_ps, b + 1)
                act.activation(w.a2_M[0:D, b, :], ps[BANKS[b]][0:D, 256:256 + D], ACT.Copy, scale=1.0 / SEQ
                               ).then_inc(m_ready, 1)

        @block.vector
        def _(dve):
            normalize(dve, v_step, per_group(w.h, w.xn, squares, sums), 1e-5, var_ready, rstd_ready, 0, ready=xn_ready)
            for i in range(NT + 1):
                if i < NT:
                    dve.wait_ge(sq_ready, i + 1)
                    dve.tensor_reduce(kv_var[:, i % 3, :], kv_sq[:, i % 2, :, :], X, ALU.add).then_inc(kv_sum, 1)
                if i < NT:
                    dve.wait_ge(kv_sum, i + 1)
                    dve.tensor_scalar(kv_var[:, i % 3, :], kv_var[:, i % 3, :], 1.0 / D, 1e-5, ALU.mult, ALU.add
                                      ).then_inc(kv_var_ready, 1)
                if i:
                    dve.wait_ge(root_ready, i)
                    dve.tensor_tensor(vals[:, i - 1, :].rearrange("p (h n) -> p h n", h=8),
                                      ps[2 * ((i - 1) % 3) + 1][0:TP, :].rearrange("p (h n) -> p h n", h=8),
                                      wide(scale[:, (i - 1) % 3, :], D), ALU.mult).then_inc(v_ready, 1)
                if i < NT:
                    dve.wait_ge(kv_var_ready, i + 1)
                    dve.tensor_tensor(scale[:, i % 3, :], kv_var[:, i % 3, 0:8], kv_var[:, i % 3, 8:16], ALU.mult
                                      ).then_inc(kv_scaled, 1)
            for b in range(NB):
                dve.wait_ge(do_ps, b + 1)
                dve.tensor_copy(dots_o[:, b, :, :], ps[BANKS[b]][:, 0:4 * D].rearrange("p (c n) -> p c n", c=4)
                                ).then_inc(do_ready, 1)
            for b in range(NB):
                dve.wait_ge(out_ps, b + 1)
                at = slice(2 * b, 2 * b + 2)
                dve.tensor_tensor(w.h[:, at, :], w.h[:, at, :], ps[BANKS[b]][0:TP, 320:320 + 2 * D].rearrange(
                    "p (t n) -> p t n", t=2), ALU.add).then_inc(out_read, 1)
            dve.wait_ge(out_read, NB)

        return sems


class Softmax:

    W3 = 3 * TP
    TERMS = ((0, 0), (0, 1), (1, 0), (1, 1), (0, 2), (2, 0))
    K = 16 * len(TERMS)

    def __init__(self, w, steps_of, index, q_of, k_of, v_of, width, units, sem):
        self.w, self.steps_of, self.index = w, steps_of, index
        self.q_of, self.k_of, self.v_of, self.width, self.units = q_of, k_of, v_of, width, units
        (self.zeroed, self.max3_ready, self.max_ps, self.max_ready, self.maxT_ps, self.maxT_ready, self.s_ps,
         self.probs_ready, self.o_ps, self.o_read) = sem(
            "max3_zeroed", "max3_ready", "max_ps", "max_ready", "maxT_ps", "maxT_ready", "s_ps", "probs_ready",
            "o_ps", "o_read")
        self.hi_ready, self.rest_ready, self.mid_ready, self.split, self.k_in, *self.q_in = sem(
            "hi_ready", "rest_ready", "mid_ready", "split", "k_in", "q_in0", "q_in1", "q_in2", "q_in3")
        self.shift_in = sem("shift_in0", "shift_in1")
        self.first = [(b, s) for u in range(0, units, 2) for pair in ((0, 1), (2, 3)) for b in (u, u + 1)
                      for s, (rows, _) in enumerate(steps_of) if rows == pair]
        self.per = 2 * len(steps_of)

    def memory(self, sb, per_row, key_rows):
        NB = self.units
        self.tiles = GROUPS * per_row
        self.parts = sb("parts", [128, 3, self.tiles, COLS], BF16)
        self.split_rest = sb("split_rest", [128, 3, COLS])
        self.qx = sb("qx", [self.K + 3, 4, self.tiles, COLS], BF16)
        self.kx = sb("kx", [self.K + 3, key_rows, self.tiles, COLS], BF16)
        self.maxima = sb("maxima", [TP, NB, 2, self.width])
        self.max3 = sb("max3", [TP, NB * 2, 96])
        self.maxT = sb("maxT", [96, NB, SEQ], BF16)
        self.rest = sb("maxT_rest", [96, 2 * SEQ])
        self.mid = sb("maxT_mid", [96, 2 * SEQ], BF16)
        self.probs = sb("probs", [TP, 3, 2, 2 * self.W3])

    def pool_prepare(self, pool):
        pool.memset(self.max3[:], 0.0).then_inc(self.zeroed, 1)
        pool.wait_ge(self.zeroed, 1)
        pool.memset(self.kx[self.K:self.K + 3, :, :, :], -1.0).then_inc(self.zeroed, 1)
        pool.wait_ge(self.zeroed, 2)

    def act_split(self, act, source, ready):
        for i in range(self.tiles + 1):
            if i < self.tiles:
                act.wait_ge(ready, i + 1)
                act.activation(self.parts[:, 0, i, :], source(i), ACT.Copy).then_inc(self.hi_ready, 1)
            if i:
                act.wait_ge(self.rest_ready, i)
                act.activation(self.parts[:, 1, i - 1, :], self.split_rest[:, (i - 1) % 3, :], ACT.Copy
                               ).then_inc(self.mid_ready, 1)

    def dve_split(self, dve, source):
        for i in range(self.tiles + 1):
            if i < self.tiles:
                dve.wait_ge(self.hi_ready, i + 1)
                if i >= 3:
                    dve.wait_ge(self.split, i - 2)
                dve.tensor_tensor(self.split_rest[:, i % 3, :], source(i), self.parts[:, 0, i, :], ALU.subtract
                                  ).then_inc(self.rest_ready, 1)
            if i:
                dve.wait_ge(self.mid_ready, i)
                dve.tensor_tensor(self.parts[:, 2, i - 1, :], self.split_rest[:, (i - 1) % 3, :],
                                  self.parts[:, 1, i - 1, :], ALU.subtract).then_inc(self.split, 1)

    def sp_stack(self, sp, shifts):
        sp.wait_ge(self.split, self.tiles)
        for r in range(self.kx.shape[1]):
            for t, (_, part) in enumerate(self.TERMS):
                sp.dma_start(self.kx[16 * t:16 * t + 16, r, :, :], self.parts[32 * r + 16:32 * r + 32, part, :, :]
                             ).then_inc(self.k_in, 16)
        for r in range(4):
            for t, (part, _) in enumerate(self.TERMS):
                sp.dma_start(self.qx[16 * t:16 * t + 16, r, :, :], self.parts[32 * r:32 * r + 16, part, :, :]
                             ).then_inc(self.q_in[r], 16)
        for g, pairs in enumerate(shifts):
            sp.wait_ge(self.maxT_ready, g + 1)
            for dst, src in pairs:
                sp.dma_start(dst, src).then_inc(self.shift_in[g], 16)
        self.n_shifts = len(shifts[0])

    def banks(self, i):
        return 2 * (i % 3)

    def pe_scores(self, pe, i, b, rows, cols, transposed):
        w, W3, K = self.w, self.W3, self.K
        for j, r in enumerate(rows):
            for k, c in enumerate(cols):
                o = w.psum[self.banks(i) + j][0:TP, k * W3:(k + 1) * W3]
                q, key = self.q_of(b, r, c), self.k_of(b, r, c)
                if not transposed:
                    parts = ((o[:, 0:TP], q[0:K, 0:TP], key[0:K, 0:TP], w.maskQ[:, TP:SEQ]),
                             (o[:, TP:W3], q[0:K, TP:SEQ], key[0:K, :], w.maskQ[:, :]))
                else:
                    parts = ((o[:, 0:SEQ], key[:, 0:TP], q, w.maskT[:, :]),
                             (o[:, SEQ:W3], key[:, TP:SEQ], q[:, TP:SEQ], w.maskT[:, 0:TP]))
                for out, lhsT, rhs, mask in parts:
                    pe.matmul(out, w.ident_b[:, :], mask, start=True, stop=False)
                    last = pe.matmul(out, lhsT, rhs, start=False, stop=True)
        return last

    def pe_all(self, pe):
        S, NB = self.steps_of, self.units
        pe.wait_ge(self.k_in, 16 * len(self.TERMS) * self.kx.shape[1])
        arrived = []
        for i, (b, s) in enumerate(self.first):
            rows, cols = S[s]
            for r in rows:
                if r not in arrived:
                    pe.wait_ge(self.q_in[r], 16 * len(self.TERMS))
                    arrived.append(r)
            if i >= 3:
                pe.wait_ge(self.max_ready, i - 2)
            self.pe_scores(pe, i, b, rows, cols, False).then_inc(self.max_ps, 1)
            if i % self.per == 1 and i > 1:
                self.pe_turn_maxima(pe, i // self.per - 1)
        self.pe_turn_maxima(pe, NB // 2 - 1)
        total = NB * len(S)
        pe.wait_ge(self.max_ready, total)
        pe.wait_ge(self.zeroed, 2)
        for i in range(total + 2):
            if i < total:
                b, s = i // len(S), i % len(S)
                pe.wait_ge(self.shift_in[b // 2], 16 * self.n_shifts)
                if i >= 3:
                    pe.wait_ge(self.probs_ready, i - 2)
                self.pe_scores(pe, i, b, *S[s], True).then_inc(self.s_ps, 1)
            if i >= 2:
                self.pe_values(pe, i - 2)

    def pe_turn_maxima(self, pe, g):
        pe.wait_ge(self.max3_ready, g + 1)
        if g >= 2:
            pe.wait_ge(self.maxT_ready, g - 1)
        for u in range(4):
            last = pe.transpose(self.w.psum[6 + g % 2][0:96, u * TP:(u + 1) * TP], self.max3[:, g * 4 + u, :],
                                self.w.ident[0:TP, 0:TP])
        last.then_inc(self.maxT_ps, 1)

    def pe_values(self, pe, i):
        S, W3 = self.steps_of, self.W3
        b, s = i // len(S), i % len(S)
        rows, cols = S[s]
        pe.wait_ge(self.probs_ready, i + 1)
        if s == 0:
            if b:
                pe.wait_ge(self.o_read, 2 * b)
            else:
                pe.wait_ge(self.maxT_ready, self.units // 2)
        for j, r in enumerate(rows):
            for k, c in enumerate(cols):
                m, pr = self.index(r, c), self.probs[:, i % 3, j, k * W3:(k + 1) * W3]
                v0, v1 = self.v_of(b, 0, r, c), self.v_of(b, 1, r, c)
                f = v0.shape[1]
                at = slice(m * f, (m + 1) * f)
                pe.matmul(self.w.psum[6][0:TP, at], pr[:, 0:TP], v0, start=True, stop=True)
                pe.matmul(self.w.psum[7][0:TP, at], pr[:, TP:SEQ], v0, start=True, stop=False)
                last = pe.matmul(self.w.psum[7][0:TP, at], pr[:, SEQ:W3], v1, start=False, stop=True)
        if s == len(S) - 1:
            last.then_inc(self.o_ps, 1)

    def act_all(self, act):
        S, NB = self.steps_of, self.units
        for i in range(NB * len(S)):
            act.wait_ge(self.s_ps, i + 1)
            if i >= 3 * len(S):
                act.wait_ge(self.o_ps, (i - 3) // len(S))
            act.activation(self.probs[:, i % 3, :, :], self.w.banks[0:TP, self.banks(i):self.banks(i) + 2, 0:2 * self.W3],
                           ACT.Exp).then_inc(self.probs_ready, 1)

    def dve_maxima(self, dve, steps, out_of):
        for i, (b, s) in enumerate(self.first):
            dve.wait_ge(self.max_ps, i + 1)
            both = self.w.banks[0:TP, self.banks(i):self.banks(i) + 2, 0:2 * self.W3].rearrange(
                "p j (k n) -> p j k n", k=2)
            dve.tensor_reduce(out_of(b, 0, s), both[:, :, :, 0:TP], X, ALU.max)
            dve.tensor_reduce(out_of(b, 1, s), both[:, :, :, TP:], X, ALU.max).then_inc(self.max_ready, 1)
            g, at = i // self.per, i % self.per
            if at == 3 and g:
                self.dve_split_maxima(dve, steps, g - 1)
            if at == self.per - 1:
                dve.wait_ge(self.max_ready, i + 1)
                dve.wait_ge(self.zeroed, 2)
                some = self.maxima[:, g * 2:(g + 1) * 2, :, :].rearrange("p b t m -> p (b t) m")
                for p in range(3):
                    last = dve.tensor_copy(self.max3[:, g * 4:(g + 1) * 4, 32 * p:32 * p + self.width], some)
                last.then_inc(self.max3_ready, 1)
        self.dve_split_maxima(dve, steps, self.units // 2 - 1)

    def dve_split_maxima(self, dve, steps, g):
        dve.wait_ge(self.maxT_ps, g + 1)
        ps, high = self.w.psum[6 + g % 2][0:96, 0:2 * SEQ], self.maxT[:, g * 2:(g + 1) * 2, :].rearrange(
            "p b n -> p (b n)")
        rest, mid = self.rest[:, :], self.mid[:, :]
        steps.did(dve.tensor_copy(high, ps))
        steps.wait(dve)
        steps.did(dve.tensor_tensor(rest, ps, high, ALU.subtract))
        steps.wait(dve)
        steps.did(dve.tensor_copy(mid, rest))
        steps.wait(dve)
        steps.did(dve.tensor_copy(high[32:64, :], mid[32:64, :]))
        dve.tensor_tensor(high[64:96, :], rest[64:96, :], mid[64:96, :], ALU.subtract).then_inc(self.maxT_ready, 1)
        dve.wait_ge(self.maxT_ready, g + 1)


def ffn1(nc, d, w):
    NT, NB = GROUPS * U, G * GROUPS
    R = U * 4
    with ExitStack() as ctx:
        sb, sem, sems = layer_memory(nc, ctx, "ffn1")
        squares, sums = sb("squares", [TP, NT, D]), sb("sums", [TP, NT])
        sxT = sb("sxT", [D, GROUPS, COLS])
        sx, nonzero = sb("sx", [TP, NT, D]), sb("nonzero", [TP, NT, D])
        vals = sb("vals", [TP, NT, 4, 17])
        den = sb("den", [TP, 2, 16])
        ov = sb("ov", [TP, NT, 256])
        ovT = sb("ovT", [128, 2, GROUPS, COLS])
        gs = sb("gs", [TP, NT, 16])
        gstat = sb("gstat", [TP, NT, 4])
        mixed = sb("mixed", [TP, NT, D])
        sums4 = sb("sums4", [TP, NT * 4])
        f_n, f_nz, hx = sb("f_n", [TP, NT, D]), sb("f_nz", [TP, NT, D]), sb("hx", [TP, NT, D])
        fg, fstat = sb("fg", [TP, NT, 4]), sb("fstat", [TP, NT])
        v_step = Steps(sem("v_step"))
        var_ready, rstd_ready, xn_ready, turned, xT_ready = sem("var", "rstd", "xn_ready", "turned", "xT_ready")
        ones_ready, sx_ps, sxT_ready, qk_ps, v_ps, v_ready = sem(
            "ones_ready", "sx_ps", "sxT_ready", "qk_ps", "v_ps", "v_ready")
        sx_read = sem("sx_read")
        ov_ready, ov_turned, ovT_ready, gate_ps, gz_ready, gex_ready = sem(
            "ov_ready", "ov_turned", "ovT_ready", "gate_ps", "gz_ready", "gex_ready")
        t_in, t_ps, t_ready, p_ps, fz_ready, fex_ready = sem("t_in", "t_ps", "t_ready", "p_ps", "fz_ready", "fex_ready")

        def of_batch(t, b, n):
            return t[:, b // G * 4 + n, (b % G) * SEQ:(b % G + 1) * SEQ]

        steps_of = [((0, 1), (0, 1)), ((2, 3), (0, 1)), ((0, 1), (2, 3)), ((2, 3), (2, 3))]
        sm = Softmax(w, steps_of, lambda e, n: 4 * n + e, lambda b, e, n: of_batch(sm.qx[:, e, :, :], b, n),
                     lambda b, e, n: of_batch(sm.kx[:, 0, :, :], b, n), lambda b, t, e, n: vals[:, 2 * b + t, n, :],
                     16, NB, sem)
        sm.memory(sb, 4, 1)
        block = ctx.enter_context(nc.Block())
        ps = w.psum

        def tok_ps(bank, n=D):
            return ps[bank][0:TP, 0:U * n].rearrange("p (u n) -> p u n", u=U)

        def qk_source(i):
            return ps[4 + i % 3][:, 0:COLS]

        def rows4(t, g):
            return tiles(t, g).rearrange("p u (r n) -> p (u r) n", r=4)

        @block.sync
        def _(sp):
            sm.sp_stack(sp, [[(sm.qx[sm.K + p:sm.K + p + 1, e, g * 4:(g + 1) * 4, :],
                              sm.maxT[32 * p + e:32 * p + e + 13:4, g * G:(g + 1) * G, :].rearrange("m b t -> m (b t)"))
                              for p in range(3) for e in range(4)] for g in range(GROUPS)])

        @block.gpsimd
        def _(pool):
            pool.memset(vals[:, :, :, 16:17], 1.0).then_inc(ones_ready, 1)
            pool.wait_ge(ones_ready, 1)
            sm.pool_prepare(pool)
            roots(pool, w, [s for s, in per_group(sums)], var_ready, rstd_ready, 0)
            for i in range(1, 3):
                roots(pool, w, [sums4[:, g * R:(g + 1) * R] for g in range(GROUPS)], var_ready, rstd_ready, i * GROUPS)

        @block.tensor
        def _(pe):
            for g in range(GROUPS):
                pe.wait_ge(xn_ready, g + 1)
                turn_tokens(pe, w, g, tiles(w.xn, g)).then_inc(turned, 1)
            for g in range(GROUPS):
                pe.wait_ge(xT_ready, g + 1)
                pe.matmul(ps[2 + g][0:D, 0:COLS], w.f1_hlT[:, :], w.xT[:, g, :], start=True, stop=True)
                for u in range(U):
                    last = pe.matmul(ps[4 + g][0:TP, u * D:(u + 1) * D], w.xT[:, g, u * TP:(u + 1) * TP],
                                     w.f1_hlT[:, :], start=True, stop=True)
                last.then_inc(sx_ps, 1)
            for g in range(GROUPS):
                pe.wait_ge(sxT_ready, g + 1)
                if g:
                    pe.wait_ge(v_ready, g)
                for u in range(U):
                    last = pe.matmul(ps[7][0:TP, u * D:(u + 1) * D], sxT[:, g, u * TP:(u + 1) * TP], w.f1_vT[:, :],
                                     start=True, stop=True)
                last.then_inc(v_ps, 1)
            for g in range(GROUPS):
                for n in range(4):
                    i = 4 * g + n
                    if i < 3:
                        pe.wait_ge(sx_read, GROUPS)
                    else:
                        pe.wait_ge(sm.rest_ready, i - 2)
                    pe.matmul(ps[4 + i % 3][:, 0:COLS], w.f1_qkT[:, n, :], sxT[:, g, :], start=True, stop=True
                              ).then_inc(qk_ps, 1)
            pe.wait_ge(sm.rest_ready, 4 * GROUPS)
            pe.wait_ge(v_ready, GROUPS)
            sm.pe_all(pe)
            for g in range(GROUPS):
                pe.wait_ge(ov_ready, (g + 1) * U)
                for c in range(2):
                    for u in range(U):
                        last = pe.transpose(ps[2 * g + c][:, u * TP:(u + 1) * TP],
                                            ov[:, g * U + u, c * 128:(c + 1) * 128], w.ident[0:TP, 0:TP])
                    last.then_inc(ov_turned, 1)
            for g in range(GROUPS):
                pe.wait_ge(ovT_ready, 2 * g + 2)
                for u in range(U):
                    o = ps[4 + g][0:TP, u * 16:(u + 1) * 16]
                    for c in range(2):
                        pe.matmul(o, ovT[:, c, g, u * TP:(u + 1) * TP], w.f1_gateT[:, c, :], start=(c == 0), stop=False)
                    last = pe.matmul(o, w.ones_row[:, 0:TP], w.f1_gate_b[:, :], start=False, stop=True)
                last.then_inc(gate_ps, 1)
            for i, (t, wt, n) in enumerate(((f_n, w.f1_fc1T[:, :], D), (hx, w.f1_fc2T[:, :], D),
                                            (mixed, w.f1_fgT[:, :], 4))):
                for g in range(GROUPS):
                    pe.wait_ge(t_in, i * GROUPS + g + 1)
                    turn_tokens(pe, w, g, tiles(t, g)).then_inc(t_ps, 1)
                for g in range(GROUPS):
                    pe.wait_ge(t_ready, i * GROUPS + g + 1)
                    for u in range(U):
                        last = pe.matmul(ps[2 + g][0:TP, u * n:(u + 1) * n],
                                         w.xT[0:wt.shape[0], g, u * TP:(u + 1) * TP], wt, start=True, stop=True)
                    last.then_inc(p_ps, 1)

        @block.scalar
        def _(act):
            act.preload_act_table(ACT.Exp)
            for g in range(GROUPS):
                act.wait_ge(turned, g + 1)
                act.activation(w.xT[0:D, g, :], ps[g][0:D, 0:COLS], ACT.Copy).then_inc(xT_ready, 1)
            for g in range(GROUPS):
                act.wait_ge(sx_ps, g + 1)
                act.activation(sxT[:, g, :], ps[2 + g][0:D, 0:COLS], ACT.Copy).then_inc(sxT_ready, 1)
            for g in range(GROUPS):
                act.wait_ge(v_ps, g + 1)
                act.activation(vals[:, g * U:(g + 1) * U, :, 0:16], ps[7][0:TP, 0:U * D].rearrange(
                    "p (u n k) -> p u n k", u=U, n=4), ACT.Copy).then_inc(v_ready, 1)
            sm.act_split(act, qk_source, qk_ps)
            sm.act_all(act)
            for g in range(GROUPS):
                for c in range(2):
                    act.wait_ge(ov_turned, 2 * g + c + 1)
                    act.activation(ovT[:, c, g, :], ps[2 * g + c][:, 0:COLS], ACT.Copy).then_inc(ovT_ready, 1)
            for g in range(GROUPS):
                act.wait_ge(gz_ready, g + 1)
                act.activation(tiles(gs, g), tiles(gs, g), ACT.Exp).then_inc(gex_ready, 1)
            for i in range(3):
                for g in range(GROUPS):
                    act.wait_ge(t_ps, i * GROUPS + g + 1)
                    act.activation(w.xT[0:D, g, :], ps[g][0:D, 0:COLS], ACT.Copy).then_inc(t_ready, 1)
            for g in range(GROUPS):
                act.wait_ge(fz_ready, g + 1)
                act.activation(tiles(fg, g), tiles(fg, g), ACT.Exp).then_inc(fex_ready, 1)

        @block.vector
        def _(dve):
            normalize(dve, v_step, per_group(w.h, w.xn, squares, sums), 1e-5, var_ready, rstd_ready, 0, ready=xn_ready)
            for g in range(GROUPS):
                dve.wait_ge(sx_ps, g + 1)
                dve.tensor_copy(tiles(sx, g), tok_ps(4 + g)).then_inc(sx_read, 1)
            sm.dve_split(dve, qk_source)
            dve.wait_ge(sx_read, GROUPS)
            v_step.did(dve.tensor_scalar(nonzero[:, :, :], sx[:, :, :], 0.0, None, ALU.not_equal))
            for n in range(4):
                dve.copy_predicated(w.resid[:, :, n, :], w.in_first[:, :, n, :], sx[:, 2 * n:2 * n + 2, 16 * n:16 * n + 16])

            def out_of(b, t, s):
                rows, cols = steps_of[s]
                return sm.maxima[:, b, t, :].rearrange("p (n e) -> p e n", e=4)[:, rows[0]:rows[0] + 2, cols[0]:cols[0] + 2]

            sm.dve_maxima(dve, v_step, out_of)
            v_step.wait(dve)
            for b in range(NB):
                for t in range(2):
                    dve.wait_ge(sm.o_ps, b + 1)
                    out = ps[6 + t][0:TP, 0:16 * 17].rearrange("p (m k) -> p m k", m=16)
                    v_step.did(dve.reciprocal(den[:, t, :], out[:, :, 16]))
                for t in range(2):
                    wait_back(v_step, dve, 1 - t)
                    i = 2 * b + t
                    out = ps[6 + t][0:TP, 0:16 * 17].rearrange("p (m k) -> p m k", m=16)
                    dve.tensor_tensor(ov[:, i, :].rearrange("p (m k) -> p m k", m=16), out[:, :, 0:16],
                                      wide(den[:, t, :], 16), ALU.mult).then_inc(sm.o_read, 1)
                for t in range(2):
                    i = 2 * b + t
                    dve.wait_ge(sm.o_read, i + 1)
                    parts = ov[:, i, :].rearrange("p (n e k) -> p n e k", n=4, e=4)
                    nz = nonzero[:, i, :].rearrange("p (n k) -> p n k", n=4).unsqueeze(2).broadcast_to([TP, 4, 4, 16])
                    dve.tensor_tensor(parts, parts, nz, ALU.mult).then_inc(ov_ready, 1)
            for g in range(GROUPS):
                dve.wait_ge(gate_ps, g + 1)
                v_step.did(dve.tensor_reduce(tiles(gstat, g), tok_ps(4 + g, 16).rearrange("p u (n e) -> p u n e", n=4),
                                             X, ALU.max))
            for g in range(GROUPS):
                wait_back(v_step, dve, GROUPS - 1 - g)
                dve.tensor_tensor(tiles(gs, g).rearrange("p u (n e) -> p (u n) e", n=4),
                                  ps[4 + g][0:TP, 0:U * 16].rearrange("p (r e) -> p r e", e=4),
                                  wide(tiles(gstat, g).rearrange("p u n -> p (u n)"), 4), ALU.subtract
                                  ).then_inc(gz_ready, 1)
            for g in range(GROUPS):
                dve.wait_ge(gex_ready, g + 1)
                v_step.did(dve.tensor_reduce(tiles(gstat, g), tiles(gs, g).rearrange("p u (n e) -> p u n e", n=4),
                                             X, ALU.add))
            for g in range(GROUPS):
                wait_back(v_step, dve, GROUPS - 1)
                v_step.did(dve.reciprocal(tiles(gstat, g), tiles(gstat, g)))
            for g in range(GROUPS):
                wait_back(v_step, dve, GROUPS - 1)
                four = tiles(gs, g).rearrange("p u (n e) -> p (u n) e", n=4)
                v_step.did(dve.tensor_tensor(four, four, wide(tiles(gstat, g).rearrange("p u n -> p (u n)"), 4), ALU.mult))
            for g in range(GROUPS):
                wait_back(v_step, dve, GROUPS - 1)
                dve.wait_ge(ov_turned, 2 * g + 2)
                part = tiles(ov, g).rearrange("p u (m k) -> p (u m) k", m=16)
                v_step.did(dve.tensor_tensor(part, part, wide(tiles(gs, g).rearrange("p u m -> p (u m)"), 16), ALU.mult))
            for g in range(GROUPS):
                wait_back(v_step, dve, GROUPS - 1)
                v_step.did(dve.tensor_reduce(rows4(mixed, g), tiles(ov, g).rearrange(
                    "p u (n e k) -> p (u n) k e", n=4, e=4), X, ALU.add))
            for g in range(GROUPS):
                wait_back(v_step, dve, GROUPS - 1)
                both = tiles(mixed, g).rearrange("p (b t) n -> p b (t n)", t=2)
                v_step.did(dve.tensor_tensor(both, both, each(w.resid[:, :, :, :].rearrange("p t n k -> p (t n k)"), G),
                                             ALU.add))
            v_step.wait(dve)

            def heads_norm(src, dst, i, gain, bias):
                normalize(dve, v_step, [(rows4(src, g), rows4(dst, g), rows4(squares, g), sums4[:, g * R:(g + 1) * R])
                                        for g in range(GROUPS)], 1e-8, var_ready, rstd_ready, i * GROUPS)
                for vec, op in ((gain, ALU.mult), (bias, ALU.add)):
                    for g in range(GROUPS):
                        wait_back(v_step, dve, GROUPS - 1)
                        v_step.did(dve.tensor_tensor(rows4(dst, g), rows4(dst, g), each(vec[:, :], R), op))
                v_step.wait(dve)

            heads_norm(mixed, f_n, 1, w.f1_ln_g, w.f1_ln_b)
            for g in range(GROUPS):
                dve.tensor_scalar(tiles(f_nz, g), tiles(f_n, g), 0.0, None, ALU.not_equal).then_inc(t_in, 1)
            dve.wait_ge(t_in, GROUPS)
            for g in range(GROUPS):
                dve.wait_ge(p_ps, g + 1)
                dve.scalar_tensor_tensor(out=tiles(hx, g), in0=tok_ps(2 + g), scalar=0.0, in1=tiles(f_nz, g),
                                         op0=ALU.max, op1=ALU.mult).then_inc(t_in, 1)
            for g in range(GROUPS):
                dve.wait_ge(p_ps, GROUPS + g + 1)
                v_step.did(dve.tensor_tensor(tiles(mixed, g), tok_ps(2 + g), tiles(f_nz, g), ALU.mult))
            for g in range(GROUPS):
                wait_back(v_step, dve, GROUPS - 1)
                v_step.did(dve.tensor_tensor(tiles(mixed, g), tiles(mixed, g), tiles(f_n, g), ALU.add))
            v_step.wait(dve)
            heads_norm(mixed, mixed, 2, w.f1_fn_g, w.f1_fn_b)
            for g in range(GROUPS):
                dve.sem_inc(t_in, 1)
            for g in range(GROUPS):
                dve.wait_ge(p_ps, 2 * GROUPS + g + 1)
                v_step.did(dve.tensor_reduce(fstat[:, g * U:(g + 1) * U], tok_ps(2 + g, 4), X, ALU.max))
            for g in range(GROUPS):
                wait_back(v_step, dve, GROUPS - 1 - g)
                dve.tensor_tensor(tiles(fg, g), tok_ps(2 + g, 4), wide(fstat[:, g * U:(g + 1) * U], 4), ALU.subtract
                                  ).then_inc(fz_ready, 1)
            for g in range(GROUPS):
                dve.wait_ge(fex_ready, g + 1)
                v_step.did(dve.tensor_reduce(fstat[:, g * U:(g + 1) * U], tiles(fg, g), X, ALU.add))
            for g in range(GROUPS):
                wait_back(v_step, dve, GROUPS - 1)
                v_step.did(dve.reciprocal(fstat[:, g * U:(g + 1) * U], fstat[:, g * U:(g + 1) * U]))
            for g in range(GROUPS):
                wait_back(v_step, dve, GROUPS - 1)
                v_step.did(dve.tensor_tensor(tiles(fg, g), tiles(fg, g), wide(fstat[:, g * U:(g + 1) * U], 4), ALU.mult))
            for g in range(GROUPS):
                wait_back(v_step, dve, GROUPS - 1)
                v_step.did(dve.tensor_tensor(rows4(mixed, g), rows4(mixed, g), wide(tiles(fg, g).rearrange(
                    "p u n -> p (u n)"), 16), ALU.mult))
            for g in range(GROUPS):
                wait_back(v_step, dve, GROUPS - 1)
                v_step.did(dve.tensor_tensor(tiles(w.h, g), tiles(w.h, g), tiles(mixed, g), ALU.add))
            v_step.wait(dve)

        return sems


def ffn2(nc, d, w):
    NT, NC = GROUPS * U, len(CHUNKS2)
    with ExitStack() as ctx:
        sb, sem, sems = layer_memory(nc, ctx, "ffn2")
        squares, sums = sb("squares", [TP, NT, D]), sb("sums", [TP, NT])
        rn = sb("rn", [TP, NT, D])
        by_cos, by_sin = sb("by_cos", [128, GROUPS, COLS]), sb("by_sin", [128, GROUPS, COLS])
        vals = sb("vals", [TP, NT, 2, 17])
        den = sb("den", [TP, 2, 8])
        act1 = sb("act1", [128, 3, COLS])
        hh = sb("hh", [128, NC, GROUPS, COLS])
        gate3 = sb("gate3", [TP, NT, 96])
        gateT = sb("gateT", [96, GROUPS, COLS], BF16)
        gate_rest = sb("gate_rest", [96, GROUPS, COLS])
        gate_mid = sb("gate_mid", [96, GROUPS, COLS], BF16)
        best, code_max, total = sb("best", [TP, NT]), sb("code_max", [TP, NT]), sb("total", [TP, NT])
        z, z2, code, hot, hot2, ex = (sb(n, [TP, NT, 8]) for n in ("z", "z2", "code", "hot", "hot2", "ex"))
        v_step = Steps(sem("v_step"))
        var_ready, rstd_ready, turn_in, turned, xT_ready = sem("var", "rstd", "turn_in", "turned", "xT_ready")
        ones_ready, qk_ps, rope_read, qk_ready, v_ps, v_ready, att_ps = sem(
            "ones_ready", "qk_ps", "rope_read", "qk_ready", "v_ps", "v_ready", "att_ps")
        h_ps, silu_ready, hh_ready, logit_ps, z_ready, ex_ready, y_ps = sem(
            "h_ps", "silu_ready", "hh_ready", "logit_ps", "z_ready", "ex_ready", "y_ps")
        gate3_zeroed, gate3_ready, gate_turned, gateT_ready, gate_ps, gated = sem(
            "gate3_zeroed", "gate3_ready", "gate_turned", "gateT_ready", "gate_ps", "gated")

        steps_of = [((0, 1), (0, 1)), ((2, 3), (0, 1))]
        sm = Softmax(w, steps_of, lambda hd, c: 4 * c + hd, lambda g, hd, c: sm.qx[:, hd, g, c * SEQ:(c + 1) * SEQ],
                     lambda g, hd, c: sm.kx[:, hd // 2, g, c * SEQ:(c + 1) * SEQ],
                     lambda g, t, hd, c: vals[:, g * U + 2 * c + t, hd // 2, :], 8, GROUPS, sem)
        sm.memory(sb, 1, 2)
        block = ctx.enter_context(nc.Block())
        ps = w.psum

        def tok_ps(bank, n=D):
            return ps[bank][0:TP, 0:U * n].rearrange("p (u n) -> p u n", u=U)

        @block.sync
        def _(sp):
            sm.sp_stack(sp, [[(sm.qx[sm.K + p:sm.K + p + 1, :, :, c * SEQ:(c + 1) * SEQ],
                              sm.maxT[32 * p + 4 * c:32 * p + 4 * c + 4, :, :]) for c in range(2) for p in range(3)]])

        @block.gpsimd
        def _(pool):
            pool.memset(vals[:, :, :, 16:17], 1.0).then_inc(ones_ready, 1)
            pool.wait_ge(ones_ready, 1)
            pool.memset(gate3[:], 0.0).then_inc(gate3_zeroed, 1)
            pool.wait_ge(gate3_zeroed, 1)
            sm.pool_prepare(pool)
            for i in range(3):
                roots(pool, w, [s for s, in per_group(sums)], var_ready, rstd_ready, i * GROUPS)

        @block.tensor
        def _(pe):
            def turn(i, src):
                for g in range(GROUPS):
                    pe.wait_ge(turn_in, i * GROUPS + g + 1)
                    turn_tokens(pe, w, 6 + g, tiles(src, g)).then_inc(turned, 1)

            turn(0, rn)
            for g in range(GROUPS):
                pe.wait_ge(xT_ready, g + 1)
                for j in range(2):
                    pe.matmul(ps[2 * g + j][:, 0:COLS], w.f2_qkT[:, j, :], w.xT[0:D, g, :], start=True, stop=True
                              ).then_inc(qk_ps, 1)
                for u in range(U):
                    last = pe.matmul(ps[4 + g][0:TP, u * 32:(u + 1) * 32], w.xT[0:D, g, u * TP:(u + 1) * TP], w.f2_vT[:, :],
                                     start=True, stop=True)
                last.then_inc(v_ps, 1)
            pe.wait_ge(rope_read, 2 * GROUPS)
            pe.wait_ge(v_ready, GROUPS)
            sm.pe_all(pe)
            pe.wait_ge(sm.o_read, 2 * GROUPS)
            turn(1, rn)
            for g in range(GROUPS):
                pe.wait_ge(xT_ready, GROUPS + g + 1)
                for u in range(U):
                    last = pe.matmul(ps[g][0:TP, u * D:(u + 1) * D], w.xT[0:D, g, u * TP:(u + 1) * TP], w.f2_oT[:, :],
                                     start=True, stop=True)
                last.then_inc(att_ps, 1)
            turn(2, rn)
            for g in range(GROUPS):
                pe.wait_ge(xT_ready, 2 * GROUPS + g + 1)
                for u in range(U):
                    last = pe.matmul(ps[g][0:TP, u * 8:(u + 1) * 8], w.xT[0:D, g, u * TP:(u + 1) * TP],
                                     w.f2_routerT[:, :], start=True, stop=True)
                last.then_inc(logit_ps, 1)
            for q in range(NC * GROUPS):
                g, c = q // NC, q % NC
                if q >= 2:
                    pe.wait_ge(silu_ready, q - 1)
                    pe.wait_ge(hh_ready, q - 1)
                for i, wt in enumerate((w.f2_w1T, w.f2_w3T)):
                    pe.matmul(ps[2 + 2 * (q % 2) + i][0:CHUNKS2[c], 0:COLS], wt[:, 128 * c:128 * c + CHUNKS2[c]],
                              w.xT[0:D, g, :], start=True, stop=True).then_inc(h_ps, 1)
            for g in range(GROUPS):
                pe.wait_ge(gate3_ready, g + 1)
                turn_tokens(pe, w, 6 + g, tiles(gate3, g)).then_inc(gate_turned, 1)
            pe.wait_ge(hh_ready, NC * GROUPS)
            for g in range(GROUPS):
                pe.wait_ge(gateT_ready, g + 1)
                for c in range(NC):
                    q = g * NC + c
                    if q >= 4:
                        pe.wait_ge(gated, q - 3)
                    pe.matmul(ps[2 + q % 4][0:CHUNKS2[c], 0:COLS], w.sel_expert[:, 128 * c:128 * c + CHUNKS2[c]],
                              gateT[:, g, :], start=True, stop=True).then_inc(gate_ps, 1)
            for g in range(GROUPS):
                pe.wait_ge(gated, (g + 1) * NC)
                for u in range(U):
                    for c, rows in enumerate(CHUNKS2):
                        last = pe.matmul(ps[g][0:TP, u * D:(u + 1) * D], hh[0:rows, c, g, u * TP:(u + 1) * TP],
                                         w.f2_w2T[0:rows, c, :], start=(c == 0), stop=(c == NC - 1))
                last.then_inc(y_ps, 1)

        @block.scalar
        def _(act):
            def turn(i):
                for g in range(GROUPS):
                    act.wait_ge(turned, i * GROUPS + g + 1)
                    act.activation(w.xT[0:D, g, :], ps[6 + g][0:D, 0:COLS], ACT.Copy).then_inc(xT_ready, 1)

            act.preload_act_table(ACT.Exp)
            turn(0)
            for g in range(GROUPS):
                act.wait_ge(v_ps, g + 1)
                act.activation(vals[:, g * U:(g + 1) * U, :, 0:16], ps[4 + g][0:TP, 0:U * 32].rearrange(
                    "p (u n k) -> p u n k", u=U, n=2), ACT.Copy).then_inc(v_ready, 1)
            sm.act_split(act, lambda g: by_cos[:, g, :], qk_ready)
            sm.act_all(act)
            turn(1)
            turn(2)
            for g in range(GROUPS):
                act.wait_ge(z_ready, g + 1)
                act.activation(tiles(ex, g), tiles(z, g), ACT.Exp).then_inc(ex_ready, 1)
            act.preload_act_table(ACT.Silu)
            for q in range(NC * GROUPS):
                act.wait_ge(h_ps, 2 * q + 1)
                if q >= 3:
                    act.wait_ge(hh_ready, q - 2)
                rows = CHUNKS2[q % NC]
                act.activation(act1[0:rows, q % 3, :], ps[2 + 2 * (q % 2)][0:rows, 0:COLS], ACT.Silu
                               ).then_inc(silu_ready, 1)

        @block.vector
        def _(dve):
            def rms(i):
                normalize(dve, v_step, per_group(w.xn, rn, squares, sums), 1e-6, var_ready, rstd_ready, i * GROUPS,
                          centre=False, ready=turn_in)

            normalize(dve, v_step, per_group(w.h, w.xn, squares, sums), 1e-5, var_ready, rstd_ready, 0)
            v_step.wait(dve)
            rms(1)
            for g in range(GROUPS):
                for j, (part, table) in enumerate(((by_cos, w.rope_cos), (by_sin, w.rope_sin))):
                    dve.wait_ge(qk_ps, 2 * g + j + 1)
                    dve.tensor_tensor(part[:, g, :].rearrange("p (b t) -> p b t", b=G),
                                      ps[2 * g + j][:, 0:COLS].rearrange("p (b t) -> p b t", b=G),
                                      each(table[:, :], G), ALU.mult).then_inc(rope_read, 1)
            for g in range(GROUPS):
                dve.wait_ge(rope_read, 2 * g + 2)
                dve.tensor_tensor(by_cos[:, g, :], by_cos[:, g, :], by_sin[:, g, :], ALU.add).then_inc(qk_ready, 1)
            sm.dve_split(dve, lambda g: by_cos[:, g, :])

            def out_of(g, t, s):
                rows, cols = steps_of[s]
                return sm.maxima[:, g, t, :].rearrange("p (c h) -> p h c", h=4)[:, rows[0]:rows[0] + 2, :]

            sm.dve_maxima(dve, v_step, out_of)
            for g in range(GROUPS):
                dve.wait_ge(sm.o_ps, g + 1)
                for t in range(2):
                    out = ps[6 + t][0:TP, 0:8 * 17].rearrange("p (m k) -> p m k", m=8)
                    v_step.did(dve.reciprocal(den[:, t, :], out[:, :, 16]))
                for t in range(2):
                    wait_back(v_step, dve, 1 - t)
                    out = ps[6 + t][0:TP, 0:8 * 17].rearrange("p (c h k) -> p c h k", c=2, h=4)
                    scale = den[:, t, :].rearrange("p (c h) -> p c h", c=2).unsqueeze(3).broadcast_to([TP, 2, 4, 16])
                    dve.tensor_tensor(rn[:, g * U + t:(g + 1) * U:2, :].rearrange("p c (h k) -> p c h k", h=4),
                                      out[:, :, :, 0:16], scale, ALU.mult).then_inc(sm.o_read, 1)
                dve.wait_ge(sm.o_read, 2 * g + 2)
                dve.sem_inc(turn_in, 1)
            for g in range(GROUPS):
                dve.wait_ge(att_ps, g + 1)
                v_step.did(dve.tensor_tensor(tiles(w.xn, g), tiles(w.xn, g), tok_ps(g), ALU.add))
            v_step.wait(dve)
            rms(2)
            for g in range(GROUPS):
                dve.wait_ge(logit_ps, g + 1)
                v_step.did(dve.tensor_reduce(best[:, g * U:(g + 1) * U], tok_ps(g, 8), X, ALU.max))
            for g in range(GROUPS):
                wait_back(v_step, dve, GROUPS - 1 - g)
                dve.tensor_tensor(tiles(z, g), tok_ps(g, 8), wide(best[:, g * U:(g + 1) * U], 8), ALU.subtract
                                  ).then_inc(z_ready, 1)
            dve.wait_ge(z_ready, GROUPS)

            def hidden(g):
                for c, rows in enumerate(CHUNKS2):
                    q = g * NC + c
                    dve.wait_ge(h_ps, 2 * q + 2)
                    dve.wait_ge(silu_ready, q + 1)
                    dve.tensor_tensor(hh[0:rows, c, g, :], act1[0:rows, q % 3, :], ps[3 + 2 * (q % 2)][0:rows, 0:COLS],
                                      ALU.mult).then_inc(hh_ready, 1)

            hidden(0)
            top_two(dve, v_step, w, z, z2, code, code_max, hot, hot2, best)

            def over_groups(f, back=GROUPS - 1):
                for g in range(GROUPS):
                    wait_back(v_step, dve, back)
                    v_step.did(f(g, total[:, g * U:(g + 1) * U]))

            dve.wait_ge(ex_ready, GROUPS)
            over_groups(lambda g, t: dve.tensor_reduce(t, tiles(ex, g), X, ALU.add))
            over_groups(lambda g, t: dve.reciprocal(t, t))
            over_groups(lambda g, t: dve.tensor_tensor(tiles(ex, g), tiles(ex, g), wide(t, 8), ALU.mult))
            over_groups(lambda g, t: dve.tensor_tensor(tiles(hot, g), tiles(hot, g), tiles(ex, g), ALU.mult))
            over_groups(lambda g, t: dve.tensor_reduce(t, tiles(hot, g), X, ALU.add))
            over_groups(lambda g, t: dve.tensor_scalar(t, t, 1e-9, None, ALU.add))
            over_groups(lambda g, t: dve.reciprocal(t, t))
            v_step.wait(dve)
            dve.wait_ge(gate3_zeroed, 1)
            for g in range(GROUPS):
                for p in range(3):
                    last = dve.tensor_tensor(tiles(gate3, g)[:, :, 32 * p:32 * p + 8], tiles(hot, g),
                                             wide(total[:, g * U:(g + 1) * U], 8), ALU.mult)
                last.then_inc(gate3_ready, 1)
            for g in range(1, GROUPS):
                hidden(g)
            for g in range(GROUPS):
                dve.wait_ge(gate_turned, g + 1)
                v_step.did(dve.tensor_copy(gateT[:, g, :], ps[6 + g][0:96, 0:COLS]))
            for g in range(GROUPS):
                wait_back(v_step, dve, GROUPS - 1)
                v_step.did(dve.tensor_tensor(gate_rest[:, g, :], ps[6 + g][0:96, 0:COLS], gateT[:, g, :], ALU.subtract))
            for g in range(GROUPS):
                wait_back(v_step, dve, GROUPS - 1)
                v_step.did(dve.tensor_copy(gate_mid[:, g, :], gate_rest[:, g, :]))
            for g in range(GROUPS):
                wait_back(v_step, dve, GROUPS - 1 - g)
                dve.tensor_copy(gateT[32:64, g, :], gate_mid[32:64, g, :])
                dve.tensor_tensor(gateT[64:96, g, :], gate_rest[64:96, g, :], gate_mid[64:96, g, :], ALU.subtract
                                  ).then_inc(gateT_ready, 1)
            dve.wait_ge(hh_ready, NC * GROUPS)
            for q in range(NC * GROUPS):
                g, c = q // NC, q % NC
                rows = CHUNKS2[c]
                dve.wait_ge(gate_ps, q + 1)
                dve.tensor_tensor(hh[0:rows, c, g, :], hh[0:rows, c, g, :], ps[2 + q % 4][0:rows, 0:COLS], ALU.mult
                                  ).then_inc(gated, 1)
            for g in range(GROUPS):
                dve.wait_ge(y_ps, g + 1)
                v_step.did(dve.tensor_tensor(tiles(w.xn, g), tiles(w.xn, g), tok_ps(g), ALU.add))
            for g in range(GROUPS):
                wait_back(v_step, dve, GROUPS - 1)
                v_step.did(dve.tensor_tensor(tiles(w.h, g), tiles(w.h, g), tiles(w.xn, g), ALU.add))
            v_step.wait(dve)

        return sems


def attn3(nc, d, w):
    NT = GROUPS * U
    STEPS = 2 * U
    ALL = GROUPS * STEPS
    PHI = (1.0 + math.sqrt(5.0)) / 2.0
    C1, C2 = PHI * math.sqrt(2.0) * 51.85, math.pi / PHI
    TURN = C1 / (2.0 * math.pi)
    HALF_PI = math.pi / 2.0
    BELOW_2PI = 6.2831845
    with ExitStack() as ctx:
        sb, sem, sems = layer_memory(nc, ctx, "attn3")
        sums = sb("sums", [TP, NT])
        qf, kf = sb("qf", [128, GROUPS, 4, COLS]), sb("kf", [128, GROUPS, 4, COLS])
        vals = sb("vals", [TP, NT, 512])
        step = [2, 2, SEQ]
        mag, low = sb("mag", [TP, 2] + step), sb("low", [TP, 2] + step)
        squares = low[:, 0, :, :, :].rearrange("p a c n -> p (a c n)")[:, 0:NT * D].rearrange("p (i n) -> p i n", n=D)
        z, frac, damp = (sb(n, [TP, STEPS] + step) for n in ("z", "frac", "damp"))
        cosine = sb("cosine", [TP, 2] + step)
        peak, total = sb("peak", [TP, STEPS, 4]), sb("total", [TP, STEPS, 4])
        half_pi = sb("half_pi", [TP, 1])
        aT = sb("aT", [TP, 2, 2, 4 * TP])
        v_step = Steps(sem("v_step"))
        var_ready, rstd_ready, xn_ready, turned, xT_ready = sem("var", "rstd", "xn_ready", "turned", "xT_ready")
        const_ready, q_ps, q_ready, k_ps, k_ready, v_ps, v_ready = sem(
            "const_ready", "q_ps", "q_ready", "k_ps", "k_ready", "v_ps", "v_ready")
        s_ps, mag_ready, low_ready, three_ready, frac_ready = sem(
            "s_ps", "mag_ready", "low_ready", "three_ready", "frac_ready")
        above_ready, held_ready, filtered, peak_ready, shift_ready = sem(
            "above_ready", "held_ready", "filtered", "peak_ready", "shift_ready")
        exp_ready, recip_ready, z_ready, turns_ready, rest_ready, square_ready, damp_ready = sem(
            "exp_ready", "recip_ready", "z_ready", "turns_ready", "rest_ready", "square_ready", "damp_ready")
        sin_ready, cos_ready, prod_ready, sum_ready, a_ready, aT_ps, aT_ready, used, o_read = sem(
            "sin_ready", "cos_ready", "prod_ready", "sum_ready", "a_ready", "aT_ps", "aT_ready", "used", "o_read")
        block = ctx.enter_context(nc.Block())
        ps = w.psum

        def scores_of(j):
            b = 2 * (j % 2)
            return w.banks[0:TP, b:b + 2, 0:2 * SEQ].rearrange("p a (c n) -> p a c n", c=2)

        def q_bank(i):
            return 4 if i >= 4 or i % 2 else 2

        def flat(t, j):
            return t[:, j, :, :, :].rearrange("p a c n -> p (a c n)")

        @block.gpsimd
        def _(pool):
            pool.memset(half_pi[:, :], HALF_PI).then_inc(const_ready, 1)
            pool.wait_ge(const_ready, 1)
            roots(pool, w, [s for s, in per_group(sums)], var_ready, rstd_ready, 0)

            def remainder(j):
                pool.wait_ge(three_ready, j + 1)
                pool.tensor_tensor(flat(mag, j % 2), flat(mag, j % 2), flat(low, j % 2), ALU.subtract
                                   ).then_inc(frac_ready, 1)

            def square(j):
                i = j % STEPS
                pool.wait_ge(z_ready, j + 1)
                pool.tensor_tensor(flat(damp, i), flat(z, i), flat(z, i), ALU.mult).then_inc(square_ready, 1)

            def product(j):
                i = j % STEPS
                pool.wait_ge(sin_ready, j + 1)
                pool.wait_ge(damp_ready, j + 1)
                pool.tensor_tensor(flat(damp, i), flat(frac, i), flat(damp, i), ALU.mult).then_inc(prod_ready, 1)

            for t in range(STEPS + 3):
                if t < STEPS:
                    remainder(t)
                if t >= 3:
                    square(t - 3)
                    pool.wait_ge(turns_ready, t - 2)
                    pool.tensor_tensor(flat(frac, t - 3), flat(z, t - 3), flat(frac, t - 3), ALU.subtract
                                       ).then_inc(rest_ready, 1)
            for g in range(1, GROUPS):
                for t in range(STEPS + 2):
                    if t >= 2:
                        remainder(g * STEPS + t - 2)
                    if t < STEPS:
                        product((g - 1) * STEPS + t)
                for i in range(STEPS):
                    square(g * STEPS + i)
            for i in range(STEPS):
                product((GROUPS - 1) * STEPS + i)

        @block.tensor
        def _(pe):
            for g in range(GROUPS):
                pe.wait_ge(xn_ready, g + 1)
                turn_tokens(pe, w, g, tiles(w.xn, g)).then_inc(turned, 1)

            def queries_keys(i):
                g, c = i // 4, i % 4
                pe.wait_ge(xT_ready, g + 1)
                if i == 2 or i == 3:
                    pe.wait_ge(q_ready, i - 1)
                    pe.wait_ge(k_ready, i - 1)
                elif i >= 4:
                    pe.wait_ge(q_ready, i)
                    pe.wait_ge(k_ready, i)
                for wt, bank, done in ((w.a3_Wq, q_bank(i), q_ps), (w.a3_Wk, q_bank(i) + 1, k_ps)):
                    pe.matmul(ps[bank][:, 0:COLS], wt[:, 2 * c:2 * c + 2, :].rearrange("p h k -> p (h k)"),
                              w.xT[:, g, :], start=True, stop=True).then_inc(done, 1)

            def values(i):
                if i >= 2:
                    pe.wait_ge(v_ready, i - 1)
                pe.matmul(ps[6 + i % 2][0:TP, :], w.xT[:, i // U, i % U * TP:(i % U + 1) * TP],
                          w.a3_Wvo[:, :, :].rearrange("p h n -> p (h n)"), start=True, stop=True).then_inc(v_ps, 1)

            def turn_weights(j):
                i = j % STEPS
                pe.wait_ge(a_ready, j + 1)
                if j:
                    pe.wait_ge(aT_ready, j)
                for par in range(2):
                    for c in range(2):
                        for t in range(2):
                            last = pe.transpose(ps[4 + par][0:TP, (2 * c + t) * TP:(2 * c + t + 1) * TP],
                                                frac[:, i, par, c, t * TP:(t + 1) * TP], w.ident[0:TP, 0:TP])
                last.then_inc(aT_ps, 1)

            def weigh(j):
                tile, pair = j // 2, j % 2
                o = ps[6 + tile % 2][0:TP, 0:D]
                if pair == 0:
                    if tile >= 2:
                        pe.wait_ge(o_read, tile - 1)
                    pe.matmul(o, w.ones_row[:, 0:TP], w.a3_bo[:, :], start=True, stop=False)
                pe.wait_ge(aT_ready, j + 1)
                for par in range(2):
                    for c in range(2):
                        hd = 2 * (2 * pair + c) + par
                        for t in range(2):
                            stop = pair == 1 and par == 1 and c == 1 and t == 1
                            last = pe.matmul(o, aT[:, j % 2, par, (2 * c + t) * TP:(2 * c + t + 1) * TP],
                                             vals[:, 2 * (tile // 2) + t, hd * D:(hd + 1) * D], start=False, stop=stop)
                last.then_inc(used, 1)

            def scores(j):
                g, tile, pair = j // STEPS, j // 2, j % 2
                if j >= 2:
                    pe.wait_ge(filtered, j - 1)
                at, keys = (tile % U) * TP, (tile % U) // 2 * SEQ
                for par in range(2):
                    rows = slice(64 * par, 64 * par + 64)
                    for c in range(2):
                        last = pe.matmul(ps[2 * (j % 2) + par][0:TP, c * SEQ:(c + 1) * SEQ],
                                         qf[rows, g, 2 * pair + c, at:at + TP],
                                         kf[rows, g, 2 * pair + c, keys:keys + SEQ], start=True, stop=True)
                last.then_inc(s_ps, 1)

            for i in range(4):
                queries_keys(i)
            pe.wait_ge(q_ready, 4)
            pe.wait_ge(k_ready, 4)
            for t in range(STEPS):
                scores(t)
                if t < 4:
                    for i in range(4 + t, 4 * GROUPS, 4):
                        queries_keys(i)
                else:
                    for i in range(2 * (t - 4), NT, 8):
                        values(i)
                        values(i + 1)
            pe.wait_ge(v_ready, NT)
            pe.wait_ge(q_ready, 4 * GROUPS)
            pe.wait_ge(k_ready, 4 * GROUPS)
            for j in range(ALL + 1):
                if j + STEPS < ALL:
                    scores(j + STEPS)
                if j < ALL:
                    turn_weights(j)
                if j:
                    weigh(j - 1)

        @block.scalar
        def _(act):
            for g in range(GROUPS):
                act.wait_ge(turned, g + 1)
                act.activation(w.xT[0:D, g, :], ps[g][0:D, 0:COLS], ACT.Copy).then_inc(xT_ready, 1)

            def keys(i):
                act.wait_ge(k_ps, i + 1)
                act.activation(kf[:, i // 4, i % 4, :], ps[q_bank(i) + 1][:, 0:COLS], ACT.Copy).then_inc(k_ready, 1)

            def values(i):
                act.wait_ge(v_ps, i + 1)
                act.activation(vals[:, i, :], ps[6 + i % 2][0:TP, :], ACT.Copy, scale=1.0 / TURN).then_inc(v_ready, 1)

            for i in range(4):
                keys(i)
            act.wait_ge(const_ready, 1)

            def size(j):
                act.wait_ge(s_ps, j + 1)
                if j >= 2:
                    act.wait_ge(held_ready, j - 1)
                act.activation(mag[:, j % 2, :, :, :], scores_of(j), ACT.Abs, scale=1618.0 / 8.0).then_inc(mag_ready, 1)

            def exponentials(j):
                i = j % STEPS
                act.wait_ge(shift_ready, j + 1)
                for m in range(4):
                    head = z[:, i, m // 2, m % 2, :]
                    last = act.activation(head, head, ACT.Exp, scale=0.125, bias=peak[:, i, m:m + 1],
                                          accum_out=total[:, i, m:m + 1])
                last.then_inc(exp_ready, 1)

            def damping(j):
                i = j % STEPS
                act.wait_ge(square_ready, j + 1)
                act.activation(flat(damp, i), flat(damp, i), ACT.Exp, scale=-1.0 / (TURN * TURN * PHI)
                               ).then_inc(damp_ready, 1)

            def waves(j):
                i = j % STEPS
                act.wait_ge(rest_ready, j + 1)
                act.activation(flat(frac, i), flat(frac, i), ACT.Sin, scale=BELOW_2PI).then_inc(sin_ready, 1)
                if j >= 2:
                    act.wait_ge(sum_ready, j - 1)
                act.activation(flat(cosine, j % 2), flat(z, i), ACT.Sin, scale=-C2 / TURN, bias=half_pi[:, 0:1]
                               ).then_inc(cos_ready, 1)

            def copy_turned(j):
                act.wait_ge(aT_ps, j + 1)
                if j >= 2:
                    act.wait_ge(used, j - 1)
                act.activation(aT[:, j % 2, :, :], w.banks[0:TP, 4:6, 0:4 * TP], ACT.Copy).then_inc(aT_ready, 1)

            act.preload_act_table(ACT.Exp)
            for t in range(STEPS + 4):
                if t < STEPS:
                    size(t)
                    if t < 4:
                        for i in range(4 + t, 4 * GROUPS, 4):
                            keys(i)
                if 1 <= t <= STEPS:
                    exponentials(t - 1)
                if 4 <= t < STEPS:
                    for i in range(2 * (t - 4), NT, 8):
                        values(i)
                        values(i + 1)
                if t >= 4:
                    damping(t - 4)
            for g in range(1, GROUPS + 1):
                act.preload_act_table(ACT.Sin)
                for t in range(STEPS + 3):
                    if g < GROUPS and 2 <= t < STEPS + 2:
                        size(g * STEPS + t - 2)
                    if t < STEPS:
                        waves((g - 1) * STEPS + t)
                    if t >= 3:
                        copy_turned((g - 1) * STEPS + t - 3)
                if g < GROUPS:
                    act.preload_act_table(ACT.Exp)
                    for t in range(STEPS + 2):
                        if t < STEPS:
                            exponentials(g * STEPS + t)
                        if t >= 2:
                            damping(g * STEPS + t - 2)

        @block.vector
        def _(dve):
            normalize(dve, v_step, per_group(w.h, w.xn, squares, sums), 1e-5, var_ready, rstd_ready, 0, ready=xn_ready)

            def queries(i):
                dve.wait_ge(q_ps, i + 1)
                dve.tensor_copy(qf[:, i // 4, i % 4, :], ps[q_bank(i)][:, 0:COLS]).then_inc(q_ready, 1)

            for i in range(4):
                queries(i)

            def add_out(tile):
                dve.wait_ge(used, 2 * tile + 2)
                dve.tensor_tensor(w.h[:, tile, :], w.h[:, tile, :], ps[6 + tile % 2][0:TP, 0:D], ALU.add
                                  ).then_inc(o_read, 1)

            def stage(j, s):
                g, i = j // STEPS, j % STEPS
                y, lo, f = flat(mag, j % 2), flat(low, j % 2), flat(z, i)
                y4, lo4, f4 = mag[:, j % 2, :, :, :], low[:, j % 2, :, :, :], z[:, i, :, :, :]
                heads = f4.rearrange("p a c n -> p (a c) n")
                if s == 0:
                    dve.wait_ge(mag_ready, j + 1)
                    dve.tensor_scalar(lo, y, 1.0 / 3.0, MAGIC, ALU.mult, ALU.add).then_inc(low_ready, 1)
                elif s == 1:
                    dve.wait_ge(low_ready, j + 1)
                    dve.tensor_scalar(lo, lo, -MAGIC, 3.0, ALU.add, ALU.mult).then_inc(three_ready, 1)
                elif s == 2:
                    dve.wait_ge(frac_ready, j + 1)
                    dve.scalar_tensor_tensor(out=lo4, in0=y4, scalar=0.0, in1=scores_of(j), op0=ALU.is_ge,
                                             op1=ALU.mult).then_inc(above_ready, 1)
                elif s == 9:
                    dve.wait_ge(above_ready, j + 1)
                    dve.scalar_tensor_tensor(out=lo, in0=y, scalar=1.0, in1=lo, op0=ALU.is_lt,
                                             op1=ALU.mult).then_inc(held_ready, 1)
                elif s == 3:
                    dve.wait_ge(held_ready, j + 1)
                    dve.scalar_tensor_tensor(out=f4, in0=lo4, scalar=1.0 / PHI - 1.0, in1=scores_of(j), op0=ALU.mult,
                                             op1=ALU.add).then_inc(filtered, 1)
                elif s == 4:
                    dve.wait_ge(filtered, j + 1)
                    dve.tensor_reduce(peak[:, i, :], heads, X, ALU.max).then_inc(peak_ready, 1)
                elif s == 5:
                    dve.wait_ge(peak_ready, j + 1)
                    dve.tensor_scalar(peak[:, i, :], peak[:, i, :], -0.125, None, ALU.mult).then_inc(shift_ready, 1)
                elif s == 6:
                    dve.wait_ge(exp_ready, j + 1)
                    dve.reciprocal(total[:, i, :], total[:, i, :]).then_inc(recip_ready, 1)
                elif s == 7:
                    dve.wait_ge(recip_ready, j + 1)
                    dve.scalar_tensor_tensor(out=heads, in0=heads, scalar=TURN, in1=wide(total[:, i, :], SEQ),
                                             op0=ALU.mult, op1=ALU.mult).then_inc(z_ready, 1)
                elif s == 10:
                    dve.wait_ge(turns_ready, j + 1)
                    dve.tensor_tensor(flat(frac, i), f, flat(frac, i), ALU.subtract).then_inc(rest_ready, 1)
                else:
                    dve.wait_ge(z_ready, j + 1)
                    if g:
                        dve.wait_ge(aT_ps, j - STEPS + 1)
                    dve.tensor_scalar(flat(frac, i), f, MAGIC, -MAGIC, ALU.add, ALU.add).then_inc(turns_ready, 1)

            def sum_up(j):
                i = j % STEPS
                dve.wait_ge(prod_ready, j + 1)
                dve.wait_ge(cos_ready, j + 1)
                dve.tensor_tensor(flat(damp, i), flat(damp, i), flat(cosine, j % 2), ALU.add).then_inc(sum_ready, 1)

            def times_weight(j):
                i = j % STEPS
                dve.wait_ge(sum_ready, j + 1)
                dve.tensor_tensor(flat(frac, i), flat(damp, i), flat(z, i), ALU.mult).then_inc(a_ready, 1)

            for t in range(STEPS + 3):
                for s, behind in ((8, 3), (0, 0), (4, 1), (1, 0), (5, 1), (6, 2), (2, 0), (7, 2), (9, 0), (3, 0)):
                    if 0 <= t - behind < STEPS:
                        stage(t - behind, s)
                    if s == 0 and t < 4:
                        for i in range(4 + t, 4 * GROUPS, 4):
                            queries(i)
            for g in range(1, GROUPS + 1):
                for t in range(STEPS + 3):
                    now, before = g * STEPS + t - 2, (g - 1) * STEPS + t - 1
                    filtering, peaks = g < GROUPS and 2 <= t < STEPS + 2, g < GROUPS and 3 <= t < STEPS + 3
                    weighing = 1 <= t <= STEPS
                    if filtering:
                        stage(now, 0)
                    if peaks:
                        stage(now - 1, 4)
                    if filtering:
                        stage(now, 1)
                    if peaks:
                        stage(now - 1, 5)
                    if weighing:
                        sum_up(before)
                    if filtering:
                        stage(now, 2)
                    if weighing:
                        times_weight(before)
                    if filtering:
                        stage(now, 9)
                    if t % 2 == 1 and before >= 4 and 3 <= t <= STEPS + 1:
                        add_out((before - 4) // 2)
                    if filtering:
                        stage(now, 3)
                if g < GROUPS:
                    for t in range(STEPS + 2):
                        for s, behind in ((8, 1), (6, 0), (10, 2), (7, 0)):
                            if 0 <= t - behind < STEPS:
                                stage(g * STEPS + t - behind, s)
            add_out(NT - 1)
            dve.wait_ge(o_read, NT)

        return sems


def early_fusion(nc, d, out):
    w = Core()
    with ExitStack() as ctx:
        allocate(nc, ctx, w)
        loaded_p = ctx.enter_context(nc.semaphore("loaded_p"))
        stored = ctx.enter_context(nc.semaphore("stored"))

        def clear(sems):
            engines = (nc.sync, nc.scalar, nc.vector, nc.gpsimd, nc.tensor)
            for i, s in enumerate(sems):
                engines[i % len(engines)].sem_clear(s)
            nc.all_engine_barrier()

        clear(load_weights(nc, d, w, loaded_p))
        with nc.Fori(0, PASSES) as p:
            clear(tok(nc, d, w, p))
            for layer in LAYERS:
                clear(layer(nc, d, w))
            store(nc, w, p, out, stored)
            clear([stored])


def store(nc, w, p, out, stored):
    NB = G * GROUPS
    with nc.Block() as block:
        @block.sync
        def _(sp):
            sp.dma_start(out[bass.ds(p * NB, NB)].rearrange("b (t q) n -> q (b t) n", t=2), w.h[:, :, :]
                         ).then_inc(stored, 16)
            sp.wait_ge(stored, 16)

        @block.gpsimd
        def _(pool):
            pool.memset(w.in_first[:], 0)


LAYERS = [mamba, ffn0, attn1, ffn1, attn2, ffn2, attn3, ffn3]


def constants():
    t = np.arange(TP)
    seen = (t[:, None] <= t[None, :])
    sel_bc = np.zeros((96, 2 * NST, 128), np.float32)
    for part in range(3):
        for n in range(2 * NST):
            sel_bc[32 * part + n, n, :] = 1.0
    sel_expert = np.zeros((96, HID2), np.float32)
    for part in range(3):
        for e in range(8):
            sel_expert[32 * part + e, HID2 // 8 * e:HID2 // 8 * (e + 1)] = 1.0
    hd = 16
    inv_freq = 1.0 / 10000.0 ** (np.arange(0, hd, 2, dtype=np.float32) / hd)
    freqs = np.outer(np.arange(SEQ, dtype=np.float32), inv_freq)
    emb = np.concatenate([freqs, freqs], axis=-1)
    cos, sin = np.zeros((128, SEQ), np.float32), np.zeros((128, SEQ), np.float32)
    for n in range(8):
        cos[hd * n:hd * (n + 1)] = np.cos(emb).T
        sin[hd * n:hd * (n + 1)] = np.sin(emb).T
        sin[hd * n:hd * n + hd // 2] *= -1.0
    return {
        "c_ident": np.eye(128, dtype=np.float32),
        "c_causal01": np.concatenate([seen, np.ones_like(seen), seen], 1).astype(np.float32),
        "c_maskT": np.concatenate([np.where(seen, 0.0, NEG), np.zeros((TP, TP))], 1).astype(np.float32),
        "c_maskQ": np.concatenate([np.zeros((TP, TP)), np.where(seen.T, 0.0, NEG)], 1).astype(np.float32),
        "c_rank": np.tile(8.0 - np.arange(8, dtype=np.float32), (TP, 1)),
        "c_sel_bc": sel_bc, "c_sel_expert": sel_expert,
        "c_less": np.array([[0, 0], [-1, 0], [-1, -1]], np.float32),
        "c_rope_cos": cos, "c_rope_sin": sin,
    }


def kernel(**inputs):
    import concourse.bacc as bacc
    from concourse.bass_utils import run_bass_kernel_spmd

    nc = bacc.Bacc("TRN2", target_bir_lowering=False, num_devices=1)
    arrays, d = {}, {}
    for name, a in {**inputs, **constants()}.items():
        a = np.ascontiguousarray(a)
        arrays[name + "_dram"] = a
        d[name] = nc.dram_tensor(name + "_dram", a.shape, mybir.dt.from_np(a.dtype), kind="ExternalInput").ap()
    out = nc.dram_tensor("out_dram", (B, SEQ, D), F32, kind="ExternalOutput").ap()
    early_fusion(nc, d, out)
    r = run_bass_kernel_spmd(nc, [arrays], core_ids=[0])
    return r.results[0]["out_dram"]
```
